# Optimizing a Trainium2 kernel written in Bass

```python
import numpy as np
import jax
import jax.numpy as jnp

def _softmax(x, axis=-1):
    return jax.nn.softmax(x, axis=axis)

def _gelu(x):
    return jax.nn.gelu(x, approximate=True)

def _silu(x):
    return jax.nn.silu(x)

def _sigmoid(x):
    return jax.nn.sigmoid(x)

def _layernorm(x, axis=-1, eps=1e-05):
    m = jnp.mean(x, axis=axis, keepdims=True)
    v = jnp.var(x, axis=axis, keepdims=True)
    return (x - m) / jnp.sqrt(v + eps)

def _scatter_add(tgt, idx, src, axis=0):
    return tgt.at[idx].add(src)

def _segment_sum(src, seg, n):
    return jax.ops.segment_sum(src, seg, n)
kernel_name = 'mk_hybrid_d1_jaxref_r4_37da21'

def setup_inputs(seed: int=0):
    np.random.seed(seed)
    _w = jnp.asarray

    def _L0_attn_a_setup():
        import jax, jax.numpy as jnp
        import numpy as np
        HEADS = 8
        DIM_HEAD = 64
        SCALE = DIM_HEAD ** (-0.5)
        key = jax.random.key(seed)
        k1, k2, k3, k4 = jax.random.split(key, 4)
        B, N, C = (4, 4096, 256)
        x = jax.random.normal(k1, (B, N, C), dtype=jnp.float32)
        Wqkv = jax.random.normal(k2, (C, DIM_HEAD * 3), dtype=jnp.float32) * C ** (-0.5)
        Wout = jax.random.normal(k3, (DIM_HEAD, C), dtype=jnp.float32) * DIM_HEAD ** (-0.5)
        bout = jax.random.normal(k4, (C,), dtype=jnp.float32) * 0.01
        return {'x': x, 'Wqkv': Wqkv, 'Wout': Wout, 'bout': bout}
    _L0_attn_a_in = _L0_attn_a_setup()

    def _L0_attn_b_setup():
        import jax, jax.numpy as jnp
        import numpy as np
        B, T, C = (4, 512, 256)
        key = jax.random.key(seed)
        ks = jax.random.split(key, 9)
        s = 1.0 / np.sqrt(C)
        return {'x': jax.random.normal(ks[0], (B, T, C), dtype=jnp.float32), 'Wq': jax.random.uniform(ks[1], (C, C), jnp.float32, -s, s), 'bq': jax.random.uniform(ks[2], (C,), jnp.float32, -s, s), 'Wk': jax.random.uniform(ks[3], (C, C), jnp.float32, -s, s), 'bk': jax.random.uniform(ks[4], (C,), jnp.float32, -s, s), 'Wv': jax.random.uniform(ks[5], (C, C), jnp.float32, -s, s), 'bv': jax.random.uniform(ks[6], (C,), jnp.float32, -s, s), 'Wo': jax.random.uniform(ks[7], (C, C), jnp.float32, -s, s), 'bo': jax.random.uniform(ks[8], (C,), jnp.float32, -s, s)}
    _L0_attn_b_in = _L0_attn_b_setup()

    def _L0_ffn_setup():
        import jax, jax.numpy as jnp
        import numpy as np
        from jax.scipy.linalg import expm
        B, S, D, E, K, NROT = (2, 512, 256, 8, 2, 3)
        EPS = 1e-05

        def _gelu(x):
            return jax.nn.gelu(x, approximate=False)

        def _forward(x, ln_gamma, ln_beta, abel_w, abel_b, moe_gate_w, moe_gate_b, ew1, eb1, ew2, eb2, gens, gc_w, gc_b):
            residual = x
            mu = jnp.mean(x, axis=-1, keepdims=True)
            var = jnp.mean((x - mu) ** 2, axis=-1, keepdims=True)
            xn = (x - mu) * jax.lax.rsqrt(var + EPS) * ln_gamma + ln_beta
            abel_out = _gelu(xn @ abel_w + abel_b)
            logits = xn @ moe_gate_w + moe_gate_b
            topw, topi = jax.lax.top_k(logits, K)
            topw = jax.nn.softmax(topw, axis=-1)
            w_dense = jnp.sum(jax.nn.one_hot(topi, E, dtype=xn.dtype) * topw[..., None], axis=-2)
            h = _gelu(jnp.einsum('bsd,edh->ebsh', xn, ew1) + eb1[:, None, None, :])
            eo = jnp.einsum('ebsh,ehd->ebsd', h, ew2) + eb2[:, None, None, :]
            moe_out = jnp.einsum('ebsd,bse->bsd', eo, w_dense)
            for i in range(NROT):
                moe_out = moe_out @ expm(gens[i])
            combined = jnp.concatenate([abel_out, moe_out], axis=-1)
            gate = jax.nn.sigmoid(combined @ gc_w + gc_b)
            mixed = abel_out * (1.0 - gate) + moe_out * gate
            return residual + mixed
        key = jax.random.key(seed)
        ks = jax.random.split(key, 16)
        sc = 0.02
        x = jax.random.normal(ks[0], (B, S, D), jnp.float32)
        ln_gamma = 1.0 + sc * jax.random.normal(ks[1], (D,), jnp.float32)
        ln_beta = sc * jax.random.normal(ks[2], (D,), jnp.float32)
        abel_w = sc * jax.random.normal(ks[3], (D, D), jnp.float32)
        abel_b = sc * jax.random.normal(ks[4], (D,), jnp.float32)
        moe_gate_w = sc * jax.random.normal(ks[5], (D, E), jnp.float32)
        moe_gate_b = sc * jax.random.normal(ks[6], (E,), jnp.float32)
        ew1 = sc * jax.random.normal(ks[7], (E, D, 2 * D), jnp.float32)
        eb1 = sc * jax.random.normal(ks[8], (E, 2 * D), jnp.float32)
        ew2 = sc * jax.random.normal(ks[9], (E, 2 * D, D), jnp.float32)
        eb2 = sc * jax.random.normal(ks[10], (E, D), jnp.float32)
        g = sc * jax.random.normal(ks[11], (NROT, D, D), jnp.float32)
        gens = 0.5 * (g - jnp.swapaxes(g, -1, -2))
        gc_w = sc * jax.random.normal(ks[12], (2 * D, 1), jnp.float32)
        gc_b = sc * jax.random.normal(ks[13], (1,), jnp.float32)
        return dict(x=x, ln_gamma=ln_gamma, ln_beta=ln_beta, abel_w=abel_w, abel_b=abel_b, moe_gate_w=moe_gate_w, moe_gate_b=moe_gate_b, ew1=ew1, eb1=eb1, ew2=ew2, eb2=eb2, gens=gens, gc_w=gc_w, gc_b=gc_b)
    _L0_ffn_in = _L0_ffn_setup()
    _d = {'L0_attn_a_x': _L0_attn_a_in['x'], 'L0_attn_a_Wqkv': _L0_attn_a_in['Wqkv'], 'L0_attn_a_Wout': _L0_attn_a_in['Wout'], 'L0_attn_a_bout': _L0_attn_a_in['bout'], 'L0_attn_b_Wq': _L0_attn_b_in['Wq'], 'L0_attn_b_bq': _L0_attn_b_in['bq'], 'L0_attn_b_Wk': _L0_attn_b_in['Wk'], 'L0_attn_b_bk': _L0_attn_b_in['bk'], 'L0_attn_b_Wv': _L0_attn_b_in['Wv'], 'L0_attn_b_bv': _L0_attn_b_in['bv'], 'L0_attn_b_Wo': _L0_attn_b_in['Wo'], 'L0_attn_b_bo': _L0_attn_b_in['bo'], 'L0_ffn_ln_gamma': _L0_ffn_in['ln_gamma'], 'L0_ffn_ln_beta': _L0_ffn_in['ln_beta'], 'L0_ffn_abel_w': _L0_ffn_in['abel_w'], 'L0_ffn_abel_b': _L0_ffn_in['abel_b'], 'L0_ffn_moe_gate_w': _L0_ffn_in['moe_gate_w'], 'L0_ffn_moe_gate_b': _L0_ffn_in['moe_gate_b'], 'L0_ffn_ew1': _L0_ffn_in['ew1'], 'L0_ffn_eb1': _L0_ffn_in['eb1'], 'L0_ffn_ew2': _L0_ffn_in['ew2'], 'L0_ffn_eb2': _L0_ffn_in['eb2'], 'L0_ffn_gens': _L0_ffn_in['gens'], 'L0_ffn_gc_w': _L0_ffn_in['gc_w'], 'L0_ffn_gc_b': _L0_ffn_in['gc_b']}
    _x0 = _d['L0_attn_a_x']
    _d['L0_attn_a_x'] = jax.random.normal(jax.random.fold_in(jax.random.key(seed), 1), (2, 2048, 256), dtype=_x0.dtype)
    del _x0
    return _d

def reference(L0_attn_a_x, L0_attn_a_Wqkv, L0_attn_a_Wout, L0_attn_a_bout, L0_attn_b_Wq, L0_attn_b_bq, L0_attn_b_Wk, L0_attn_b_bk, L0_attn_b_Wv, L0_attn_b_bv, L0_attn_b_Wo, L0_attn_b_bo, L0_ffn_ln_gamma, L0_ffn_ln_beta, L0_ffn_abel_w, L0_ffn_abel_b, L0_ffn_moe_gate_w, L0_ffn_moe_gate_b, L0_ffn_ew1, L0_ffn_eb1, L0_ffn_ew2, L0_ffn_eb2, L0_ffn_gens, L0_ffn_gc_w, L0_ffn_gc_b):

    def _L0_attn_a_ref(x, Wqkv, Wout, bout):
        import jax, jax.numpy as jnp
        import numpy as np
        HEADS = 8
        DIM_HEAD = 64
        SCALE = DIM_HEAD ** (-0.5)
        B, N, C = x.shape
        h = HEADS
        d = DIM_HEAD // h
        qkv = x @ Wqkv
        q, k, v = jnp.split(qkv, 3, axis=-1)
        to_heads = lambda t: t.reshape(B, N, h, d).transpose(0, 2, 1, 3)
        q = to_heads(q) * SCALE
        k = jax.nn.softmax(to_heads(k), axis=-1)
        v = to_heads(v)
        context = jnp.einsum('bhnd,bhne->bhde', k, v)
        out = jnp.einsum('bhnd,bhde->bhne', q, context)
        out = out.transpose(0, 2, 1, 3).reshape(B, N, h * d)
        return out @ Wout + bout

    def _L0_attn_b_ref(x, Wq, bq, Wk, bk, Wv, bv, Wo, bo):
        import jax, jax.numpy as jnp
        import numpy as np
        B, T, C = (4, 512, 256)
        Bs, Ts, Cs = x.shape
        Q = x @ Wq.T + bq
        K = x @ Wk.T + bk
        V = x @ Wv.T + bv
        scale = 1.0 / jnp.sqrt(jnp.asarray(Cs, x.dtype))
        scores = jnp.einsum('btc,bsc->bts', Q, K) * scale
        causal = jnp.tril(jnp.ones((Ts, Ts), dtype=bool))[None]
        scores = jnp.where(causal, scores, jnp.asarray(-jnp.inf, x.dtype))
        w = jax.nn.softmax(scores, axis=-1)
        out = jnp.einsum('bts,bsc->btc', w, V)
        return out @ Wo.T + bo

    def _L0_ffn_ref(x, ln_gamma, ln_beta, abel_w, abel_b, moe_gate_w, moe_gate_b, ew1, eb1, ew2, eb2, gens, gc_w, gc_b):
        import jax, jax.numpy as jnp
        import numpy as np
        from jax.scipy.linalg import expm
        B, S, D, E, K, NROT = (2, 512, 256, 8, 2, 3)
        EPS = 1e-05

        def _gelu(x):
            return jax.nn.gelu(x, approximate=False)

        def _forward(x, ln_gamma, ln_beta, abel_w, abel_b, moe_gate_w, moe_gate_b, ew1, eb1, ew2, eb2, gens, gc_w, gc_b):
            residual = x
            mu = jnp.mean(x, axis=-1, keepdims=True)
            var = jnp.mean((x - mu) ** 2, axis=-1, keepdims=True)
            xn = (x - mu) * jax.lax.rsqrt(var + EPS) * ln_gamma + ln_beta
            abel_out = _gelu(xn @ abel_w + abel_b)
            logits = xn @ moe_gate_w + moe_gate_b
            topw, topi = jax.lax.top_k(logits, K)
            topw = jax.nn.softmax(topw, axis=-1)
            w_dense = jnp.sum(jax.nn.one_hot(topi, E, dtype=xn.dtype) * topw[..., None], axis=-2)
            h = _gelu(jnp.einsum('bsd,edh->ebsh', xn, ew1) + eb1[:, None, None, :])
            eo = jnp.einsum('ebsh,ehd->ebsd', h, ew2) + eb2[:, None, None, :]
            moe_out = jnp.einsum('ebsd,bse->bsd', eo, w_dense)
            for i in range(NROT):
                moe_out = moe_out @ expm(gens[i])
            combined = jnp.concatenate([abel_out, moe_out], axis=-1)
            gate = jax.nn.sigmoid(combined @ gc_w + gc_b)
            mixed = abel_out * (1.0 - gate) + moe_out * gate
            return residual + mixed
        return _forward(x, ln_gamma, ln_beta, abel_w, abel_b, moe_gate_w, moe_gate_b, ew1, eb1, ew2, eb2, gens, gc_w, gc_b)
    x = L0_attn_a_x
    x = x + _L0_attn_a_ref(_layernorm(x, axis=-1), L0_attn_a_Wqkv, L0_attn_a_Wout, L0_attn_a_bout)
    x = x + _L0_ffn_ref(_layernorm(x, axis=-1), L0_ffn_ln_gamma, L0_ffn_ln_beta, L0_ffn_abel_w, L0_ffn_abel_b, L0_ffn_moe_gate_w, L0_ffn_moe_gate_b, L0_ffn_ew1, L0_ffn_eb1, L0_ffn_ew2, L0_ffn_eb2, L0_ffn_gens, L0_ffn_gc_w, L0_ffn_gc_b)
    x = x + _L0_attn_b_ref(_layernorm(x, axis=-1), L0_attn_b_Wq, L0_attn_b_bq, L0_attn_b_Wk, L0_attn_b_bk, L0_attn_b_Wv, L0_attn_b_bv, L0_attn_b_Wo, L0_attn_b_bo)
    x = x + _L0_ffn_ref(_layernorm(x, axis=-1), L0_ffn_ln_gamma, L0_ffn_ln_beta, L0_ffn_abel_w, L0_ffn_abel_b, L0_ffn_moe_gate_w, L0_ffn_moe_gate_b, L0_ffn_ew1, L0_ffn_eb1, L0_ffn_ew2, L0_ffn_eb2, L0_ffn_gens, L0_ffn_gc_w, L0_ffn_gc_b)
    return x

_drawn_inputs = setup_inputs


def setup_inputs(seed=0):
    import zlib

    import numpy as np

    out = dict(_drawn_inputs(seed))
    spreads = {}
    factors = {'L0_attn_a_bout': 8.0,
     'L0_attn_b_Wq': 8.0,
     'L0_attn_b_bq': 8.0,
     'L0_attn_b_Wk': 8.0,
     'L0_attn_b_bk': 8.0,
     'L0_attn_b_Wv': 8.0,
     'L0_attn_b_bv': 8.0,
     'L0_attn_b_Wo': 8.0,
     'L0_attn_b_bo': 8.0,
     'L0_ffn_ln_gamma': 8.0,
     'L0_ffn_ln_beta': 8.0,
     'L0_ffn_abel_b': 8.0,
     'L0_ffn_moe_gate_w': 7.475,
     'L0_ffn_moe_gate_b': 8.0,
     'L0_ffn_ew1': 7.045,
     'L0_ffn_eb1': 8.0,
     'L0_ffn_ew2': 6.838,
     'L0_ffn_eb2': 8.0,
     'L0_ffn_gens': 8.0,
     'L0_ffn_gc_w': 8.0}
    for name, (base, spread) in spreads.items():
        noise = np.random.default_rng([zlib.crc32(name.encode()), seed]).standard_normal(out[name].shape)
        drawn = base * np.exp(spread * noise) if base else spread * noise
        out[name] = jnp.asarray(drawn.astype(out[name].dtype))
    for name, factor in factors.items():
        out[name] = (out[name] * factor).astype(out[name].dtype)
    return out
```

```python
from contextlib import ExitStack

import concourse.bass as bass
from concourse import mybir

F32, BF16, I32 = mybir.dt.float32, mybir.dt.bfloat16, mybir.dt.int32
ACT, ALU, AX = mybir.ActivationFunctionType, mybir.AluOpType, mybir.AxisListType
P = 128
EPS = 1e-5
BANK = 512
LOWEST = -3.0e38


def build(nc, d, out):
    B, N, C = d["L0_attn_a_x"].shape
    HD = d["L0_attn_a_Wout"].shape[0]
    E, _, H = d["L0_ffn_ew1"].shape
    NROT = d["L0_ffn_gens"].shape[0]
    HEADS = 8
    DH = HD // HEADS
    T = B * N
    NT = T // P
    BT = N // P
    KC = C // P
    HC = H // P
    GT = BANK // P
    NG = NT // GT
    SLOTS = 2 * T // P + E - 1
    QROW = 32

    ctx = ExitStack()
    with ctx:
        def sb(name, shape, dt=F32):
            return ctx.enter_context(nc.sbuf_tensor(name, shape, dt))

        taken = []

        def sem(name):
            taken.append(nc.alloc_semaphore(name))
            return taken[-1]

        def release(first):
            nc.clear_and_free_semaphores(taken[first:])
            del taken[first:]
            nc.all_engine_barrier()

        xs = sb("xs", [P, NT, C])
        xh = sb("xh", [P, NT, C])
        ab = sb("ab", [P, NT, C])
        ew1 = sb("ew1", [P, KC, E, H])
        ew2 = sb("ew2", [P, HC, E, C])
        abw = sb("abw", [P, KC, C])
        gw = sb("gw", [P, KC, E])
        gcw = sb("gcw", [P, 2, C])
        gcb = sb("gcb", [P, 1])
        gateb = sb("gateb", [1, E])
        eb1p = sb("eb1p", [2 * QROW + E, H], BF16)
        eb2p = sb("eb2p", [2 * QROW + E, C], BF16)
        abbp = sb("abbp", [2 * QROW + 1, C], BF16)
        vbp = sb("vbp", [2 * QROW + 1, C], BF16)
        sel = sb("sel", [2 * QROW + E, E, P], BF16)
        wa = sb("wa", [P, KC, C])
        wvo = sb("wvo", [P, KC, C])
        qbias = sb("qbias", [P, KC])
        ident = sb("ident", [P, P])
        identb = sb("identb", [P, P], BF16)
        causal = sb("causal", [P, P], BF16)
        tri = sb("tri", [P, P], BF16)
        onesb = sb("onesb", [P, P], BF16)
        onesf = sb("onesf", [1, P])
        mhalf = sb("mhalf", [P, 2 * GT])
        eidx = sb("eidx", [P, E])
        steps = sb("steps", [P, NT])
        sidx = sb("sidx", [P, SLOTS])
        ctxm = sb("ctxm", [HD + 1, B, C])
        wqkv = sb("wqkv", [P, KC, 3 * HD])
        wout = sb("wout", [HD, C])
        hmask = sb("hmask", [HD, HD])
        work = sb("work", [P, 7136])
        bank = ctx.enter_context(nc.psum_tensor("bank", [P, 8, BANK], F32))
        xg = nc.dram_tensor("slots_in", (SLOTS * P, C), F32).ap()
        yg = nc.dram_tensor("slots_out", (SLOTS * P, C), F32).ap()

        x_in = sem("x_in")

        class Arena:
            def __init__(self, flat):
                self.flat, self.at = flat, 0

            def take(self, *shape, dt=F32, rows=P):
                n = 1
                for s in shape:
                    n *= s
                w = n if dt in (F32, I32) else (n + 1) // 2
                v = self.flat[0:rows, self.at:self.at + w]
                self.at += w
                assert self.at <= self.flat.shape[1], self.at
                if dt != F32:
                    v = v.bitcast(dt)
                if len(shape) == 2:
                    v = v.rearrange("p (a b) -> p a b", a=shape[0])
                if len(shape) == 3:
                    v = v.rearrange("p (a b c) -> p a b c", a=shape[0], b=shape[1])
                return v

        def flat(t):
            return t[:].rearrange("p a b -> p (a b)")

        def cols(view, bc):
            return view.unsqueeze(len(view.shape)).to_broadcast(list(view.shape) + [bc])

        def psum(b, n=1):
            return bank[:, b:b + n, :].rearrange("p a b -> p (a b)")

        def copy(eng, o, i, scale=1.0):
            return eng.activation(o, i, ACT.Copy, scale=scale)

        def weights():
            a = Arena(flat(xh))
            gens = a.take(NROT, KC, C)
            A = a.take(NROT, KC, C)
            AT = a.take(NROT, KC, C)
            X = a.take(NROT, KC, C)
            eye = a.take(KC, C)
            R = a.take(KC, C)
            w = work[:]
            a2 = Arena(w)
            zeros, a3 = flat(ab)[:, 0:NT * C // 2], Arena(flat(ab)[:, NT * C // 2:])
            w4 = [a3.take(KC, C) for _ in range(4)]
            woT = a2.take(KC, C)
            ew2T = [a2.take(KC, H) for _ in range(2)]
            bsel = a2.take(KC, E * E)
            gam, bet = a2.take(KC), a2.take(KC)
            bqc, bvc = a2.take(KC), a2.take(KC)
            eb2s = a2.take(C, rows=E)
            eb2T = a2.take(KC, E)
            eb1s = a2.take(H, rows=E)
            row = a.take(3, C, rows=1)
            grow = a2.take(E, rows=1)
            rem = a2.take(H, rows=E)
            rem2 = a2.take(C, rows=E)
            p2 = a2.take(H, rows=E, dt=BF16)
            gsum = a2.take(NROT * KC)
            gmx, gall = a2.take(1), a2.take(1)
            thr = a2.take(24)
            cmp = a2.take(24)
            sf, scf, scale = a2.take(1), a2.take(1), a2.take(1)
            sqi = a2.take(1, dt=I32)
            ki = a2.take(24, dt=I32)
            ei = a2.take(E, dt=I32)
            ti = a2.take(NT, dt=I32)
            ji = a2.take(SLOTS, dt=I32)

            w_small, w_ew, w_gens, w_proj = sem("w_small"), sem("w_ew"), sem("w_gens"), sem("w_proj")
            zero_ab, zeroed = sem("zero_ab"), sem("slots_zeroed")
            consts, iotas, order = sem("consts"), sem("iotas"), sem("pool_order")
            bsel_ok, beta_mm, row_ok = sem("bsel_ok"), sem("beta_mm"), sem("row_ok")
            dve = sem("dve_order")
            g_mx, g_all, A_ok, AT_ps, AT_ok = sem("g_mx"), sem("g_all"), sem("A_ok"), sem("AT_ps"), sem("AT_ok")
            horner_ps, X_ok, s_ok = sem("horner_ps"), sem("X_ok"), sem("s_ok")
            sq_T, ET_ok, sq_Y = sem("sq_T"), sem("ET_ok"), sem("sq_Y")
            rot_T, rot_TS, rot_Y, rot_ok = sem("rot_T"), sem("rot_TS"), sem("rot_Y"), sem("rot_ok")
            fold_T, fold_TS, fold_Y, fold_ok = sem("fold_T"), sem("fold_TS"), sem("fold_Y"), sem("fold_ok")
            eb2_T, eb2_TS, eb2_Y = sem("eb2_T"), sem("eb2_TS"), sem("eb2_Y")
            at_ps, at_ok, vb_ok = sem("at_ps"), sem("at_ok"), sem("vb_ok")
            HORNER = 10

            with nc.Block() as block:
                @block.sync
                def _(sp):
                    one = lambda k: d[k].rearrange("(o n) -> o n", o=1)
                    colv = lambda k: d[k].rearrange("(c p) -> p c", p=P)
                    chunked = lambda k: d[k].rearrange("(c p) n -> p c n", p=P)
                    small = [
                        (gam, colv("L0_ffn_ln_gamma")), (bet, colv("L0_ffn_ln_beta")),
                        (bqc, colv("L0_attn_b_bq")), (bvc, colv("L0_attn_b_bv")),
                        (abw[:], chunked("L0_ffn_abel_w")), (gw[:], chunked("L0_ffn_moe_gate_w")),
                        (eb1s, d["L0_ffn_eb1"]), (eb2s, d["L0_ffn_eb2"]),
                        (row[:, 0, :], one("L0_ffn_abel_b")), (row[:, 1, :], one("L0_attn_b_bo")),
                        (grow, one("L0_ffn_moe_gate_b")),
                    ]
                    assert len(small) == 11
                    for o, i in small:
                        sp.dma_start(o, i, allow_slow_non_contiguous=True).then_inc(w_small, 16)
                    for h in range(2):
                        sp.dma_start(gcw[:, h, :], d["L0_ffn_gc_w"][(1 - h) * C:(2 - h) * C, :].rearrange("n o -> (o n)")
                                     .partition_broadcast(P)).then_inc(w_small, 16)
                    sp.dma_start(gcb[:], d["L0_ffn_gc_b"].partition_broadcast(P)).then_inc(w_small, 16)
                    for c in range(KC):
                        sp.dma_start(ew1[:, c, :, :], d["L0_ffn_ew1"][:, c * P:(c + 1) * P, :].rearrange("e p h -> p e h")
                                     ).then_inc(w_ew, 16)
                    for c in range(HC):
                        sp.dma_start(ew2[:, c, :, :], d["L0_ffn_ew2"][:, c * P:(c + 1) * P, :].rearrange("e p h -> p e h")
                                     ).then_inc(w_ew, 16)
                    sp.wait_ge(zero_ab, 1)
                    slots = xg.rearrange("(p r) c -> p (r c)", p=P)
                    width, z = SLOTS * C, zeros
                    at = 0
                    while at < width:
                        n = min(width - at, z.shape[1])
                        sp.dma_start(slots[:, at:at + n], z[:, 0:n]).then_inc(zeroed, 16)
                        at += n
                    sp.wait_ge(zeroed, 16 * -(-width // z.shape[1]))

                @block.gpsimd
                def _(pool):
                    n = 0

                    def then(ins):
                        nonlocal n
                        n += 1
                        ins.then_inc(order, 1)
                        pool.wait_ge(order, n)

                    def select(t, pattern, base, cm, op, fill):
                        return pool.affine_select(out=t, in_=t, compare_op=op, fill=fill, base=base, pattern=pattern,
                                                  channel_multiplier=cm)

                    then(pool.memset(ident[:], 0.0))
                    select(ident[:], [[-1, P]], 0, 1, ALU.not_equal, 1.0).then_inc(consts, 1)
                    then(pool.memset(eye, 0.0))
                    select(eye, [[P, KC], [-1, C]], 0, 1, ALU.not_equal, 1.0).then_inc(consts, 1)
                    then(pool.memset(identb[:], 0.0))
                    select(identb[:], [[-1, P]], 0, 1, ALU.not_equal, 1.0).then_inc(consts, 1)
                    pool.memset(zeros, 0.0).then_inc(zero_ab, 1)
                    then(pool.memset(tri[:], 1.0))
                    select(tri[:], [[1, P]], 0, -1, ALU.is_gt, 0.0).then_inc(consts, 1)
                    then(pool.memset(causal[:], 0.0))
                    select(causal[:], [[-1, P]], 0, 1, ALU.is_ge, LOWEST).then_inc(consts, 1)
                    then(pool.memset(sel[:], 0.0))
                    for q in range(3):
                        then(select(sel[:], [[-1, E], [0, P]], -QROW * q, 1, ALU.not_equal, 1.0))
                    hm = hmask[:].rearrange("p (h e) -> p h e", h=HEADS)
                    then(pool.memset(hmask[:], 1.0))
                    then(select(hm, [[-DH, HEADS], [0, DH]], 0, 1, ALU.is_ge, 0.0))
                    then(select(hm, [[DH, HEADS], [0, DH]], DH - 1, -1, ALU.is_ge, 0.0))
                    pool.memset(onesb[:], 1.0).then_inc(consts, 1)
                    pool.memset(onesf[:], 1.0).then_inc(consts, 1)
                    pool.memset(mhalf[:], -0.5).then_inc(consts, 1)
                    for t in (eb1p, eb2p, abbp, vbp):
                        pool.memset(t[:], 0.0).then_inc(consts, 1)
                    pool.iota(ki, pattern=[[1, 24]], base=127, channel_multiplier=0).then_inc(iotas, 1)
                    pool.iota(ei, pattern=[[1, E]], base=-E, channel_multiplier=0).then_inc(iotas, 1)
                    pool.iota(ti, pattern=[[P, NT]], base=0, channel_multiplier=0).then_inc(iotas, 1)
                    pool.iota(ji, pattern=[[1, SLOTS]], base=0, channel_multiplier=0).then_inc(iotas, 1)
                    pool.wait_ge(g_mx, 1)
                    pool.partition_all_reduce(gall, gmx, P, bass.bass_isa.ReduceOp.max).then_inc(g_all, 1)

                @block.vector
                def _(v):
                    n = 0

                    def then(ins):
                        nonlocal n
                        n += 1
                        ins.then_inc(dve, 1)
                        v.wait_ge(dve, n)

                    def parts(o, src, width, rows):
                        r, q = rem[0:rows, 0:width], p2[0:rows, 0:width]
                        then(v.tensor_copy(o[0:rows, :], src))
                        then(v.tensor_tensor(r, src, o[0:rows, :], ALU.subtract))
                        then(v.tensor_copy(q, r))
                        then(v.tensor_copy(o[QROW:QROW + rows, :], q))
                        then(v.tensor_tensor(r, r, q, ALU.subtract))
                        then(v.tensor_copy(o[2 * QROW:2 * QROW + rows, :], r))

                    then(v.memset(bsel, 0.0))
                    v.wait_ge(w_small, 16 * 14)
                    for c in range(KC):
                        last = v.tensor_copy(bsel[:, c, 0:E * E:E + 1], bet[:, c:c + 1].to_broadcast([P, E]))
                    last.then_inc(bsel_ok, 1)
                    then(v.tensor_tensor(gcw[:, 1, :], gcw[:, 1, :], gcw[:, 0, :], ALU.add))
                    v.wait_ge(iotas, 4)
                    then(v.tensor_scalar(thr.bitcast(I32), ki, 23, None, ALU.logical_shift_left))
                    v.tensor_copy(eidx[:], ei)
                    v.tensor_copy(steps[:], ti)
                    then(v.tensor_copy(sidx[:], ji))
                    v.wait_ge(w_gens, 16)
                    then(v.tensor_reduce(gsum, gens.rearrange("p m c j -> p (m c) j"), AX.X, ALU.add,
                                         apply_absolute_value=True))
                    v.tensor_reduce(gmx, gsum, AX.X, ALU.max).then_inc(g_mx, 1)
                    v.wait_ge(g_all, 1)
                    then(v.tensor_scalar(cmp, thr, gall, None, ALU.is_lt))
                    then(v.tensor_reduce(sf, cmp, AX.X, ALU.add))
                    then(v.tensor_scalar(sf, sf, 1.0, None, ALU.max))
                    v.tensor_copy(sqi, sf).then_inc(s_ok, 1)
                    then(v.tensor_scalar(scf, sf, -1.0, 127.0, ALU.mult, ALU.add))
                    then(v.tensor_copy(scale.bitcast(I32), scf))
                    then(v.tensor_scalar(scale.bitcast(I32), scale.bitcast(I32), 23, None, ALU.logical_shift_left))
                    for m in range(NROT):
                        v.tensor_scalar(A[:, m], gens[:, m], scale, None, ALU.mult).then_inc(A_ok, 1)
                    v.wait_ge(A_ok, NROT)
                    v.wait_ge(consts, 2)
                    for m in range(NROT):
                        v.scalar_tensor_tensor(X[:, m], A[:, m], 1.0 / HORNER, eye, ALU.mult, ALU.add).then_inc(X_ok, 1)
                    for s, k in enumerate(range(HORNER - 1, 0, -1)):
                        for m in range(NROT):
                            v.wait_ge(horner_ps, NROT * s + m + 1)
                            v.scalar_tensor_tensor(X[:, m], bank[:, m, :].rearrange("p (c j) -> p c j", c=KC), 1.0 / k, eye,
                                                   ALU.mult, ALU.add).then_inc(X_ok, 1)
                    v.wait_ge(s_ok, 1)
                    s = v.value_load(sqi[0:1, 0:1], min_val=1, max_val=24)
                    with v.Fori(0, s) as i:
                        for m in range(NROT):
                            v.wait_ge(sq_Y, i * NROT + (m + 1))
                            v.tensor_copy(X[:, m], bank[:, NROT + m, :].rearrange("p (c j) -> p c j", c=KC)).then_inc(X_ok, 1)
                    v.wait_ge(rot_Y, 1)
                    v.tensor_copy(X[:, 0], bank[:, 6, :].rearrange("p (c j) -> p c j", c=KC)).then_inc(rot_ok, 1)
                    v.wait_ge(rot_Y, 2)
                    v.tensor_copy(R, bank[:, 7, :].rearrange("p (c j) -> p c j", c=KC)).then_inc(rot_ok, 1)
                    v.wait_ge(consts, 12)
                    v.wait_ge(beta_mm, 1)
                    then(v.tensor_tensor(eb1s, eb1s, bank[0:E, 3, :], ALU.add))
                    then(v.tensor_tensor(row[:, 0, :], row[:, 0, :], bank[0:1, 4, 0:C], ALU.add))
                    then(v.tensor_tensor(gateb[:], grow, bank[0:1, 4, C:C + E], ALU.add))
                    parts(eb1p, eb1s, H, E)
                    parts(abbp, row[:, 0, :], C, 1)
                    for c in range(KC):
                        v.tensor_scalar(ew1[:, c], ew1[:, c], gam[:, c:c + 1], None, ALU.mult)
                        v.tensor_scalar(abw[:, c], abw[:, c], gam[:, c:c + 1], None, ALU.mult)
                        v.tensor_scalar(gw[:, c], gw[:, c], gam[:, c:c + 1], None, ALU.mult)
                    v.wait_ge(at_ps, 4)
                    then(v.tensor_tensor(row[:, 2, :], row[:, 1, :], bank[0:1, 5, 0:C], ALU.add))
                    parts(vbp, row[:, 2, :], C, 1)
                    v.tensor_scalar(qbias[:], bank[:, 6, 0:KC], C ** -0.5, None, ALU.mult).then_inc(vb_ok, 1)
                    v.wait_ge(eb2_Y, 1)
                    then(v.tensor_copy(rem2[0:E, :], bank[0:E, 2, 0:C]))
                    parts(eb2p, rem2[0:E, :], C, E)
                    for e in range(E):
                        v.wait_ge(fold_Y, e + 1)
                        v.tensor_copy(ew2[:, :, e, :], psum(6, 2).rearrange("p (h c) -> p h c", h=HC)).then_inc(fold_ok, 1)

                @block.scalar
                def _(act):
                    act.dma_start(gens, d["L0_ffn_gens"].rearrange("m (c p) j -> p m c j", p=P)).then_inc(w_gens, 16)
                    for o, k in zip(w4, "qkvo"):
                        act.dma_start(o, d[f"L0_attn_b_W{k}"].rearrange("(c p) n -> p c n", p=P)).then_inc(w_proj, 16)
                    for q in range(4):
                        ts = slice(q * NT // 4, (q + 1) * NT // 4)
                        act.dma_start(xs[:, ts, :], d["L0_attn_a_x"].rearrange("b (n p) c -> p (b n) c", p=P)[:, ts, :]
                                      ).then_inc(x_in, 16)
                    act.dma_start(wqkv[:], d["L0_attn_a_Wqkv"].rearrange("(c p) n -> p c n", p=P)).then_inc(x_in, 16)
                    act.dma_start(wout[:], d["L0_attn_a_Wout"]).then_inc(x_in, 16)
                    for b in range(B):
                        act.dma_start(ctxm[HD:HD + 1, b, :], d["L0_attn_a_bout"].rearrange("(o n) -> o n", o=1)).then_inc(x_in, 16)
                    for m in range(NROT):
                        act.wait_ge(AT_ps, m + 1)
                        copy(act, AT[:, m], bank[:, m, :].rearrange("p (c j) -> p c j", c=KC)).then_inc(AT_ok, 1)
                    act.wait_ge(s_ok, 1)
                    s = act.value_load(sqi[0:1, 0:1], min_val=1, max_val=24)
                    with act.Fori(0, s) as i:
                        for m in range(NROT):
                            act.wait_ge(sq_T, i * NROT + (m + 1))
                            copy(act, AT[:, m], bank[:, m, :].rearrange("p (c j) -> p c j", c=KC)).then_inc(ET_ok, 1)
                    for q in range(2):
                        act.wait_ge(rot_T, q + 1)
                        copy(act, AT[:, 0], bank[:, 0, :].rearrange("p (c j) -> p c j", c=KC)).then_inc(rot_TS, 1)
                    act.wait_ge(at_ps, 1)
                    copy(act, wa[:], bank[:, 0, :].rearrange("p (c j) -> p c j", c=KC), C ** -0.5).then_inc(at_ok, 1)
                    act.wait_ge(at_ps, 2)
                    copy(act, woT, bank[:, 1, :].rearrange("p (c j) -> p c j", c=KC)).then_inc(at_ok, 1)
                    act.wait_ge(at_ps, 3)
                    copy(act, wvo[:], bank[:, 2, :].rearrange("p (c j) -> p c j", c=KC)).then_inc(at_ok, 1)
                    act.wait_ge(eb2_T, 1)
                    copy(act, eb2T, bank[:, 0, 0:KC * E].rearrange("p (c e) -> p c e", c=KC)).then_inc(eb2_TS, 1)
                    for e in range(E):
                        act.wait_ge(fold_T, e + 1)
                        if e >= 2:
                            act.wait_ge(fold_Y, e - 1)
                        copy(act, ew2T[e % 2], psum(4, 2).rearrange("p (c h) -> p c h", c=KC)).then_inc(fold_TS, 1)

                @block.tensor
                def _(pe):
                    def transposed(b, src, m):
                        for kc in range(KC):
                            for ic in range(KC):
                                last = pe.transpose(bank[:, b, kc * C + ic * P:kc * C + (ic + 1) * P],
                                                    src[:, ic, kc * P:(kc + 1) * P], ident[:])
                        return last

                    def product(b, leftT, right):
                        for rc in range(KC):
                            for kc in range(KC):
                                last = pe.matmul(bank[:, b, rc * C:(rc + 1) * C], leftT[:, kc, rc * P:(rc + 1) * P],
                                                 right[:, kc, :], start=(kc == 0), stop=(kc == KC - 1))
                        return last

                    pe.wait_ge(consts, 1)
                    for m in range(NROT):
                        pe.wait_ge(A_ok, m + 1)
                        transposed(m, A[:, m], m).then_inc(AT_ps, 1)
                    for s in range(HORNER - 1):
                        for m in range(NROT):
                            if s == 0:
                                pe.wait_ge(AT_ok, m + 1)
                            pe.wait_ge(X_ok, NROT * s + m + 1)
                            product(m, AT[:, m], X[:, m]).then_inc(horner_ps, 1)
                    pe.wait_ge(s_ok, 1)
                    done = NROT * (HORNER - 1)
                    s = pe.value_load(sqi[0:1, 0:1], min_val=1, max_val=24)
                    with pe.Fori(0, s) as i:
                        for m in range(NROT):
                            pe.wait_ge(X_ok, i * NROT + (done + m + 1))
                            transposed(m, X[:, m], m).then_inc(sq_T, 1)
                        for m in range(NROT):
                            pe.wait_ge(ET_ok, i * NROT + (m + 1))
                            product(NROT + m, AT[:, m], X[:, m]).then_inc(sq_Y, 1)
                    pe.wait_ge(X_ok, s * NROT + (done + NROT))
                    transposed(0, X[:, 0], 0).then_inc(rot_T, 1)
                    pe.wait_ge(rot_TS, 1)
                    product(6, AT[:, 0], X[:, 1]).then_inc(rot_Y, 1)
                    pe.wait_ge(rot_ok, 1)
                    transposed(0, X[:, 0], 0).then_inc(rot_T, 1)
                    pe.wait_ge(rot_TS, 2)
                    product(7, AT[:, 0], X[:, 2]).then_inc(rot_Y, 1)
                    pe.wait_ge(w_small, 16 * 14)
                    pe.wait_ge(w_ew, 16 * (KC + HC))
                    pe.wait_ge(bsel_ok, 1)
                    for e in range(E):
                        for c in range(KC):
                            pe.matmul(bank[0:E, 3, :], bsel[:, c, e * E:(e + 1) * E], ew1[:, c, e, :],
                                      start=(e == 0 and c == 0), stop=(e == E - 1 and c == KC - 1))
                    for c in range(KC):
                        pe.matmul(bank[0:1, 4, 0:C], bet[:, c:c + 1], abw[:, c, :], start=(c == 0), stop=(c == KC - 1))
                    for c in range(KC):
                        last = pe.matmul(bank[0:1, 4, C:C + E], bet[:, c:c + 1], gw[:, c, :],
                                         start=False, stop=(c == KC - 1), skip_group_check=True)
                    last.then_inc(beta_mm, 1)
                    pe.wait_ge(w_proj, 16 * 4)
                    wq, wk, wv, wo = w4
                    product(0, wq, wk).then_inc(at_ps, 1)
                    transposed(1, wo, 0).then_inc(at_ps, 1)
                    pe.wait_ge(at_ok, 2)
                    product(2, wv, woT).then_inc(at_ps, 1)
                    for c in range(KC):
                        pe.matmul(bank[0:1, 5, 0:C], bvc[:, c:c + 1], woT[:, c, :], start=(c == 0), stop=(c == KC - 1))
                    for j in range(KC):
                        for c in range(KC):
                            last = pe.matmul(bank[:, 6, j:j + 1], wk[:, c, j * P:(j + 1) * P], bqc[:, c:c + 1],
                                             start=(j == 0 and c == 0), stop=(c == KC - 1), skip_group_check=True)
                    last.then_inc(at_ps, 1)
                    pe.wait_ge(rot_ok, 2)
                    pe.wait_ge(at_ok, 3)
                    for c in range(KC):
                        last = pe.transpose(bank[:, 0, c * E:(c + 1) * E], eb2s[:, c * P:(c + 1) * P], ident[0:E, 0:E])
                    last.then_inc(eb2_T, 1)
                    pe.wait_ge(eb2_TS, 1)
                    for c in range(KC):
                        last = pe.matmul(bank[0:E, 2, 0:C], eb2T[:, c, :], R[:, c, :], start=(c == 0), stop=(c == KC - 1))
                    last.then_inc(eb2_Y, 1)
                    pe.wait_ge(vb_ok, 1)
                    for e in range(E + 1):
                        if e < E:
                            pe.wait_ge(fold_TS, e)
                            for c in range(KC):
                                for h in range(HC):
                                    last = pe.transpose(bank[:, 4 + c, h * P:(h + 1) * P], ew2[:, h, e, c * P:(c + 1) * P], ident[:])
                            last.then_inc(fold_T, 1)
                        if e >= 1:
                            pe.wait_ge(fold_TS, e)
                            if e >= 2:
                                pe.wait_ge(fold_ok, e - 1)
                            y = psum(6, 2).rearrange("p (h c) -> p h c", h=HC)
                            for h in range(HC):
                                for c in range(KC):
                                    last = pe.matmul(y[:, h, :], ew2T[(e - 1) % 2][:, c, h * P:(h + 1) * P], R[:, c, :],
                                                     start=(c == 0), stop=(c == KC - 1))
                            last.then_inc(fold_Y, 1)


        def after(eng, semaphore, value):
            if not isinstance(value, int) or value >= 1:
                eng.wait_ge(semaphore, value)

        class Norm:
            def __init__(self, name, arena):
                self.st = [arena.take(GT, 6) for _ in range(2)]
                self.sum = [arena.take(GT) for _ in range(2)]
                self.dif, self.m2, self.var = arena.take(GT), arena.take(GT), arena.take(GT)
                self.arg = [arena.take(2, GT) for _ in range(2)]
                self.root = [arena.take(2, GT) for _ in range(2)]
                self.stats_ok, self.sums_ok = sem(name + "_stats"), sem(name + "_sums")
                self.var_ok, self.arg_ok, self.root_ok = sem(name + "_var"), sem(name + "_arg"), sem(name + "_root")

            def statistics(self, v, n, tiles):
                u = n % 2
                st, dif, m2, var = self.st[u], self.dif, self.m2, self.var
                for t in range(GT):
                    v.bn_stats(st[:, t, :], tiles[:, t, :]).then_inc(self.stats_ok, 1)
                v.wait_ge(self.stats_ok, GT * (n + 1))
                v.tensor_tensor(self.sum[u], st[:, :, 1], st[:, :, 4], ALU.add).then_inc(self.sums_ok, 1)
                v.tensor_tensor(dif, st[:, :, 1], st[:, :, 4], ALU.subtract).then_inc(self.sums_ok, 1)
                v.tensor_tensor(m2, st[:, :, 2], st[:, :, 5], ALU.add).then_inc(self.sums_ok, 1)
                v.wait_ge(self.sums_ok, 3 * (n + 1))
                v.scalar_tensor_tensor(dif, dif, 0.25, dif, ALU.mult, ALU.mult).then_inc(self.var_ok, 1)
                v.wait_ge(self.var_ok, 2 * n + 1)
                v.scalar_tensor_tensor(var, m2, 1.0 / C, dif, ALU.mult, ALU.add).then_inc(self.var_ok, 1)
                v.wait_ge(self.var_ok, 2 * n + 2)
                v.tensor_scalar(self.arg[u][:, 0, :], var, EPS, None, ALU.add).then_inc(self.arg_ok, 1)
                v.tensor_scalar(self.arg[u][:, 1, :], var, 1.0 + EPS, EPS * EPS, ALU.mult, ALU.add).then_inc(self.arg_ok, 1)

            def roots(self, pool, n):
                u = n % 2
                pool.wait_ge(self.arg_ok, 2 * (n + 1))
                pool.tensor_tensor(self.root[u].rearrange("p a t -> p (a t)"), self.arg[u].rearrange("p a t -> p (a t)"),
                                   mhalf[:], ALU.pow).then_inc(self.root_ok, 1)

        qT = work[0:HD + 1, 0:T]
        route = Arena(work[:, 6560:7136])
        logits, zab = route.take(NT, E), route.take(NT)
        wts, slot = route.take(2, NT), route.take(2, NT, dt=I32)
        texp = route.take(SLOTS, dt=I32)

        def context():
            a = Arena(flat(ab))
            ln = [a.take(GT, C) for _ in range(2)]
            lnT = [a.take(KC, BANK) for _ in range(2)]
            vs = [a.take(GT, HD) for _ in range(2)]
            ks = [a.take(GT * HEADS, DH) for _ in range(2)]
            kmax, ksum = a.take(GT * HEADS), a.take(GT * HEADS)
            nb = [a.take(GT) for _ in range(2)]
            cm = [a.take(HD, rows=HD) for _ in range(B)]
            nrm = Norm("a", a)
            nb_ok, ln_ok, lnT_ps, lnT_ok = sem("a_nb"), sem("a_ln"), sem("a_lnT_ps"), sem("a_lnT")
            kvq_ps, vq_ok, kmax_ok, ksh_ok = sem("a_kvq_ps"), sem("a_vq"), sem("a_kmax"), sem("a_kshift")
            kexp_ok, ksum_ok, k_ok, ctx_ps = sem("a_kexp"), sem("a_ksum"), sem("a_k"), sem("a_ctx_ps")
            cm_ok, m_ps, ones_ok, m_ok = sem("a_cm"), sem("a_m_ps"), sem("a_ones"), sem("a_m")
            GB = NG // B

            with nc.Block() as block:
                @block.gpsimd
                def _(pool):
                    pool.memset(work[HD:HD + 1, 0:T], 1.0).then_inc(ones_ok, 1)
                    pool.wait_ge(ones_ok, 1)
                    for g in range(NG):
                        nrm.roots(pool, g)

                @block.vector
                def _(v):
                    v.wait_ge(x_in, 16 * 8)
                    for g in range(NG + 1):
                        if g < NG:
                            u = g % 2
                            nrm.statistics(v, g, xs[:, g * GT:(g + 1) * GT, :])
                            v.wait_ge(nrm.root_ok, g + 1)
                            v.scalar_tensor_tensor(nb[u], nrm.sum[u], -0.5, nrm.root[u][:, 0, :], ALU.mult, ALU.mult
                                                   ).then_inc(nb_ok, 1)
                            v.wait_ge(nb_ok, g + 1)
                            after(v, lnT_ps, g - 1)
                            for t in range(GT):
                                v.tensor_scalar(ln[u][:, t, :], xs[:, g * GT + t, :], nrm.root[u][:, 0, t:t + 1],
                                                nb[u][:, t:t + 1], ALU.mult, ALU.add).then_inc(ln_ok, 1)
                        if g >= 1:
                            h, u = g - 1, (g - 1) % 2
                            kps = bank[:, 4, :].rearrange("p (t x) -> p t x", t=GT)[:, :, 0:HD].rearrange(
                                "p t (h e) -> p t h e", h=HEADS)
                            k4 = ks[u].rearrange("p (t h) e -> p t h e", t=GT)
                            v.wait_ge(kvq_ps, h + 1)
                            v.tensor_reduce(kmax.rearrange("p (t h) -> p t h", t=GT), kps, AX.X, ALU.max).then_inc(kmax_ok, 1)
                            v.wait_ge(kmax_ok, h + 1)
                            after(v, ctx_ps, h - 1)
                            v.tensor_tensor(k4, kps, cols(kmax.rearrange("p (t h) -> p t h", t=GT), DH), ALU.subtract
                                            ).then_inc(ksh_ok, 1)
                            v.wait_ge(kexp_ok, h + 1)
                            v.tensor_reduce(ksum, ks[u], AX.X, ALU.add).then_inc(ksum_ok, 1)
                            v.wait_ge(ksum_ok, 2 * h + 1)
                            v.reciprocal(ksum, ksum).then_inc(ksum_ok, 1)
                            v.wait_ge(ksum_ok, 2 * h + 2)
                            v.tensor_tensor(ks[u], ks[u], cols(ksum, DH), ALU.mult).then_inc(k_ok, 1)
                    for b in range(B):
                        v.wait_ge(ctx_ps, GB * (b + 1))
                        v.tensor_tensor(cm[b], bank[0:HD, 6 + b, 0:HD], hmask[:], ALU.mult).then_inc(cm_ok, 1)

                @block.scalar
                def _(act):
                    for g in range(NG + 1):
                        if g < NG:
                            u = g % 2
                            act.wait_ge(lnT_ps, g + 1)
                            after(act, kvq_ps, g - 1)
                            copy(act, lnT[u].rearrange("p c n -> p (c n)"), psum(2 * u, 2)).then_inc(lnT_ok, 1)
                        if g >= 1:
                            h, u = g - 1, (g - 1) % 2
                            act.wait_ge(kvq_ps, h + 1)
                            after(act, ctx_ps, h - 1)
                            copy(act, qT[0:HD, h * BANK:(h + 1) * BANK], bank[0:HD, 5, :]).then_inc(vq_ok, 1)
                            act.wait_ge(ksh_ok, h + 1)
                            copy(act, vs[u], bank[:, 4, :].rearrange("p (t x) -> p t x", t=GT)[:, :, HD:2 * HD]).then_inc(vq_ok, 1)
                            act.activation(ks[u], ks[u], ACT.Exp).then_inc(kexp_ok, 1)
                    for b in range(B):
                        act.wait_ge(m_ps, b + 1)
                        copy(act, ctxm[0:HD, b, :], bank[0:HD, 2 * b, 0:C], HD ** -0.5).then_inc(m_ok, 1)

                @block.tensor
                def _(pe):
                    for g in range(NG + 2):
                        if g < NG:
                            u = g % 2
                            pe.wait_ge(ln_ok, GT * (g + 1))
                            after(pe, lnT_ok, g - 1)
                            for c in range(KC):
                                for t in range(GT):
                                    last = pe.transpose(bank[:, 2 * u + c, t * P:(t + 1) * P], ln[u][:, t, c * P:(c + 1) * P],
                                                        ident[:])
                            last.then_inc(lnT_ps, 1)
                        if 1 <= g <= NG:
                            h, u = g - 1, (g - 1) % 2
                            pe.wait_ge(lnT_ok, h + 1)
                            after(pe, ksh_ok, h)
                            after(pe, vq_ok, 2 * h)
                            for t in range(GT):
                                for c in range(KC):
                                    pe.matmul(bank[:, 4, t * 2 * HD:(t + 1) * 2 * HD], lnT[u][:, c, t * P:(t + 1) * P],
                                              wqkv[:, c, HD:3 * HD], start=(c == 0), stop=(c == KC - 1))
                            for c in range(KC):
                                last = pe.matmul(bank[0:HD, 5, :], wqkv[:, c, 0:HD], lnT[u][:, c, :],
                                                 start=(c == 0), stop=(c == KC - 1))
                            last.then_inc(kvq_ps, 1)
                        if g >= 2:
                            h, u = g - 2, (g - 2) % 2
                            b = h // GB
                            pe.wait_ge(k_ok, h + 1)
                            pe.wait_ge(vq_ok, 2 * (h + 1))
                            for t in range(GT):
                                last = pe.matmul(bank[0:HD, 6 + b, 0:HD], vs[u][:, t, :],
                                                 ks[u].rearrange("p (t h) e -> p t (h e)", t=GT)[:, t, :],
                                                 start=(h % GB == 0 and t == 0), stop=(h % GB == GB - 1 and t == GT - 1))
                            last.then_inc(ctx_ps, 1)
                    for b in range(B):
                        pe.wait_ge(cm_ok, b + 1)
                        pe.matmul(bank[0:HD, 2 * b, 0:C], cm[b], wout[:], start=True, stop=True).then_inc(m_ps, 1)

        def front(r):
            a = Arena(work[:, T:6560])
            xT = [a.take(KC, BANK) for _ in range(2)]
            nrm = Norm(f"f{r}", a)
            nb = [a.take(2, GT) for _ in range(2)]
            c1 = [a.take(GT) for _ in range(2)]
            junk = a.take(C, dt=BF16)
            att_ps, x1_ok, nb_ok, xh_ok = sem(f"f{r}_att_ps"), sem(f"f{r}_x1"), sem(f"f{r}_nb"), sem(f"f{r}_xh")
            res_ok, xT_ps, xT_ok, mm_ps = sem(f"f{r}_res"), sem(f"f{r}_xT_ps"), sem(f"f{r}_xT"), sem(f"f{r}_mm_ps")
            gelu_ok, lg_ok, zab_ok, sum_ok = sem(f"f{r}_gelu"), sem(f"f{r}_logits"), sem(f"f{r}_zab"), sem(f"f{r}_sum")

            with nc.Block() as block:
                @block.gpsimd
                def _(pool):
                    for g in range(NG + 1):
                        if g < NG:
                            nrm.roots(pool, g)
                        if g >= 1:
                            gs = slice((g - 1) * GT, g * GT)
                            pool.wait_ge(res_ok, GT * g)
                            pool.wait_ge(gelu_ok, g)
                            pool.tensor_tensor(xs[:, gs, :], xs[:, gs, :], ab[:, gs, :], ALU.add).then_inc(sum_ok, 1)

                @block.vector
                def _(v):
                    for g in range(NG + 1):
                        if g < NG:
                            u = g % 2
                            if r == 0:
                                v.wait_ge(att_ps, g + 1)
                                for h in range(2):
                                    x2 = xs[:, g * GT + 2 * h:g * GT + 2 * h + 2, :].rearrange("p t c -> p (t c)")
                                    v.tensor_tensor(x2, x2, bank[:, h, :], ALU.add).then_inc(x1_ok, 1)
                                v.wait_ge(x1_ok, 2 * (g + 1))
                            nrm.statistics(v, g, xs[:, g * GT:(g + 1) * GT, :])
                            v.wait_ge(nrm.root_ok, g + 1)
                            for k in range(2):
                                v.scalar_tensor_tensor(nb[u][:, k, :], nrm.sum[u], -0.5, nrm.root[u][:, k, :], ALU.mult, ALU.mult
                                                       ).then_inc(nb_ok, 1)
                            v.tensor_scalar(c1[u], nrm.root[u][:, 0, :], 1.0, None, ALU.add).then_inc(nb_ok, 1)
                            v.wait_ge(nb_ok, 3 * (g + 1))
                            for t in range(GT):
                                v.tensor_scalar(xh[:, g * GT + t, :], xs[:, g * GT + t, :], nrm.root[u][:, 1, t:t + 1],
                                                nb[u][:, 1, t:t + 1], ALU.mult, ALU.add).then_inc(xh_ok, 1)
                            for t in range(GT):
                                v.tensor_scalar(xs[:, g * GT + t, :], xs[:, g * GT + t, :], c1[u][:, t:t + 1],
                                                nb[u][:, 0, t:t + 1], ALU.mult, ALU.add).then_inc(res_ok, 1)
                        if g >= 1:
                            h = g - 1
                            v.wait_ge(mm_ps, h + 1)
                            v.tensor_copy(logits[:, h * GT:(h + 1) * GT, :], bank[:, 6, 0:GT * E].rearrange("p (t e) -> p t e", t=GT)
                                          ).then_inc(lg_ok, 1)
                            v.wait_ge(gelu_ok, h + 1)
                            for t in range(h * GT, (h + 1) * GT):
                                after(v, zab_ok, t)
                                v.scalar_tensor_tensor(junk, ab[:, t, :], 1.0, gcw[:, 1, :], ALU.mult, ALU.mult,
                                                       accum_out=zab[:, t:t + 1]).then_inc(zab_ok, 1)

                @block.scalar
                def _(act):
                    for g in range(NG + 1):
                        if g < NG:
                            act.wait_ge(xT_ps, g + 1)
                            after(act, mm_ps, g - 1)
                            copy(act, xT[g % 2].rearrange("p c n -> p (c n)"), psum(2, 2)).then_inc(xT_ok, 1)
                        if g >= 1:
                            act.wait_ge(mm_ps, g)
                            act.activation(ab[:, (g - 1) * GT:g * GT, :].rearrange("p t c -> p (t c)"), psum(4, 2), ACT.Gelu
                                           ).then_inc(gelu_ok, 1)

                @block.tensor
                def _(pe):
                    def attend(g):
                        after(pe, x1_ok, 2 * g)
                        for t in range(GT):
                            last = pe.matmul(bank[:, t // 2, (t % 2) * C:(t % 2 + 1) * C],
                                             qT[:, (g * GT + t) * P:(g * GT + t + 1) * P], ctxm[:, g * B // NG, :],
                                             start=True, stop=True)
                        last.then_inc(att_ps, 1)

                    if r == 0:
                        attend(0)
                    for g in range(NG + 1):
                        if r == 0 and g + 1 < NG:
                            attend(g + 1)
                        if g < NG:
                            pe.wait_ge(xh_ok, GT * (g + 1))
                            after(pe, xT_ok, g)
                            for c in range(KC):
                                for t in range(GT):
                                    last = pe.transpose(bank[:, 2 + c, t * P:(t + 1) * P], xh[:, g * GT + t, c * P:(c + 1) * P],
                                                        ident[:])
                            last.then_inc(xT_ps, 1)
                        if g >= 1:
                            h, u = g - 1, (g - 1) % 2
                            pe.wait_ge(xT_ok, h + 1)
                            after(pe, gelu_ok, h)
                            after(pe, lg_ok, h)
                            for t in range(GT):
                                lhs = [xT[u][:, c, t * P:(t + 1) * P] for c in range(KC)]
                                o = bank[:, 6, t * E:(t + 1) * E]
                                for c in range(KC):
                                    pe.matmul(o, lhs[c], gw[:, c, :], start=(c == 0), stop=False)
                                pe.matmul(o, onesf[:], gateb[:], start=False, stop=True)
                                o = bank[:, 4 + t // 2, (t % 2) * C:(t % 2 + 1) * C]
                                for c in range(KC):
                                    pe.matmul(o, lhs[c], abw[:, c, :], start=(c == 0), stop=False)
                                last = pe.matmul(o, onesb[0:2 * QROW + 1, :], abbp[:], start=False, stop=True)
                            last.then_inc(mm_ps, 1)

        def mixture(r):
            a = Arena(work[:, 0:6560])
            RING = 4
            xr = [a.take(C) for _ in range(RING)]
            xrT = [a.take(KC, P) for _ in range(2)]
            hid = [a.take(H) for _ in range(2)]
            hidT = [a.take(HC, P) for _ in range(2)]
            yr = [a.take(C) for _ in range(RING)]
            rt = Arena(work[:, 0:6560])
            m1, m2, i1, i2 = (rt.take(NT) for _ in range(4))
            eq, cand, oh1, oh2, l2 = (rt.take(NT, E) for _ in range(5))
            cnt = rt.take(NT, E, dt=BF16)
            incl, pos = rt.take(NT, E), rt.take(NT, E)
            ones = rt.take(NT)
            ntile, tincl, texcl = rt.take(E), rt.take(E), rt.take(E)
            cmpn, cmpt = rt.take(E, NT), rt.take(SLOTS, E - 1)
            posf, tf = rt.take(2, NT), rt.take(SLOTS)
            cb = Arena(work[:, 0:6560])
            g1 = [cb.take(C) for _ in range(RING)]
            g2 = [cb.take(C) for _ in range(RING)]
            dif = [cb.take(C) for _ in range(2 * GT)]
            junk = cb.take(C)
            z = [cb.take(GT) for _ in range(2)]
            dve = sem(f"m{r}_order")
            cnt_ok, rank_ps, d_ok, ed_ok = sem(f"m{r}_cnt"), sem(f"m{r}_rank_ps"), sem(f"m{r}_d"), sem(f"m{r}_ed")
            wts_ok = sem(f"m{r}_wts")
            slot_ok, texp_ok, scat = sem(f"m{r}_slot"), sem(f"m{r}_texp"), sem(f"m{r}_scattered")
            x_ld = [sem(f"m{r}_x_loaded{k}") for k in range(RING)]
            y_st = [sem(f"m{r}_y_stored{k}") for k in range(RING)]
            xrT_ps, xrT_ok, up_ps, hid_ok = sem(f"m{r}_xT_ps"), sem(f"m{r}_xT"), sem(f"m{r}_up_ps"), sem(f"m{r}_hid")
            hidT_ps, hidT_ok, dn_ps, y_ok = sem(f"m{r}_hidT_ps"), sem(f"m{r}_hidT"), sem(f"m{r}_down_ps"), sem(f"m{r}_y")
            g_ld = [sem(f"m{r}_gathered{k}") for k in range(RING)]
            dif_ok, z_ok, ez_ok, gate_ok, x2_ok = (sem(f"m{r}_dif"), sem(f"m{r}_z"), sem(f"m{r}_ez"), sem(f"m{r}_gate"),
                                                   sem(f"m{r}_x2"))
            o_st = sem(f"m{r}_stored")
            ZN = GT + 2
            FIRST = 2 * RING - 1
            TURNS = (SLOTS - 1 - FIRST) // RING
            TAIL = FIRST + TURNS * RING

            def over_tiles(eng, step):
                for j in range(FIRST):
                    step(j, j % RING, j // RING)
                with eng.Fori(0, TURNS) as i:
                    for k in range(RING):
                        step(i * RING + (FIRST + k), (FIRST + k) % RING, i + (FIRST + k) // RING)
                for j in range(TAIL, SLOTS):
                    step(j, j % RING, j // RING)

            def is_last(j):
                return isinstance(j, int) and j == SLOTS - 1

            with nc.Block() as block:
                @block.vector
                def _(v):
                    n = 0

                    def then(ins):
                        nonlocal n
                        n += 1
                        ins.then_inc(dve, 1)
                        v.wait_ge(dve, n)

                    eb = eidx[:].unsqueeze(1).to_broadcast([P, NT, E])

                    def best(src, m, i, oh):
                        then(v.tensor_reduce(m, src, AX.X, ALU.max))
                        then(v.tensor_tensor(eq, src, cols(m, E), ALU.is_ge))
                        then(v.tensor_tensor(cand, eq, eb, ALU.mult))
                        then(v.tensor_reduce(i, cand, AX.X, ALU.min))
                        then(v.tensor_tensor(oh, eb, cols(i, E), ALU.is_equal))

                    best(logits, m1, i1, oh1)
                    then(v.scalar_tensor_tensor(l2, oh1, LOWEST, logits, ALU.mult, ALU.add))
                    best(l2, m2, i2, oh2)
                    v.tensor_tensor(cnt, oh1, oh2, ALU.add).then_inc(cnt_ok, 1)
                    v.tensor_tensor(m2, m2, m1, ALU.subtract).then_inc(d_ok, 1)
                    then(v.memset(ones, 1.0))
                    v.wait_ge(rank_ps, 1)
                    tot = bank[:, 1, 0:NT * E].rearrange("p (t e) -> p t e", e=E)
                    for e in range(E):
                        last = v.tensor_tensor_scan(incl[:, :, e], ones, tot[:, :, e], 0.0, ALU.mult, ALU.add)
                    then(last)
                    then(v.tensor_tensor(cmpn, cols(incl[:, NT - 1, :], NT), steps[:].unsqueeze(1).to_broadcast([P, E, NT]), ALU.is_gt))
                    then(v.tensor_reduce(ntile, cmpn, AX.X, ALU.add))
                    then(v.tensor_tensor_scan(tincl, ones[:, 0:E], ntile, 0.0, ALU.mult, ALU.add))
                    then(v.tensor_tensor(texcl, tincl, ntile, ALU.subtract))
                    then(v.tensor_tensor(pos, incl, tot, ALU.subtract))
                    then(v.tensor_tensor(pos, pos, bank[:, 0, 0:NT * E].rearrange("p (t e) -> p t e", e=E), ALU.add))
                    then(v.scalar_tensor_tensor(pos, texcl.unsqueeze(1).to_broadcast([P, NT, E]), float(P), pos, ALU.mult, ALU.add))
                    for k, oh in enumerate((oh1, oh2)):
                        then(v.tensor_tensor(cand, oh, pos, ALU.mult))
                        then(v.tensor_reduce(posf[:, k, :], cand, AX.X, ALU.add))
                    v.tensor_copy(slot, posf).then_inc(slot_ok, 1)
                    then(v.tensor_tensor(cmpt, cols(sidx[:], E - 1), tincl[:, 0:E - 1].unsqueeze(1).to_broadcast([P, SLOTS, E - 1]), ALU.is_ge))
                    then(v.tensor_reduce(tf, cmpt, AX.X, ALU.add))
                    v.tensor_copy(texp, tf).then_inc(texp_ok, 1)
                    v.wait_ge(ed_ok, 1)
                    then(v.tensor_scalar(i1, m1, 1.0, None, ALU.add))
                    then(v.reciprocal(wts[:, 0, :], i1))
                    v.tensor_tensor(wts[:, 1, :], m1, wts[:, 0, :], ALU.mult).then_inc(wts_ok, 1)

                    def copy_x(j, k, turn):
                        v.wait_ge(xrT_ps, j + 1)
                        after(v, up_ps, j - 1)
                        v.tensor_copy(xrT[k % 2].rearrange("p c n -> p (c n)"), bank[:, k % 2, 0:C]).then_inc(xrT_ok, 1)

                    def step(j, k, turn):
                        if not is_last(j):
                            copy_x(j + 1, k + 1, turn)
                        v.wait_ge(hidT_ps, j + 1)
                        after(v, dn_ps, j - 1)
                        v.tensor_copy(hidT[k % 2].rearrange("p c n -> p (c n)"), bank[:, 4 + k % 2, :]).then_inc(hidT_ok, 1)

                    copy_x(0, 0, 0)
                    over_tiles(v, step)

                    v.wait_ge(y_ok, SLOTS)
                    for g in range(NG + 1):
                        if g < NG:
                            for t in range(g * GT, (g + 1) * GT):
                                q, k = dif[t % (2 * GT)], t % RING
                                v.wait_ge(g_ld[k], 32 * (t // RING + 1))
                                after(v, x2_ok, t - 2 * GT + 1)
                                v.scalar_tensor_tensor(q, g1[k], wts[:, 0, t:t + 1], ab[:, t, :], ALU.mult, ALU.subtract).then_inc(dif_ok, 1)
                                v.wait_ge(dif_ok, 2 * t + 1)
                                v.scalar_tensor_tensor(q, g2[k], wts[:, 1, t:t + 1], q, ALU.mult, ALU.add).then_inc(dif_ok, 1)
                                v.wait_ge(dif_ok, 2 * t + 2)
                                after(v, z_ok, ZN * g + t % GT)
                                v.scalar_tensor_tensor(junk, q, 1.0, gcw[:, 0, :], ALU.mult, ALU.mult,
                                                       accum_out=z[g % 2][:, t % GT:t % GT + 1]).then_inc(z_ok, 1)
                            v.wait_ge(z_ok, ZN * g + GT)
                            v.scalar_tensor_tensor(z[g % 2], z[g % 2], gcb[:], zab[:, g * GT:(g + 1) * GT], ALU.add, ALU.add).then_inc(z_ok, 1)
                            v.wait_ge(z_ok, ZN * g + GT + 1)
                            v.tensor_scalar(z[g % 2], z[g % 2], -87.0, None, ALU.max).then_inc(z_ok, 1)
                        if g >= 1:
                            h = g - 1
                            gate = z[h % 2]
                            v.wait_ge(ez_ok, h + 1)
                            v.tensor_scalar(gate, gate, 1.0, None, ALU.add).then_inc(gate_ok, 1)
                            v.wait_ge(gate_ok, 2 * h + 1)
                            v.reciprocal(gate, gate).then_inc(gate_ok, 1)
                            v.wait_ge(gate_ok, 2 * h + 2)
                            for t in range(h * GT, (h + 1) * GT):
                                v.scalar_tensor_tensor(xs[:, t, :], dif[t % (2 * GT)], gate[:, t % GT:t % GT + 1], xs[:, t, :],
                                                       ALU.mult, ALU.add).then_inc(x2_ok, 1)

                @block.gpsimd
                def _(pool):
                    pool.wait_ge(slot_ok, 1)
                    for t in range(NT):
                        for k in range(2):
                            pool.indirect_dma_start(out=xg, out_offset=bass.IndirectOffsetOnAxis(ap=slot[:, k, t:t + 1], axis=0),
                                                    in_=xh[:, t, :], in_offset=None).then_inc(scat, 16)
                    for k in range(RING):
                        pool.wait_ge(y_st[k], 16 * len(range(k, SLOTS, RING)))
                    for t in range(NT):
                        after(pool, dif_ok, 2 * (t - RING + 1))
                        for k, buf in enumerate((g1, g2)):
                            pool.indirect_dma_start(out=buf[t % RING], out_offset=None, in_=yg,
                                                    in_offset=bass.IndirectOffsetOnAxis(ap=slot[:, k, t:t + 1], axis=0)
                                                    ).then_inc(g_ld[t % RING], 16)

                @block.sync
                def _(sp):
                    rows = lambda dram, j: dram.rearrange("(t p) c -> t p c", p=P)[
                        j if isinstance(j, int) else bass.ds(j, 1), :, :]

                    def fetch(j, k):
                        o = xr[k % RING] if isinstance(j, int) else xr[k % RING].unsqueeze(0)
                        i = rows(xg, j)
                        sp.dma_start(xr[k % RING], i if isinstance(j, int) else i.rearrange("o p c -> (o p) c")
                                     ).then_inc(x_ld[k % RING], 16)

                    def step(j, k, turn):
                        if not isinstance(j, int) or j + RING < SLOTS:
                            sp.wait_ge(xrT_ps, j + 1)
                            fetch(j + RING, k)
                        sp.wait_ge(y_ok, j + 1)
                        o = rows(yg, j)
                        sp.dma_start(o if isinstance(j, int) else o.rearrange("o p c -> (o p) c"), yr[k]).then_inc(y_st[k], 16)

                    sp.wait_ge(scat, 16 * 2 * NT)
                    sp.wait_ge(wts_ok, 1)
                    for j in range(RING):
                        fetch(j, j)
                    over_tiles(sp, step)
                    if r == 1:
                        o = out.rearrange("b (n p) c -> p (b n) c", p=P)
                        for g in range(NG):
                            sp.wait_ge(x2_ok, GT * (g + 1))
                            sp.dma_start(o[:, g * GT:(g + 1) * GT, :], xs[:, g * GT:(g + 1) * GT, :]).then_inc(o_st, 16)
                        sp.wait_ge(o_st, 16 * NG)

                @block.scalar
                def _(act):
                    act.wait_ge(d_ok, 1)
                    act.activation(m1, m2, ACT.Exp).then_inc(ed_ok, 1)

                    def copy_y(j, k, turn):
                        act.wait_ge(dn_ps, j + 1)
                        after(act, y_st[k % RING], turn * 16)
                        copy(act, yr[k % RING], bank[:, 6 + k % 2, 0:C]).then_inc(y_ok, 1)

                    def step(j, k, turn):
                        act.wait_ge(up_ps, j + 1)
                        after(act, hidT_ps, j - 1)
                        act.activation(hid[k % 2], bank[:, 2 + k % 2, :], ACT.Gelu).then_inc(hid_ok, 1)
                        if not isinstance(j, int) or j >= 1:
                            copy_y(j - 1, (k - 1) % RING, turn if k >= 1 else turn - 1)

                    over_tiles(act, step)
                    copy_y(SLOTS - 1, (SLOTS - 1) % RING, (SLOTS - 1) // RING)
                    for g in range(NG):
                        act.wait_ge(z_ok, ZN * (g + 1))
                        act.activation(z[g % 2], z[g % 2], ACT.Exp, scale=-1.0).then_inc(ez_ok, 1)

                @block.tensor
                def _(pe):
                    pe.wait_ge(cnt_ok, 1)
                    c2 = cnt.rearrange("p t e -> p (t e)")
                    pe.matmul(bank[:, 0, 0:NT * E], tri[:], c2, start=True, stop=True)
                    pe.matmul(bank[:, 1, 0:NT * E], onesb[:], c2, start=True, stop=True).then_inc(rank_ps, 1)
                    pe.wait_ge(texp_ok, 1)

                    def expert(j):
                        return pe.value_load(texp[0:1, j:j + 1] if isinstance(j, int) else texp[0:1, bass.ds(j, 1)],
                                             min_val=0, max_val=E - 1)

                    def turn_x(j, k, turn):
                        pe.wait_ge(x_ld[k % RING], turn * 16 + 16)
                        after(pe, xrT_ok, j - 1)
                        for c in range(KC):
                            last = pe.transpose(bank[:, k % 2, c * P:(c + 1) * P], xr[k % RING][:, c * P:(c + 1) * P], ident[:])
                        last.then_inc(xrT_ps, 1)

                    def up(j, k):
                        e = expert(j)
                        pe.wait_ge(xrT_ok, j + 1)
                        after(pe, hid_ok, j - 1)
                        o = bank[:, 2 + k % 2, :]
                        for c in range(KC):
                            pe.matmul(o, xrT[k % 2][:, c, :], ew1[:, c, bass.ds(e, 1), :], start=(c == 0), stop=False)
                        pe.matmul(o, sel[:, bass.ds(e, 1), :], eb1p[:], start=False, stop=True).then_inc(up_ps, 1)

                    def turn_h(j, k):
                        pe.wait_ge(hid_ok, j + 1)
                        after(pe, hidT_ok, j - 1)
                        for c in range(HC):
                            last = pe.transpose(bank[:, 4 + k % 2, c * P:(c + 1) * P], hid[k % 2][:, c * P:(c + 1) * P], ident[:])
                        last.then_inc(hidT_ps, 1)

                    def down(j, k):
                        e = expert(j)
                        pe.wait_ge(hidT_ok, j + 1)
                        after(pe, y_ok, j - 1)
                        o = bank[:, 6 + k % 2, 0:C]
                        for c in range(HC):
                            pe.matmul(o, hidT[k % 2][:, c, :], ew2[:, c, bass.ds(e, 1), :], start=(c == 0), stop=False)
                        pe.matmul(o, sel[:, bass.ds(e, 1), :], eb2p[:], start=False, stop=True).then_inc(dn_ps, 1)

                    def step(j, k, turn):
                        up(j, k)
                        if not is_last(j):
                            turn_x(j + 1, k + 1, turn + (k + 1) // RING)
                        if not isinstance(j, int) or j >= 1:
                            down(j - 1, k - 1)
                        turn_h(j, k)

                    turn_x(0, 0, 0)
                    over_tiles(pe, step)
                    down(SLOTS - 1, SLOTS - 1)

        def attention():
            a = Arena(flat(xh))
            lnT, qpT = a.take(KC, N), a.take(KC, N)
            a2 = Arena(flat(ab))
            val = a2.take(BT, C)
            prob = [a2.take(N) for _ in range(2)]
            w = Arena(work[:])
            ln = [w.take(GT, C) for _ in range(2)]
            pT = [w.take(BANK) for _ in range(2)]
            nb = [w.take(GT) for _ in range(2)]
            nmax, rsum, rinv = w.take(BT), w.take(BT), w.take(BT)
            nrm = Norm("b", w)
            nb_ok, ln_ok, lnT_ps, lnT_ok = sem("b_nb"), sem("b_ln"), sem("b_lnT_ps"), sem("b_lnT")
            qv_ps, q_ok, v_ok = sem("b_qv_ps"), sem("b_q"), sem("b_v")
            sc_ps, max_ok, exp_ok = sem("b_sc_ps"), sem("b_max"), sem("b_exp")
            pT_ps, pT_ok, pv_ok, inv_ok, x3_ok = sem("b_pT_ps"), sem("b_pT"), sem("b_pv"), sem("b_inv"), sem("b_x3")
            GB = NG // B
            chunks = [(b, i, c) for b in range(B) for i in range(BT) for c in range(i // GT + 1)]
            at = {x: n for n, x in enumerate(chunks)}

            def weighed(n):
                return at[(n - 1) // BT, (n - 1) % BT, (n - 1) % BT // GT] + 1 if n >= 1 else 0

            def blocks(i, c):
                return min(GT, i + 1 - c * GT)

            with nc.Block() as block:
                @block.gpsimd
                def _(pool):
                    for g in range(NG):
                        nrm.roots(pool, g)

                @block.vector
                def _(v):
                    for b in range(B):
                        for g in range(b * GB, (b + 1) * GB):
                            u = g % 2
                            nrm.statistics(v, g, xs[:, g * GT:(g + 1) * GT, :])
                            v.wait_ge(nrm.root_ok, g + 1)
                            v.scalar_tensor_tensor(nb[u], nrm.sum[u], -0.5, nrm.root[u][:, 0, :], ALU.mult, ALU.mult).then_inc(nb_ok, 1)
                            v.wait_ge(nb_ok, g + 1)
                            after(v, lnT_ps, g - 1)
                            for t in range(GT):
                                v.tensor_scalar(ln[u][:, t, :], xs[:, g * GT + t, :], nrm.root[u][:, 0, t:t + 1],
                                                nb[u][:, t:t + 1], ALU.mult, ALU.add).then_inc(ln_ok, 1)
                        for i in range(BT + 1):
                            n = b * BT + i
                            if i < BT:
                                v.wait_ge(sc_ps, n + 1)
                                v.tensor_reduce(nmax[:, i:i + 1], psum(0, 4)[:, 0:(i + 1) * P], AX.X, ALU.max, negate=True).then_inc(max_ok, 1)
                            if i >= 1:
                                v.wait_ge(exp_ok, n)
                                v.reciprocal(rinv[:, i - 1:i], rsum[:, i - 1:i]).then_inc(inv_ok, 1)
                                v.wait_ge(inv_ok, n)
                                v.wait_ge(pv_ok, weighed(n))
                                v.scalar_tensor_tensor(xs[:, n - 1, :], bank[:, 6 + (n - 1) % 2, 0:C], rinv[:, i - 1:i], xs[:, n - 1, :],
                                                       ALU.mult, ALU.add).then_inc(x3_ok, 1)

                @block.scalar
                def _(act):
                    for b in range(B):
                        after(act, pv_ok, weighed(b * BT))
                        for g in range(b * GB, (b + 1) * GB + 1):
                            l = g - b * GB
                            if l < GB:
                                act.wait_ge(lnT_ps, g + 1)
                                copy(act, lnT[:, :, l * BANK:(l + 1) * BANK], bank[:, 0:2, :]).then_inc(lnT_ok, 1)
                            if l >= 1:
                                act.wait_ge(qv_ps, g)
                                for c in range(KC):
                                    act.activation(qpT[:, c, (l - 1) * BANK:l * BANK], bank[:, 2 + c, :], ACT.Identity,
                                                   bias=qbias[:, c:c + 1]).then_inc(q_ok, 1)
                                copy(act, val[:, (l - 1) * GT:l * GT, :].rearrange("p t c -> p (t c)"), psum(4, 2)).then_inc(v_ok, 1)
                        for i in range(BT + 1):
                            n = b * BT + i
                            if i >= 1:
                                for c in range((i - 1) // GT + 1):
                                    k = at[b, i - 1, c]
                                    act.wait_ge(pT_ps, k + 1)
                                    after(act, pv_ok, k - 1)
                                    wd = blocks(i - 1, c) * P
                                    copy(act, pT[k % 2][:, 0:wd], bank[:, 4 + k % 2, 0:wd]).then_inc(pT_ok, 1)
                            if i < BT:
                                act.wait_ge(max_ok, n + 1)
                                after(act, pv_ok, weighed(n - 1))
                                act.activation(prob[n % 2][:, 0:(i + 1) * P], psum(0, 4)[:, 0:(i + 1) * P], ACT.Exp,
                                               bias=nmax[:, i:i + 1], accum_out=rsum[:, i:i + 1]).then_inc(exp_ok, 1)

                @block.tensor
                def _(pe):
                    def scores(b, i):
                        n = b * BT + i
                        if i == 0:
                            pe.wait_ge(q_ok, KC * GB * (b + 1))
                            pe.wait_ge(v_ok, GB * (b + 1))
                        else:
                            pe.wait_ge(exp_ok, n)
                        for c in range(i // GT + 1):
                            wd = blocks(i, c) * P
                            for k in range(KC):
                                last = pe.matmul(bank[:, c, 0:wd], qpT[:, k, i * P:(i + 1) * P], lnT[:, k, c * BANK:c * BANK + wd],
                                                 start=(k == 0), stop=(k == KC - 1 and c < i // GT), skip_group_check=True)
                        last = pe.matmul(bank[:, i // GT, (i % GT) * P:(i % GT + 1) * P], identb[:], causal[:],
                                         start=False, stop=True, skip_group_check=True)
                        last.then_inc(sc_ps, 1)

                    def weigh(b, i):
                        n = b * BT + i
                        pe.wait_ge(exp_ok, n + 1)
                        o = bank[:, 6 + n % 2, 0:C]
                        last_c = i // GT
                        for c in range(last_c + 2):
                            if c <= last_c:
                                k = at[b, i, c]
                                after(pe, pT_ok, k - 1)
                                for q in range(blocks(i, c)):
                                    last = pe.transpose(bank[:, 4 + k % 2, q * P:(q + 1) * P],
                                                        prob[n % 2][:, (c * GT + q) * P:(c * GT + q + 1) * P], ident[:])
                                last.then_inc(pT_ps, 1)
                            if c >= 1:
                                k = at[b, i, c - 1]
                                pe.wait_ge(pT_ok, k + 1)
                                if c == 1:
                                    after(pe, x3_ok, n - 1)
                                for q in range(blocks(i, c - 1)):
                                    s = (c - 1) * GT + q
                                    last = pe.matmul(o, pT[k % 2][:, q * P:(q + 1) * P], val[:, s, :], start=(s == 0), stop=(s == i))
                                last.then_inc(pv_ok, 1)

                    for b in range(B):
                        for g in range(b * GB, (b + 1) * GB + 1):
                            l = g - b * GB
                            if l < GB:
                                u = g % 2
                                pe.wait_ge(ln_ok, GT * (g + 1))
                                after(pe, lnT_ok, g)
                                if l == 0:
                                    after(pe, exp_ok, b * BT)
                                for c in range(KC):
                                    for t in range(GT):
                                        last = pe.transpose(bank[:, c, t * P:(t + 1) * P], ln[u][:, t, c * P:(c + 1) * P], ident[:])
                                last.then_inc(lnT_ps, 1)
                            if l >= 1:
                                h, m = g - 1, l - 1
                                pe.wait_ge(lnT_ok, h + 1)
                                after(pe, q_ok, KC * h)
                                after(pe, v_ok, h)
                                for j in range(KC):
                                    for c in range(KC):
                                        pe.matmul(bank[:, 2 + j, :], wa[:, c, j * P:(j + 1) * P], lnT[:, c, m * BANK:(m + 1) * BANK],
                                                  start=(c == 0), stop=(c == KC - 1))
                                for t in range(GT):
                                    o = bank[:, 4 + t // 2, (t % 2) * C:(t % 2 + 1) * C]
                                    for c in range(KC):
                                        pe.matmul(o, lnT[:, c, (m * GT + t) * P:(m * GT + t + 1) * P], wvo[:, c, :],
                                                  start=(c == 0), stop=False)
                                    last = pe.matmul(o, onesb[0:2 * QROW + 1, :], vbp[:], start=False, stop=True)
                                last.then_inc(qv_ps, 1)
                        for i in range(BT + 1):
                            if i < BT:
                                scores(b, i)
                            if i >= 1:
                                weigh(b, i - 1)

        weights()
        context()
        release(1)
        front(0)
        mixture(0)
        attention()
        front(1)
        mixture(1)


_INS = ["L0_attn_a_x", "L0_attn_a_Wqkv", "L0_attn_a_Wout", "L0_attn_a_bout", "L0_attn_b_Wq", "L0_attn_b_bq",
        "L0_attn_b_Wk", "L0_attn_b_bk", "L0_attn_b_Wv", "L0_attn_b_bv", "L0_attn_b_Wo", "L0_attn_b_bo",
        "L0_ffn_ln_gamma", "L0_ffn_ln_beta", "L0_ffn_abel_w", "L0_ffn_abel_b", "L0_ffn_moe_gate_w",
        "L0_ffn_moe_gate_b", "L0_ffn_ew1", "L0_ffn_eb1", "L0_ffn_ew2", "L0_ffn_eb2", "L0_ffn_gens", "L0_ffn_gc_w",
        "L0_ffn_gc_b"]


def kernel(**inputs):
    import numpy as _np
    import concourse.bacc as _bacc
    from concourse import mybir as _mybir
    from concourse.bass_utils import run_bass_kernel_spmd as _run

    nc = _bacc.Bacc("TRN2", target_bir_lowering=False, num_devices=1)
    arrays, aps = {}, {}
    for name in _INS:
        a = _np.ascontiguousarray(inputs[name])
        arrays[f"in_{name}_dram"] = a
        aps[name] = nc.dram_tensor(f"in_{name}_dram", a.shape, _mybir.dt.from_np(a.dtype), kind="ExternalInput").ap()
    shape = arrays["in_L0_attn_a_x_dram"].shape
    out = nc.dram_tensor("out_0_dram", shape, _mybir.dt.float32, kind="ExternalOutput").ap()
    build(nc, aps, out)
    r = _run(nc, [arrays], core_ids=[0])
    return r.results[0]["out_0_dram"]
```

```python
from contextlib import ExitStack

import concourse.bass as bass
from concourse import mybir

F32, BF16, I32 = mybir.dt.float32, mybir.dt.bfloat16, mybir.dt.int32
ACT, ALU, AX = mybir.ActivationFunctionType, mybir.AluOpType, mybir.AxisListType
P = 128
EPS = 1e-5
BANK = 512
LOWEST = -3.0e38


def build(nc, d, out):
    B, N, C = d["L0_attn_a_x"].shape
    HD = d["L0_attn_a_Wout"].shape[0]
    E, _, H = d["L0_ffn_ew1"].shape
    NROT = d["L0_ffn_gens"].shape[0]
    HEADS = 8
    DH = HD // HEADS
    T = B * N
    NT = T // P
    BT = N // P
    KC = C // P
    HC = H // P
    GT = BANK // P
    NG = NT // GT
    SLOTS = 2 * T // P + E - 1
    REGION = T + P
    WORK = 7280
    ROUTE = 672
    QROW = 32

    ctx = ExitStack()
    with ctx:
        def sb(name, shape, dt=F32):
            return ctx.enter_context(nc.sbuf_tensor(name, shape, dt))

        taken = []

        def sem(name):
            taken.append(nc.alloc_semaphore(name))
            return taken[-1]

        def release(first):
            nc.clear_and_free_semaphores(taken[first:])
            del taken[first:]
            nc.all_engine_barrier()

        xs = sb("xs", [P, NT, C])
        xh = sb("xh", [P, NT, C])
        ab = sb("ab", [P, NT, C])
        ew1 = sb("ew1", [P, KC, E, H])
        ew2 = sb("ew2", [P, HC, E, C])
        abw = sb("abw", [P, KC, C])
        gw = sb("gw", [P, KC, E])
        gcw = sb("gcw", [P, 2, C])
        gcb = sb("gcb", [P, 1])
        gateb = sb("gateb", [1, E])
        eb1p = sb("eb1p", [2 * QROW + E, H], BF16)
        eb2p = sb("eb2p", [2 * QROW + E, C], BF16)
        abbp = sb("abbp", [2 * QROW + 1, C], BF16)
        vbp = sb("vbp", [2 * QROW + 1, C], BF16)
        sel = sb("sel", [2 * QROW + E, E, P], BF16)
        wa = sb("wa", [P, KC, C])
        wvo = sb("wvo", [P, KC, C])
        qbias = sb("qbias", [P, KC])
        ident = sb("ident", [P, P])
        identb = sb("identb", [P, P], BF16)
        causal = sb("causal", [P, P], BF16)
        tri = sb("tri", [P, P], BF16)
        onesb = sb("onesb", [P, P], BF16)
        onesf = sb("onesf", [1, P])
        mhalf = sb("mhalf", [P, 2 * GT])
        eidx = sb("eidx", [P, E])
        ebase = sb("ebase", [P, E])
        steps = sb("steps", [P, NT])
        sidx = sb("sidx", [P, SLOTS])
        zero = sb("zero", [P, C])
        ctxm = sb("ctxm", [HD + 1, B, C])
        wout = sb("wout", [HD, C])
        hmask = sb("hmask", [HD, HD])
        work = sb("work", [P, WORK])
        bank = ctx.enter_context(nc.psum_tensor("bank", [P, 8, BANK], F32))
        xg = nc.dram_tensor("slots_in", (E * REGION + P, C), F32).ap()
        yg = nc.dram_tensor("slots_out", (SLOTS * P, C), F32).ap()

        x_in = sem("x_in")

        class Arena:
            def __init__(self, flat):
                self.flat, self.at = flat, 0

            def take(self, *shape, dt=F32, rows=P):
                n = 1
                for s in shape:
                    n *= s
                w = n if dt in (F32, I32) else (n + 1) // 2
                v = self.flat[0:rows, self.at:self.at + w]
                self.at += w
                assert self.at <= self.flat.shape[1], self.at
                if dt != F32:
                    v = v.bitcast(dt)
                if len(shape) == 2:
                    v = v.rearrange("p (a b) -> p a b", a=shape[0])
                if len(shape) == 3:
                    v = v.rearrange("p (a b c) -> p a b c", a=shape[0], b=shape[1])
                return v

        def flat(t):
            return t[:].rearrange("p a b -> p (a b)")

        wqkv = flat(ab)[:, NT * C - KC * 3 * HD:].rearrange("p (c n) -> p c n", c=KC)

        def cols(view, bc):
            return view.unsqueeze(len(view.shape)).to_broadcast(list(view.shape) + [bc])

        def psum(b, n=1):
            return bank[:, b:b + n, :].rearrange("p a b -> p (a b)")

        def copy(eng, o, i, scale=1.0):
            return eng.activation(o, i, ACT.Copy, scale=scale)

        def weights():
            a = Arena(flat(xh))
            gens = a.take(NROT, KC, C)
            A = a.take(NROT, KC, C)
            AT = a.take(NROT, KC, C)
            X = a.take(NROT, KC, C)
            eye = a.take(KC, C)
            R = a.take(KC, C)
            w = work[:]
            a2 = Arena(w)
            a3 = Arena(flat(ab)[:, NT * C // 2:])
            w4 = [a3.take(KC, C) for _ in range(4)]
            woT = a2.take(KC, C)
            ew2T = [a2.take(KC, H) for _ in range(2)]
            bsel = a2.take(KC, E * E)
            gam, bet = a2.take(KC), a2.take(KC)
            bqc, bvc = a2.take(KC), a2.take(KC)
            eb2s = a2.take(C, rows=E)
            eb2T = a2.take(KC, E)
            eb1s = a2.take(H, rows=E)
            row = a.take(3, C, rows=1)
            grow = a2.take(E, rows=1)
            rem = a2.take(H, rows=E)
            rem2 = a2.take(C, rows=E)
            p2 = a2.take(H, rows=E, dt=BF16)
            gsum = a2.take(NROT * KC)
            gmx, gall = a2.take(1), a2.take(1)
            thr = a2.take(24)
            cmp = a2.take(24)
            sf, scf, scale = a2.take(1), a2.take(1), a2.take(1)
            sqi = a2.take(1, dt=I32)
            ki = a2.take(24, dt=I32)
            ei, bi = a2.take(E, dt=I32), a2.take(E, dt=I32)
            ti = a2.take(NT, dt=I32)
            ji = a2.take(SLOTS, dt=I32)

            w_small, w_ew, w_gens, w_proj = sem("w_small"), sem("w_ew"), sem("w_gens"), sem("w_proj")
            zero_ok, zeroed = sem("zero_ok"), sem("blank_tile")
            consts, iotas, order = sem("consts"), sem("iotas"), sem("pool_order")
            bsel_ok, beta_mm, row_ok = sem("bsel_ok"), sem("beta_mm"), sem("row_ok")
            dve = sem("dve_order")
            g_mx, g_all, A_ok, AT_ps, AT_ok = sem("g_mx"), sem("g_all"), sem("A_ok"), sem("AT_ps"), sem("AT_ok")
            horner_ps, X_ok, s_ok = sem("horner_ps"), sem("X_ok"), sem("s_ok")
            sq_T, ET_ok, sq_Y = sem("sq_T"), sem("ET_ok"), sem("sq_Y")
            rot_T, rot_TS, rot_Y, rot_ok = sem("rot_T"), sem("rot_TS"), sem("rot_Y"), sem("rot_ok")
            fold_T, fold_TS, fold_Y, fold_ok = sem("fold_T"), sem("fold_TS"), sem("fold_Y"), sem("fold_ok")
            eb2_T, eb2_TS, eb2_Y = sem("eb2_T"), sem("eb2_TS"), sem("eb2_Y")
            at_ps, at_ok, vb_ok = sem("at_ps"), sem("at_ok"), sem("vb_ok")
            HORNER = 10

            with nc.Block() as block:
                @block.sync
                def _(sp):
                    one = lambda k: d[k].rearrange("(o n) -> o n", o=1)
                    colv = lambda k: d[k].rearrange("(c p) -> p c", p=P)
                    chunked = lambda k: d[k].rearrange("(c p) n -> p c n", p=P)
                    small = [
                        (gam, colv("L0_ffn_ln_gamma")), (bet, colv("L0_ffn_ln_beta")),
                        (bqc, colv("L0_attn_b_bq")), (bvc, colv("L0_attn_b_bv")),
                        (abw[:], chunked("L0_ffn_abel_w")), (gw[:], chunked("L0_ffn_moe_gate_w")),
                        (eb1s, d["L0_ffn_eb1"]), (eb2s, d["L0_ffn_eb2"]),
                        (row[:, 0, :], one("L0_ffn_abel_b")), (row[:, 1, :], one("L0_attn_b_bo")),
                        (grow, one("L0_ffn_moe_gate_b")),
                    ]
                    assert len(small) == 11
                    for o, i in small:
                        sp.dma_start(o, i, allow_slow_non_contiguous=True).then_inc(w_small, 16)
                    for h in range(2):
                        sp.dma_start(gcw[:, h, :], d["L0_ffn_gc_w"][(1 - h) * C:(2 - h) * C, :].rearrange("n o -> (o n)")
                                     .partition_broadcast(P)).then_inc(w_small, 16)
                    sp.dma_start(gcb[:], d["L0_ffn_gc_b"].partition_broadcast(P)).then_inc(w_small, 16)
                    for c in range(KC):
                        sp.dma_start(ew1[:, c, :, :], d["L0_ffn_ew1"][:, c * P:(c + 1) * P, :].rearrange("e p h -> p e h")
                                     ).then_inc(w_ew, 16)
                    for c in range(HC):
                        sp.dma_start(ew2[:, c, :, :], d["L0_ffn_ew2"][:, c * P:(c + 1) * P, :].rearrange("e p h -> p e h")
                                     ).then_inc(w_ew, 16)
                    sp.wait_ge(zero_ok, 1)
                    sp.dma_start(xg[E * REGION:E * REGION + P, :], zero[:]).then_inc(zeroed, 16)
                    sp.wait_ge(zeroed, 16)

                @block.gpsimd
                def _(pool):
                    n = 0

                    def then(ins):
                        nonlocal n
                        n += 1
                        ins.then_inc(order, 1)
                        pool.wait_ge(order, n)

                    def select(t, pattern, base, cm, op, fill):
                        return pool.affine_select(out=t, in_=t, compare_op=op, fill=fill, base=base, pattern=pattern,
                                                  channel_multiplier=cm)

                    then(pool.memset(ident[:], 0.0))
                    select(ident[:], [[-1, P]], 0, 1, ALU.not_equal, 1.0).then_inc(consts, 1)
                    then(pool.memset(eye, 0.0))
                    select(eye, [[P, KC], [-1, C]], 0, 1, ALU.not_equal, 1.0).then_inc(consts, 1)
                    then(pool.memset(identb[:], 0.0))
                    select(identb[:], [[-1, P]], 0, 1, ALU.not_equal, 1.0).then_inc(consts, 1)
                    pool.memset(zero[:], 0.0).then_inc(zero_ok, 1)
                    then(pool.memset(tri[:], 1.0))
                    select(tri[:], [[1, P]], 0, -1, ALU.is_gt, 0.0).then_inc(consts, 1)
                    then(pool.memset(causal[:], 0.0))
                    select(causal[:], [[-1, P]], 0, 1, ALU.is_ge, LOWEST).then_inc(consts, 1)
                    then(pool.memset(sel[:], 0.0))
                    for q in range(3):
                        then(select(sel[:], [[-1, E], [0, P]], -QROW * q, 1, ALU.not_equal, 1.0))
                    hm = hmask[:].rearrange("p (h e) -> p h e", h=HEADS)
                    then(pool.memset(hmask[:], 1.0))
                    then(select(hm, [[-DH, HEADS], [0, DH]], 0, 1, ALU.is_ge, 0.0))
                    then(select(hm, [[DH, HEADS], [0, DH]], DH - 1, -1, ALU.is_ge, 0.0))
                    pool.memset(onesb[:], 1.0).then_inc(consts, 1)
                    pool.memset(onesf[:], 1.0).then_inc(consts, 1)
                    pool.memset(mhalf[:], -0.5).then_inc(consts, 1)
                    for t in (eb1p, eb2p, abbp, vbp):
                        pool.memset(t[:], 0.0).then_inc(consts, 1)
                    pool.iota(ki, pattern=[[1, 24]], base=127, channel_multiplier=0).then_inc(iotas, 1)
                    pool.iota(ei, pattern=[[1, E]], base=-E, channel_multiplier=0).then_inc(iotas, 1)
                    pool.iota(bi, pattern=[[REGION, E]], base=0, channel_multiplier=0).then_inc(iotas, 1)
                    pool.iota(ti, pattern=[[P, NT]], base=0, channel_multiplier=0).then_inc(iotas, 1)
                    pool.iota(ji, pattern=[[1, SLOTS]], base=0, channel_multiplier=0).then_inc(iotas, 1)
                    pool.wait_ge(g_mx, 1)
                    pool.partition_all_reduce(gall, gmx, P, bass.bass_isa.ReduceOp.max).then_inc(g_all, 1)

                @block.vector
                def _(v):
                    n = 0

                    def then(ins):
                        nonlocal n
                        n += 1
                        ins.then_inc(dve, 1)
                        v.wait_ge(dve, n)

                    def parts(o, src, width, rows):
                        r, q = rem[0:rows, 0:width], p2[0:rows, 0:width]
                        then(v.tensor_copy(o[0:rows, :], src))
                        then(v.tensor_tensor(r, src, o[0:rows, :], ALU.subtract))
                        then(v.tensor_copy(q, r))
                        then(v.tensor_copy(o[QROW:QROW + rows, :], q))
                        then(v.tensor_tensor(r, r, q, ALU.subtract))
                        then(v.tensor_copy(o[2 * QROW:2 * QROW + rows, :], r))

                    then(v.memset(bsel, 0.0))
                    v.wait_ge(w_small, 16 * 14)
                    for c in range(KC):
                        last = v.tensor_copy(bsel[:, c, 0:E * E:E + 1], bet[:, c:c + 1].to_broadcast([P, E]))
                    last.then_inc(bsel_ok, 1)
                    then(v.tensor_tensor(gcw[:, 1, :], gcw[:, 1, :], gcw[:, 0, :], ALU.add))
                    v.wait_ge(iotas, 5)
                    then(v.tensor_scalar(thr.bitcast(I32), ki, 23, None, ALU.logical_shift_left))
                    v.tensor_copy(eidx[:], ei)
                    v.tensor_copy(ebase[:], bi)
                    v.tensor_copy(steps[:], ti)
                    then(v.tensor_copy(sidx[:], ji))
                    v.wait_ge(w_gens, 16)
                    then(v.tensor_reduce(gsum, gens.rearrange("p m c j -> p (m c) j"), AX.X, ALU.add,
                                         apply_absolute_value=True))
                    v.tensor_reduce(gmx, gsum, AX.X, ALU.max).then_inc(g_mx, 1)
                    v.wait_ge(g_all, 1)
                    then(v.tensor_scalar(cmp, thr, gall, None, ALU.is_lt))
                    then(v.tensor_reduce(sf, cmp, AX.X, ALU.add))
                    then(v.tensor_scalar(sf, sf, 1.0, None, ALU.max))
                    v.tensor_copy(sqi, sf).then_inc(s_ok, 1)
                    then(v.tensor_scalar(scf, sf, -1.0, 127.0, ALU.mult, ALU.add))
                    then(v.tensor_copy(scale.bitcast(I32), scf))
                    then(v.tensor_scalar(scale.bitcast(I32), scale.bitcast(I32), 23, None, ALU.logical_shift_left))
                    for m in range(NROT):
                        v.tensor_scalar(A[:, m], gens[:, m], scale, None, ALU.mult).then_inc(A_ok, 1)
                    v.wait_ge(A_ok, NROT)
                    v.wait_ge(consts, 2)
                    for m in range(NROT):
                        v.scalar_tensor_tensor(X[:, m], A[:, m], 1.0 / HORNER, eye, ALU.mult, ALU.add).then_inc(X_ok, 1)
                    for s, k in enumerate(range(HORNER - 1, 0, -1)):
                        for m in range(NROT):
                            v.wait_ge(horner_ps, NROT * s + m + 1)
                            v.scalar_tensor_tensor(X[:, m], bank[:, m, :].rearrange("p (c j) -> p c j", c=KC), 1.0 / k, eye,
                                                   ALU.mult, ALU.add).then_inc(X_ok, 1)
                    v.wait_ge(s_ok, 1)
                    s = v.value_load(sqi[0:1, 0:1], min_val=1, max_val=24)
                    with v.Fori(0, s) as i:
                        for m in range(NROT):
                            v.wait_ge(sq_Y, i * NROT + (m + 1))
                            v.tensor_copy(X[:, m], bank[:, NROT + m, :].rearrange("p (c j) -> p c j", c=KC)).then_inc(X_ok, 1)
                    v.wait_ge(rot_Y, 1)
                    v.tensor_copy(X[:, 0], bank[:, 6, :].rearrange("p (c j) -> p c j", c=KC)).then_inc(rot_ok, 1)
                    v.wait_ge(rot_Y, 2)
                    v.tensor_copy(R, bank[:, 7, :].rearrange("p (c j) -> p c j", c=KC)).then_inc(rot_ok, 1)
                    v.wait_ge(consts, 12)
                    v.wait_ge(beta_mm, 1)
                    then(v.tensor_tensor(eb1s, eb1s, bank[0:E, 3, :], ALU.add))
                    then(v.tensor_tensor(row[:, 0, :], row[:, 0, :], bank[0:1, 4, 0:C], ALU.add))
                    then(v.tensor_tensor(gateb[:], grow, bank[0:1, 4, C:C + E], ALU.add))
                    parts(eb1p, eb1s, H, E)
                    parts(abbp, row[:, 0, :], C, 1)
                    for c in range(KC):
                        v.tensor_scalar(ew1[:, c], ew1[:, c], gam[:, c:c + 1], None, ALU.mult)
                        v.tensor_scalar(abw[:, c], abw[:, c], gam[:, c:c + 1], None, ALU.mult)
                        v.tensor_scalar(gw[:, c], gw[:, c], gam[:, c:c + 1], None, ALU.mult)
                    v.wait_ge(at_ps, 4)
                    then(v.tensor_tensor(row[:, 2, :], row[:, 1, :], bank[0:1, 5, 0:C], ALU.add))
                    parts(vbp, row[:, 2, :], C, 1)
                    v.tensor_scalar(qbias[:], bank[:, 6, 0:KC], C ** -0.5, None, ALU.mult).then_inc(vb_ok, 1)
                    v.wait_ge(eb2_Y, 1)
                    then(v.tensor_copy(rem2[0:E, :], bank[0:E, 2, 0:C]))
                    parts(eb2p, rem2[0:E, :], C, E)
                    for e in range(E):
                        v.wait_ge(fold_Y, e + 1)
                        v.tensor_copy(ew2[:, :, e, :], psum(6, 2).rearrange("p (h c) -> p h c", h=HC)).then_inc(fold_ok, 1)

                @block.scalar
                def _(act):
                    act.dma_start(gens, d["L0_ffn_gens"].rearrange("m (c p) j -> p m c j", p=P)).then_inc(w_gens, 16)
                    for o, k in zip(w4, "qkvo"):
                        act.dma_start(o, d[f"L0_attn_b_W{k}"].rearrange("(c p) n -> p c n", p=P)).then_inc(w_proj, 16)
                    for q in range(4):
                        ts = slice(q * NT // 4, (q + 1) * NT // 4)
                        act.dma_start(xs[:, ts, :], d["L0_attn_a_x"].rearrange("b (n p) c -> p (b n) c", p=P)[:, ts, :]
                                      ).then_inc(x_in, 16)
                    act.dma_start(wqkv, d["L0_attn_a_Wqkv"].rearrange("(c p) n -> p c n", p=P)).then_inc(x_in, 16)
                    act.dma_start(wout[:], d["L0_attn_a_Wout"]).then_inc(x_in, 16)
                    for b in range(B):
                        act.dma_start(ctxm[HD:HD + 1, b, :], d["L0_attn_a_bout"].rearrange("(o n) -> o n", o=1)).then_inc(x_in, 16)
                    for m in range(NROT):
                        act.wait_ge(AT_ps, m + 1)
                        copy(act, AT[:, m], bank[:, m, :].rearrange("p (c j) -> p c j", c=KC)).then_inc(AT_ok, 1)
                    act.wait_ge(s_ok, 1)
                    s = act.value_load(sqi[0:1, 0:1], min_val=1, max_val=24)
                    with act.Fori(0, s) as i:
                        for m in range(NROT):
                            act.wait_ge(sq_T, i * NROT + (m + 1))
                            copy(act, AT[:, m], bank[:, m, :].rearrange("p (c j) -> p c j", c=KC)).then_inc(ET_ok, 1)
                    for q in range(2):
                        act.wait_ge(rot_T, q + 1)
                        copy(act, AT[:, 0], bank[:, 0, :].rearrange("p (c j) -> p c j", c=KC)).then_inc(rot_TS, 1)
                    act.wait_ge(at_ps, 1)
                    copy(act, wa[:], bank[:, 0, :].rearrange("p (c j) -> p c j", c=KC), C ** -0.5).then_inc(at_ok, 1)
                    act.wait_ge(at_ps, 2)
                    copy(act, woT, bank[:, 1, :].rearrange("p (c j) -> p c j", c=KC)).then_inc(at_ok, 1)
                    act.wait_ge(at_ps, 3)
                    copy(act, wvo[:], bank[:, 2, :].rearrange("p (c j) -> p c j", c=KC)).then_inc(at_ok, 1)
                    act.wait_ge(eb2_T, 1)
                    copy(act, eb2T, bank[:, 0, 0:KC * E].rearrange("p (c e) -> p c e", c=KC)).then_inc(eb2_TS, 1)
                    for e in range(E):
                        act.wait_ge(fold_T, e + 1)
                        if e >= 2:
                            act.wait_ge(fold_Y, e - 1)
                        copy(act, ew2T[e % 2], psum(4, 2).rearrange("p (c h) -> p c h", c=KC)).then_inc(fold_TS, 1)

                @block.tensor
                def _(pe):
                    def transposed(b, src, m):
                        for kc in range(KC):
                            for ic in range(KC):
                                last = pe.transpose(bank[:, b, kc * C + ic * P:kc * C + (ic + 1) * P],
                                                    src[:, ic, kc * P:(kc + 1) * P], ident[:])
                        return last

                    def product(b, leftT, right):
                        for rc in range(KC):
                            for kc in range(KC):
                                last = pe.matmul(bank[:, b, rc * C:(rc + 1) * C], leftT[:, kc, rc * P:(rc + 1) * P],
                                                 right[:, kc, :], start=(kc == 0), stop=(kc == KC - 1))
                        return last

                    pe.wait_ge(consts, 1)
                    for m in range(NROT):
                        pe.wait_ge(A_ok, m + 1)
                        transposed(m, A[:, m], m).then_inc(AT_ps, 1)
                    for s in range(HORNER - 1):
                        for m in range(NROT):
                            if s == 0:
                                pe.wait_ge(AT_ok, m + 1)
                            pe.wait_ge(X_ok, NROT * s + m + 1)
                            product(m, AT[:, m], X[:, m]).then_inc(horner_ps, 1)
                    pe.wait_ge(s_ok, 1)
                    done = NROT * (HORNER - 1)
                    s = pe.value_load(sqi[0:1, 0:1], min_val=1, max_val=24)
                    with pe.Fori(0, s) as i:
                        for m in range(NROT):
                            pe.wait_ge(X_ok, i * NROT + (done + m + 1))
                            transposed(m, X[:, m], m).then_inc(sq_T, 1)
                        for m in range(NROT):
                            pe.wait_ge(ET_ok, i * NROT + (m + 1))
                            product(NROT + m, AT[:, m], X[:, m]).then_inc(sq_Y, 1)
                    pe.wait_ge(X_ok, s * NROT + (done + NROT))
                    transposed(0, X[:, 0], 0).then_inc(rot_T, 1)
                    pe.wait_ge(rot_TS, 1)
                    product(6, AT[:, 0], X[:, 1]).then_inc(rot_Y, 1)
                    pe.wait_ge(rot_ok, 1)
                    transposed(0, X[:, 0], 0).then_inc(rot_T, 1)
                    pe.wait_ge(rot_TS, 2)
                    product(7, AT[:, 0], X[:, 2]).then_inc(rot_Y, 1)
                    pe.wait_ge(w_small, 16 * 14)
                    pe.wait_ge(w_ew, 16 * (KC + HC))
                    pe.wait_ge(bsel_ok, 1)
                    for e in range(E):
                        for c in range(KC):
                            pe.matmul(bank[0:E, 3, :], bsel[:, c, e * E:(e + 1) * E], ew1[:, c, e, :],
                                      start=(e == 0 and c == 0), stop=(e == E - 1 and c == KC - 1))
                    for c in range(KC):
                        pe.matmul(bank[0:1, 4, 0:C], bet[:, c:c + 1], abw[:, c, :], start=(c == 0), stop=(c == KC - 1))
                    for c in range(KC):
                        last = pe.matmul(bank[0:1, 4, C:C + E], bet[:, c:c + 1], gw[:, c, :],
                                         start=False, stop=(c == KC - 1), skip_group_check=True)
                    last.then_inc(beta_mm, 1)
                    pe.wait_ge(w_proj, 16 * 4)
                    wq, wk, wv, wo = w4
                    product(0, wq, wk).then_inc(at_ps, 1)
                    transposed(1, wo, 0).then_inc(at_ps, 1)
                    pe.wait_ge(at_ok, 2)
                    product(2, wv, woT).then_inc(at_ps, 1)
                    for c in range(KC):
                        pe.matmul(bank[0:1, 5, 0:C], bvc[:, c:c + 1], woT[:, c, :], start=(c == 0), stop=(c == KC - 1))
                    for j in range(KC):
                        for c in range(KC):
                            last = pe.matmul(bank[:, 6, j:j + 1], wk[:, c, j * P:(j + 1) * P], bqc[:, c:c + 1],
                                             start=(j == 0 and c == 0), stop=(c == KC - 1), skip_group_check=True)
                    last.then_inc(at_ps, 1)
                    pe.wait_ge(rot_ok, 2)
                    pe.wait_ge(at_ok, 3)
                    for c in range(KC):
                        last = pe.transpose(bank[:, 0, c * E:(c + 1) * E], eb2s[:, c * P:(c + 1) * P], ident[0:E, 0:E])
                    last.then_inc(eb2_T, 1)
                    pe.wait_ge(eb2_TS, 1)
                    for c in range(KC):
                        last = pe.matmul(bank[0:E, 2, 0:C], eb2T[:, c, :], R[:, c, :], start=(c == 0), stop=(c == KC - 1))
                    last.then_inc(eb2_Y, 1)
                    pe.wait_ge(vb_ok, 1)
                    for e in range(E + 1):
                        if e < E:
                            pe.wait_ge(fold_TS, e)
                            for c in range(KC):
                                for h in range(HC):
                                    last = pe.transpose(bank[:, 4 + c, h * P:(h + 1) * P], ew2[:, h, e, c * P:(c + 1) * P], ident[:])
                            last.then_inc(fold_T, 1)
                        if e >= 1:
                            pe.wait_ge(fold_TS, e)
                            if e >= 2:
                                pe.wait_ge(fold_ok, e - 1)
                            y = psum(6, 2).rearrange("p (h c) -> p h c", h=HC)
                            for h in range(HC):
                                for c in range(KC):
                                    last = pe.matmul(y[:, h, :], ew2T[(e - 1) % 2][:, c, h * P:(h + 1) * P], R[:, c, :],
                                                     start=(c == 0), stop=(c == KC - 1))
                            last.then_inc(fold_Y, 1)


        def after(eng, semaphore, value):
            if not isinstance(value, int) or value >= 1:
                eng.wait_ge(semaphore, value)

        class Norm:
            def __init__(self, name, arena):
                self.st = [arena.take(GT, 6) for _ in range(2)]
                self.sum = [arena.take(GT) for _ in range(2)]
                self.dif, self.m2, self.var = arena.take(GT), arena.take(GT), arena.take(GT)
                self.arg = [arena.take(2, GT) for _ in range(2)]
                self.root = [arena.take(2, GT) for _ in range(2)]
                self.stats_ok, self.sums_ok = sem(name + "_stats"), sem(name + "_sums")
                self.var_ok, self.arg_ok, self.root_ok = sem(name + "_var"), sem(name + "_arg"), sem(name + "_root")

            def statistics(self, v, n, tiles):
                u = n % 2
                st, dif, m2, var = self.st[u], self.dif, self.m2, self.var
                for t in range(GT):
                    v.bn_stats(st[:, t, :], tiles[:, t, :]).then_inc(self.stats_ok, 1)
                v.wait_ge(self.stats_ok, GT * (n + 1))
                v.tensor_tensor(self.sum[u], st[:, :, 1], st[:, :, 4], ALU.add).then_inc(self.sums_ok, 1)
                v.tensor_tensor(dif, st[:, :, 1], st[:, :, 4], ALU.subtract).then_inc(self.sums_ok, 1)
                v.tensor_tensor(m2, st[:, :, 2], st[:, :, 5], ALU.add).then_inc(self.sums_ok, 1)
                v.wait_ge(self.sums_ok, 3 * (n + 1))
                v.scalar_tensor_tensor(dif, dif, 0.25, dif, ALU.mult, ALU.mult).then_inc(self.var_ok, 1)
                v.wait_ge(self.var_ok, 2 * n + 1)
                v.scalar_tensor_tensor(var, m2, 1.0 / C, dif, ALU.mult, ALU.add).then_inc(self.var_ok, 1)
                v.wait_ge(self.var_ok, 2 * n + 2)
                v.tensor_scalar(self.arg[u][:, 0, :], var, EPS, None, ALU.add).then_inc(self.arg_ok, 1)
                v.tensor_scalar(self.arg[u][:, 1, :], var, 1.0 + EPS, EPS * EPS, ALU.mult, ALU.add).then_inc(self.arg_ok, 1)

            def roots(self, pool, n):
                u = n % 2
                pool.wait_ge(self.arg_ok, 2 * (n + 1))
                pool.tensor_tensor(self.root[u].rearrange("p a t -> p (a t)"), self.arg[u].rearrange("p a t -> p (a t)"),
                                   mhalf[:], ALU.pow).then_inc(self.root_ok, 1)

        qT = work[0:HD + 1, 0:T]
        route = Arena(work[:, WORK - ROUTE:WORK])
        zab = route.take(NT)
        oh = route.take(2 * NT, E, dt=BF16).rearrange("p (k t) e -> p k t e", k=2)
        dtop, wts = route.take(NT), route.take(2, NT)
        slot = route.take(2, NT, dt=I32)
        texp, trow = route.take(SLOTS, dt=I32), route.take(SLOTS, dt=I32)
        posf = route.take(2, NT)
        tails = route.take(E, dt=I32)

        def context():
            a = Arena(flat(ab))
            ln = [a.take(GT, C) for _ in range(2)]
            lnT = [a.take(KC, BANK) for _ in range(2)]
            vs = [a.take(GT, HD) for _ in range(2)]
            ks = [a.take(GT * HEADS, DH) for _ in range(2)]
            kmax, ksum = a.take(GT * HEADS), a.take(GT * HEADS)
            nb = [a.take(GT) for _ in range(2)]
            cm = [a.take(HD, rows=HD) for _ in range(B)]
            nrm = Norm("a", a)
            nb_ok, ln_ok, lnT_ps, lnT_ok = sem("a_nb"), sem("a_ln"), sem("a_lnT_ps"), sem("a_lnT")
            kvq_ps, vq_ok, kmax_ok, ksh_ok = sem("a_kvq_ps"), sem("a_vq"), sem("a_kmax"), sem("a_kshift")
            kexp_ok, ksum_ok, k_ok, ctx_ps = sem("a_kexp"), sem("a_ksum"), sem("a_k"), sem("a_ctx_ps")
            cm_ok, m_ps, ones_ok, m_ok = sem("a_cm"), sem("a_m_ps"), sem("a_ones"), sem("a_m")
            GB = NG // B

            with nc.Block() as block:
                @block.gpsimd
                def _(pool):
                    pool.memset(work[HD:HD + 1, 0:T], 1.0).then_inc(ones_ok, 1)
                    pool.wait_ge(ones_ok, 1)
                    for g in range(NG):
                        nrm.roots(pool, g)

                @block.vector
                def _(v):
                    v.wait_ge(x_in, 16 * 8)
                    for g in range(NG + 1):
                        if g < NG:
                            u = g % 2
                            nrm.statistics(v, g, xs[:, g * GT:(g + 1) * GT, :])
                            v.wait_ge(nrm.root_ok, g + 1)
                            v.scalar_tensor_tensor(nb[u], nrm.sum[u], -0.5, nrm.root[u][:, 0, :], ALU.mult, ALU.mult
                                                   ).then_inc(nb_ok, 1)
                            v.wait_ge(nb_ok, g + 1)
                            after(v, lnT_ps, g - 1)
                            for t in range(GT):
                                v.tensor_scalar(ln[u][:, t, :], xs[:, g * GT + t, :], nrm.root[u][:, 0, t:t + 1],
                                                nb[u][:, t:t + 1], ALU.mult, ALU.add).then_inc(ln_ok, 1)
                        if g >= 1:
                            h, u = g - 1, (g - 1) % 2
                            kps = bank[:, 4, :].rearrange("p (t x) -> p t x", t=GT)[:, :, 0:HD].rearrange(
                                "p t (h e) -> p t h e", h=HEADS)
                            k4 = ks[u].rearrange("p (t h) e -> p t h e", t=GT)
                            v.wait_ge(kvq_ps, h + 1)
                            v.tensor_reduce(kmax.rearrange("p (t h) -> p t h", t=GT), kps, AX.X, ALU.max).then_inc(kmax_ok, 1)
                            v.wait_ge(kmax_ok, h + 1)
                            after(v, ctx_ps, h - 1)
                            v.tensor_tensor(k4, kps, cols(kmax.rearrange("p (t h) -> p t h", t=GT), DH), ALU.subtract
                                            ).then_inc(ksh_ok, 1)
                            v.wait_ge(kexp_ok, h + 1)
                            v.tensor_reduce(ksum, ks[u], AX.X, ALU.add).then_inc(ksum_ok, 1)
                            v.wait_ge(ksum_ok, 2 * h + 1)
                            v.reciprocal(ksum, ksum).then_inc(ksum_ok, 1)
                            v.wait_ge(ksum_ok, 2 * h + 2)
                            v.tensor_tensor(ks[u], ks[u], cols(ksum, DH), ALU.mult).then_inc(k_ok, 1)
                    for b in range(B):
                        v.wait_ge(ctx_ps, GB * (b + 1))
                        v.tensor_tensor(cm[b], bank[0:HD, 6 + b, 0:HD], hmask[:], ALU.mult).then_inc(cm_ok, 1)

                @block.scalar
                def _(act):
                    for g in range(NG + 1):
                        if g < NG:
                            u = g % 2
                            act.wait_ge(lnT_ps, g + 1)
                            after(act, kvq_ps, g - 1)
                            copy(act, lnT[u].rearrange("p c n -> p (c n)"), psum(2 * u, 2)).then_inc(lnT_ok, 1)
                        if g >= 1:
                            h, u = g - 1, (g - 1) % 2
                            act.wait_ge(kvq_ps, h + 1)
                            after(act, ctx_ps, h - 1)
                            copy(act, qT[0:HD, h * BANK:(h + 1) * BANK], bank[0:HD, 5, :]).then_inc(vq_ok, 1)
                            act.wait_ge(ksh_ok, h + 1)
                            copy(act, vs[u], bank[:, 4, :].rearrange("p (t x) -> p t x", t=GT)[:, :, HD:2 * HD]).then_inc(vq_ok, 1)
                            act.activation(ks[u], ks[u], ACT.Exp).then_inc(kexp_ok, 1)
                    for b in range(B):
                        act.wait_ge(m_ps, b + 1)
                        copy(act, ctxm[0:HD, b, :], bank[0:HD, 2 * b, 0:C], HD ** -0.5).then_inc(m_ok, 1)

                @block.tensor
                def _(pe):
                    for g in range(NG + 2):
                        if g < NG:
                            u = g % 2
                            pe.wait_ge(ln_ok, GT * (g + 1))
                            after(pe, lnT_ok, g - 1)
                            for c in range(KC):
                                for t in range(GT):
                                    last = pe.transpose(bank[:, 2 * u + c, t * P:(t + 1) * P], ln[u][:, t, c * P:(c + 1) * P],
                                                        ident[:])
                            last.then_inc(lnT_ps, 1)
                        if 1 <= g <= NG:
                            h, u = g - 1, (g - 1) % 2
                            pe.wait_ge(lnT_ok, h + 1)
                            after(pe, ksh_ok, h)
                            after(pe, vq_ok, 2 * h)
                            for t in range(GT):
                                for c in range(KC):
                                    pe.matmul(bank[:, 4, t * 2 * HD:(t + 1) * 2 * HD], lnT[u][:, c, t * P:(t + 1) * P],
                                              wqkv[:, c, HD:3 * HD], start=(c == 0), stop=(c == KC - 1))
                            for c in range(KC):
                                last = pe.matmul(bank[0:HD, 5, :], wqkv[:, c, 0:HD], lnT[u][:, c, :],
                                                 start=(c == 0), stop=(c == KC - 1))
                            last.then_inc(kvq_ps, 1)
                        if g >= 2:
                            h, u = g - 2, (g - 2) % 2
                            b = h // GB
                            pe.wait_ge(k_ok, h + 1)
                            pe.wait_ge(vq_ok, 2 * (h + 1))
                            for t in range(GT):
                                last = pe.matmul(bank[0:HD, 6 + b, 0:HD], vs[u][:, t, :],
                                                 ks[u].rearrange("p (t h) e -> p t (h e)", t=GT)[:, t, :],
                                                 start=(h % GB == 0 and t == 0), stop=(h % GB == GB - 1 and t == GT - 1))
                            last.then_inc(ctx_ps, 1)
                    for b in range(B):
                        pe.wait_ge(cm_ok, b + 1)
                        pe.matmul(bank[0:HD, 2 * b, 0:C], cm[b], wout[:], start=True, stop=True).then_inc(m_ps, 1)

        def mixture(r):
            a = Arena(work[:, T:WORK - ROUTE])
            xT = [a.take(KC, BANK) for _ in range(2)]
            nrm = Norm(f"f{r}", a)
            nb = [a.take(2, GT) for _ in range(2)]
            c1 = [a.take(GT) for _ in range(2)]
            junk = a.take(C, dt=BF16)
            m1, m2, i1 = a.take(GT), a.take(GT), a.take(GT)
            mine, l2 = a.take(2, GT, E), a.take(GT, E)
            eq, cand = mine[:, 0], mine[:, 1]
            cnt = [a.take(GT, E, dt=BF16) for _ in range(2)]
            csum = a.take(E)
            run = [a.take(E, dt=BF16) for _ in range(2)]
            pos = a.take(GT, E)
            z = [a.take(GT) for _ in range(2)]
            rt = Arena(work[:, 0:T])
            ones, total = rt.take(NT), rt.take(E)
            ntile, tincl, texcl, shift = rt.take(E), rt.take(E), rt.take(E), rt.take(E)
            cmpn, cmpt, weight = rt.take(E, NT), rt.take(SLOTS, E - 1), rt.take(SLOTS, E - 1)
            tf, row, used, place = rt.take(SLOTS), rt.take(SLOTS), rt.take(SLOTS), rt.take(2 * NT, E)
            moved = rt.take(2 * NT)
            RING = 4
            x = Arena(flat(xh))
            xr = [x.take(C) for _ in range(RING)]
            xrT = [x.take(KC, P) for _ in range(2)]
            hid = [x.take(H) for _ in range(2)]
            hidT = [x.take(HC, P) for _ in range(2)]
            yr = [x.take(C) for _ in range(RING)]
            cb = Arena(work[:, 0:T])
            g1 = [cb.take(C) for _ in range(RING)]
            g2 = [cb.take(C) for _ in range(RING)]
            dif = [cb.take(C) for _ in range(2 * GT)]
            s = lambda name: sem(f"m{r}_" + name)
            att_ps, x1_ok, nb_ok, xh_ok, res_ok = s("att_ps"), s("x1"), s("nb"), s("xh"), s("res")
            xT_ps, xT_ok, lg_ps, ab_ps, gelu_ok = s("xT_ps"), s("xT"), s("logits_ps"), s("dense_ps"), s("gelu")
            dve, cnt_ok, rank_ps, pos_ok, slot_ok, zab_ok = (s("order"), s("cnt"), s("rank_ps"), s("pos"), s("slot"), s("zab"))
            run_ok, d_ok, ed_ok, wts_ok, tot_ps, sum_ok = s("run"), s("d"), s("ed"), s("wts"), s("tot_ps"), s("sum")
            tails_ok, padded, texp_ok, index_ok, scat = s("tails"), s("padded"), s("texp"), s("index"), s("scattered")
            x_ld = [s(f"x_loaded{k}") for k in range(RING)]
            y_st = [s(f"y_stored{k}") for k in range(RING)]
            xrT_ps, xrT_ok, up_ps, hid_ok = s("xrT_ps"), s("xrT"), s("up_ps"), s("hid")
            hidT_ps, hidT_ok, dn_ps, y_ok = s("hidT_ps"), s("hidT"), s("down_ps"), s("y")
            g_ld = [s(f"gathered{k}") for k in range(RING)]
            dif_ok, z_ok, ez_ok, gate_ok, x2_ok, o_st = s("dif"), s("z"), s("ez"), s("gate"), s("x2"), s("stored")
            ZN = GT + 2
            FIRST = 2 * RING - 1
            TURNS = (SLOTS - 1 - FIRST) // RING
            TAIL = FIRST + TURNS * RING
            tiles = lambda g: slice(g * GT, (g + 1) * GT)

            def over_tiles(eng, step):
                for j in range(FIRST):
                    step(j, j % RING, j // RING)
                with eng.Fori(0, TURNS) as i:
                    for k in range(RING):
                        step(i * RING + (FIRST + k), (FIRST + k) % RING, i + (FIRST + k) // RING)
                for j in range(TAIL, SLOTS):
                    step(j, j % RING, j // RING)

            def is_last(j):
                return isinstance(j, int) and j == SLOTS - 1

            with nc.Block() as block:
                @block.vector
                def _(v):
                    n = 0

                    def then(ins):
                        nonlocal n
                        n += 1
                        ins.then_inc(dve, 1)
                        v.wait_ge(dve, n)

                    def statistics(g):
                        if r == 0:
                            v.wait_ge(att_ps, g + 1)
                            for h in range(2):
                                x2 = xs[:, g * GT + 2 * h:g * GT + 2 * h + 2, :].rearrange("p t c -> p (t c)")
                                v.tensor_tensor(x2, x2, bank[:, h, :], ALU.add).then_inc(x1_ok, 1)
                            v.wait_ge(x1_ok, 2 * (g + 1))
                        nrm.statistics(v, g, xs[:, tiles(g), :])

                    def normalise(g):
                        u = g % 2
                        v.wait_ge(nrm.root_ok, g + 1)
                        after(v, res_ok, GT * (g - 1))
                        for k in range(2):
                            v.scalar_tensor_tensor(nb[u][:, k, :], nrm.sum[u], -0.5, nrm.root[u][:, k, :], ALU.mult, ALU.mult
                                                   ).then_inc(nb_ok, 1)
                        v.tensor_scalar(c1[u], nrm.root[u][:, 0, :], 1.0, None, ALU.add).then_inc(nb_ok, 1)
                        v.wait_ge(nb_ok, 3 * (g + 1))
                        for t in range(GT):
                            v.tensor_scalar(xh[:, g * GT + t, :], xs[:, g * GT + t, :], nrm.root[u][:, 1, t:t + 1],
                                            nb[u][:, 1, t:t + 1], ALU.mult, ALU.add).then_inc(xh_ok, 1)

                    eb = eidx[:].unsqueeze(1).to_broadcast([P, GT, E])

                    def best(src, m, onehot):
                        then(v.tensor_reduce(m, src, AX.X, ALU.max))
                        then(v.tensor_tensor(eq, src, cols(m, E), ALU.is_ge))
                        then(v.tensor_tensor(cand, eq, eb, ALU.mult))
                        then(v.tensor_reduce(i1, cand, AX.X, ALU.min))
                        then(v.tensor_tensor(onehot, eb, cols(i1, E), ALU.is_equal))

                    def choose(g):
                        logits = bank[:, 6, 0:GT * E].rearrange("p (t e) -> p t e", t=GT)
                        oh1, oh2 = oh[:, 0, tiles(g), :], oh[:, 1, tiles(g), :]
                        v.wait_ge(lg_ps, g + 1)
                        best(logits, m1, oh1)
                        then(v.scalar_tensor_tensor(l2, oh1, LOWEST, logits, ALU.mult, ALU.add))
                        best(l2, m2, oh2)
                        v.tensor_tensor(cnt[g % 2], oh1, oh2, ALU.add).then_inc(cnt_ok, 1)
                        v.tensor_tensor(dtop[:, tiles(g)], m2, m1, ALU.subtract).then_inc(d_ok, 1)
                        v.wait_ge(cnt_ok, g + 1)
                        then(v.tensor_reduce(csum, cnt[g % 2].rearrange("p t e -> p e t"), AX.X, ALU.add))
                        v.tensor_tensor(run[(g + 1) % 2], run[g % 2], csum, ALU.add).then_inc(run_ok, 1)
                        v.wait_ge(run_ok, g + 1)

                    def dense_gate(g):
                        v.wait_ge(gelu_ok, g + 1)
                        for t in range(g * GT, (g + 1) * GT):
                            after(v, zab_ok, t)
                            v.scalar_tensor_tensor(junk, ab[:, t, :], 1.0, gcw[:, 1, :], ALU.mult, ALU.mult,
                                                   accum_out=zab[:, t:t + 1]).then_inc(zab_ok, 1)

                    def locate(g):
                        v.wait_ge(rank_ps, g + 1)
                        v.tensor_tensor(pos, bank[:, 7, 0:GT * E].rearrange("p (t e) -> p t e", t=GT),
                                        ebase[:].unsqueeze(1).to_broadcast([P, GT, E]), ALU.add).then_inc(pos_ok, 1)
                        v.wait_ge(pos_ok, g + 1)
                        then(v.tensor_tensor(mine, oh[:, :, tiles(g), :], pos.unsqueeze(1).to_broadcast([P, 2, GT, E]), ALU.mult))
                        then(v.tensor_reduce(posf[:, :, tiles(g)], mine, AX.X, ALU.add))
                        v.tensor_copy(slot[:, :, tiles(g)], posf[:, :, tiles(g)]).then_inc(slot_ok, 1)

                    then(v.memset(run[0], 0.0))
                    statistics(0)
                    for g in range(NG + 2):
                        if g >= 2:
                            choose(g - 2)
                        if g + 1 < NG:
                            statistics(g + 1)
                        if g < NG:
                            normalise(g)
                        if g >= 2:
                            locate(g - 2)
                            dense_gate(g - 2)

                    then(v.memset(ones, 1.0))
                    v.wait_ge(tot_ps, 1)
                    then(v.tensor_copy(total, bank[:, 6, 0:E]))
                    then(v.tensor_tensor(shift, total, ebase[:], ALU.add))
                    v.tensor_copy(tails, shift).then_inc(tails_ok, 1)
                    then(v.tensor_tensor(cmpn, cols(total, NT), steps[:].unsqueeze(1).to_broadcast([P, E, NT]), ALU.is_gt))
                    then(v.tensor_reduce(ntile, cmpn, AX.X, ALU.add))
                    then(v.tensor_tensor_scan(tincl, ones[:, 0:E], ntile, 0.0, ALU.mult, ALU.add))
                    sx = cols(sidx[:], E - 1)
                    then(v.tensor_tensor(cmpt, sx, tincl[:, 0:E - 1].unsqueeze(1).to_broadcast([P, SLOTS, E - 1]), ALU.is_ge))
                    then(v.tensor_reduce(tf, cmpt, AX.X, ALU.add))
                    v.tensor_copy(texp, tf).then_inc(texp_ok, 1)
                    then(v.tensor_tensor(weight, cmpt, ntile[:, 0:E - 1].unsqueeze(1).to_broadcast([P, SLOTS, E - 1]), ALU.mult))
                    then(v.tensor_reduce(row, weight, AX.X, ALU.add))
                    then(v.tensor_tensor(row, sidx[:], row, ALU.subtract))
                    then(v.tensor_scalar(tf, tf, float(REGION), float(-E * REGION), ALU.mult, ALU.add))
                    then(v.scalar_tensor_tensor(row, row, float(P), tf, ALU.mult, ALU.add))
                    then(v.tensor_scalar(used, sidx[:], tincl[:, E - 1:E], None, ALU.is_lt))
                    then(v.tensor_tensor(row, row, used, ALU.mult))
                    then(v.tensor_scalar(row, row, float(E * REGION), None, ALU.add))
                    v.tensor_copy(trow, row).then_inc(texp_ok, 1)
                    v.wait_ge(ed_ok, 1)
                    then(v.tensor_scalar(wts[:, 0, :], dtop, 1.0, None, ALU.add))
                    then(v.reciprocal(wts[:, 0, :], wts[:, 0, :]))
                    v.tensor_tensor(wts[:, 1, :], dtop, wts[:, 0, :], ALU.mult).then_inc(wts_ok, 1)
                    then(v.tensor_tensor(texcl, tincl, ntile, ALU.subtract))
                    then(v.scalar_tensor_tensor(shift, texcl, float(P), ebase[:], ALU.mult, ALU.subtract))
                    then(v.tensor_tensor(place, oh[:].rearrange("p k t e -> p (k t) e"),
                                         shift.unsqueeze(1).to_broadcast([P, 2 * NT, E]), ALU.mult))
                    then(v.tensor_reduce(moved, place, AX.X, ALU.add))
                    pf = posf[:].rearrange("p k t -> p (k t)")
                    then(v.tensor_tensor(pf, pf, moved, ALU.add))
                    v.wait_ge(scat, 16 * 2 * NT)
                    v.tensor_copy(slot[:], posf[:]).then_inc(index_ok, 1)

                    def copy_x(j, k, turn):
                        v.wait_ge(xrT_ps, j + 1)
                        after(v, up_ps, j - 1)
                        v.tensor_copy(xrT[k % 2].rearrange("p c n -> p (c n)"), bank[:, k % 2, 0:C]).then_inc(xrT_ok, 1)

                    def step(j, k, turn):
                        if not is_last(j):
                            copy_x(j + 1, k + 1, turn)
                        v.wait_ge(hidT_ps, j + 1)
                        after(v, dn_ps, j - 1)
                        v.tensor_copy(hidT[k % 2].rearrange("p c n -> p (c n)"), bank[:, 4 + k % 2, :]).then_inc(hidT_ok, 1)

                    copy_x(0, 0, 0)
                    over_tiles(v, step)

                    v.wait_ge(sum_ok, NG)
                    for g in range(NG + 1):
                        if g < NG:
                            for t in range(g * GT, (g + 1) * GT):
                                q, k = dif[t % (2 * GT)], t % RING
                                v.wait_ge(g_ld[k], 32 * (t // RING + 1))
                                after(v, x2_ok, t - 2 * GT + 1)
                                v.scalar_tensor_tensor(q, g1[k], wts[:, 0, t:t + 1], ab[:, t, :], ALU.mult, ALU.subtract).then_inc(dif_ok, 1)
                                v.wait_ge(dif_ok, 2 * t + 1)
                                v.scalar_tensor_tensor(q, g2[k], wts[:, 1, t:t + 1], q, ALU.mult, ALU.add).then_inc(dif_ok, 1)
                                v.wait_ge(dif_ok, 2 * t + 2)
                                after(v, z_ok, ZN * g + t % GT)
                                v.scalar_tensor_tensor(junk, q, 1.0, gcw[:, 0, :], ALU.mult, ALU.mult,
                                                       accum_out=z[g % 2][:, t % GT:t % GT + 1]).then_inc(z_ok, 1)
                            v.wait_ge(z_ok, ZN * g + GT)
                            v.scalar_tensor_tensor(z[g % 2], z[g % 2], gcb[:], zab[:, tiles(g)], ALU.add, ALU.add).then_inc(z_ok, 1)
                            v.wait_ge(z_ok, ZN * g + GT + 1)
                            v.tensor_scalar(z[g % 2], z[g % 2], -87.0, None, ALU.max).then_inc(z_ok, 1)
                        if g >= 1:
                            h = g - 1
                            gate = z[h % 2]
                            v.wait_ge(ez_ok, h + 1)
                            v.tensor_scalar(gate, gate, 1.0, None, ALU.add).then_inc(gate_ok, 1)
                            v.wait_ge(gate_ok, 2 * h + 1)
                            v.reciprocal(gate, gate).then_inc(gate_ok, 1)
                            v.wait_ge(gate_ok, 2 * h + 2)
                            for t in range(h * GT, (h + 1) * GT):
                                v.scalar_tensor_tensor(xs[:, t, :], dif[t % (2 * GT)], gate[:, t % GT:t % GT + 1], xs[:, t, :],
                                                       ALU.mult, ALU.add).then_inc(x2_ok, 1)

                @block.gpsimd
                def _(pool):
                    nrm.roots(pool, 0)
                    for g in range(NG + 2):
                        if g + 1 < NG:
                            nrm.roots(pool, g + 1)
                        if g >= 2:
                            pool.wait_ge(slot_ok, g - 1)
                            for t in range((g - 2) * GT, (g - 1) * GT):
                                for k in range(2):
                                    pool.indirect_dma_start(out=xg, out_offset=bass.IndirectOffsetOnAxis(ap=slot[:, k, t:t + 1], axis=0),
                                                            in_=xh[:, t, :], in_offset=None).then_inc(scat, 16)
                    pool.wait_ge(res_ok, GT * NG)
                    pool.wait_ge(gelu_ok, NG)
                    for g in range(NG):
                        pool.tensor_tensor(xs[:, tiles(g), :], xs[:, tiles(g), :], ab[:, tiles(g), :], ALU.add).then_inc(sum_ok, 1)
                    pool.wait_ge(index_ok, 1)
                    for k in range(RING):
                        pool.wait_ge(y_st[k], 16 * len(range(k, SLOTS, RING)))
                    for t in range(NT):
                        after(pool, dif_ok, 2 * (t - RING + 1))
                        for k, buf in enumerate((g1, g2)):
                            pool.indirect_dma_start(out=buf[t % RING], out_offset=None, in_=yg,
                                                    in_offset=bass.IndirectOffsetOnAxis(ap=slot[:, k, t:t + 1], axis=0)
                                                    ).then_inc(g_ld[t % RING], 16)

                @block.sync
                def _(sp):
                    sp.wait_ge(tails_ok, 1)
                    for e in range(E):
                        at = sp.value_load(tails[0:1, e:e + 1], min_val=e * REGION, max_val=e * REGION + T)
                        sp.dma_start(xg[bass.ds(at, P), :], zero[:]).then_inc(padded, 16)
                    sp.wait_ge(texp_ok, 2)
                    sp.wait_ge(padded, 16 * E)
                    sp.wait_ge(scat, 16 * 2 * NT)

                    def fetch(j, k):
                        at = sp.value_load(trow[0:1, j:j + 1] if isinstance(j, int) else trow[0:1, bass.ds(j, 1)],
                                           min_val=0, max_val=E * REGION)
                        sp.dma_start(xr[k % RING], xg[bass.ds(at, P), :]).then_inc(x_ld[k % RING], 16)

                    def step(j, k, turn):
                        if not isinstance(j, int) or j + RING < SLOTS:
                            sp.wait_ge(xrT_ps, j + 1)
                            fetch(j + RING, k)
                        sp.wait_ge(y_ok, j + 1)
                        o = yg.rearrange("(t p) c -> t p c", p=P)
                        o = o[j] if isinstance(j, int) else o[bass.ds(j, 1), :, :].rearrange("o p c -> (o p) c")
                        sp.dma_start(o, yr[k]).then_inc(y_st[k], 16)

                    for j in range(RING):
                        fetch(j, j)
                    over_tiles(sp, step)
                    if r == 1:
                        o = out.rearrange("b (n p) c -> p (b n) c", p=P)
                        for g in range(NG):
                            sp.wait_ge(x2_ok, GT * (g + 1))
                            sp.dma_start(o[:, tiles(g), :], xs[:, tiles(g), :]).then_inc(o_st, 16)
                        sp.wait_ge(o_st, 16 * NG)

                @block.scalar
                def _(act):
                    for g in range(NG + 1):
                        if g < NG:
                            act.wait_ge(xT_ps, g + 1)
                            after(act, ab_ps, g - 1)
                            copy(act, xT[g % 2].rearrange("p c n -> p (c n)"), psum(2, 2)).then_inc(xT_ok, 1)
                            act.wait_ge(xh_ok, GT * (g + 1))
                            for t in range(GT):
                                act.activation(xs[:, g * GT + t, :], xs[:, g * GT + t, :], ACT.Identity, scale=c1[g % 2][:, t:t + 1],
                                               bias=nb[g % 2][:, 0, t:t + 1]).then_inc(res_ok, 1)
                        if g >= 1:
                            act.wait_ge(ab_ps, g)
                            act.activation(ab[:, tiles(g - 1), :].rearrange("p t c -> p (t c)"), psum(4, 2), ACT.Gelu
                                           ).then_inc(gelu_ok, 1)
                    act.wait_ge(d_ok, NG)
                    act.activation(dtop, dtop, ACT.Exp).then_inc(ed_ok, 1)

                    def copy_y(j, k, turn):
                        act.wait_ge(dn_ps, j + 1)
                        after(act, y_st[k % RING], turn * 16)
                        copy(act, yr[k % RING], bank[:, 6 + k % 2, 0:C]).then_inc(y_ok, 1)

                    def step(j, k, turn):
                        act.wait_ge(up_ps, j + 1)
                        after(act, hidT_ps, j - 1)
                        act.activation(hid[k % 2], bank[:, 2 + k % 2, :], ACT.Gelu).then_inc(hid_ok, 1)
                        if not isinstance(j, int) or j >= 1:
                            copy_y(j - 1, (k - 1) % RING, turn if k >= 1 else turn - 1)

                    over_tiles(act, step)
                    copy_y(SLOTS - 1, (SLOTS - 1) % RING, (SLOTS - 1) // RING)
                    for g in range(NG):
                        act.wait_ge(z_ok, ZN * (g + 1))
                        act.activation(z[g % 2], z[g % 2], ACT.Exp, scale=-1.0).then_inc(ez_ok, 1)

                @block.tensor
                def _(pe):
                    def attend(g):
                        after(pe, x1_ok, 2 * g)
                        for t in range(GT):
                            last = pe.matmul(bank[:, t // 2, (t % 2) * C:(t % 2 + 1) * C],
                                             qT[:, (g * GT + t) * P:(g * GT + t + 1) * P], ctxm[:, g * B // NG, :],
                                             start=True, stop=True)
                        last.then_inc(att_ps, 1)

                    def logits(g):
                        pe.wait_ge(xT_ok, g + 1)
                        after(pe, cnt_ok, g)
                        for t in range(GT):
                            o = bank[:, 6, t * E:(t + 1) * E]
                            for c in range(KC):
                                pe.matmul(o, xT[g % 2][:, c, t * P:(t + 1) * P], gw[:, c, :], start=(c == 0), stop=False)
                            last = pe.matmul(o, onesf[:], gateb[:], start=False, stop=True)
                        last.then_inc(lg_ps, 1)

                    def dense(g):
                        after(pe, gelu_ok, g)
                        for t in range(GT):
                            o = bank[:, 4 + t // 2, (t % 2) * C:(t % 2 + 1) * C]
                            for c in range(KC):
                                pe.matmul(o, xT[g % 2][:, c, t * P:(t + 1) * P], abw[:, c, :], start=(c == 0), stop=False)
                            last = pe.matmul(o, onesb[0:2 * QROW + 1, :], abbp[:], start=False, stop=True)
                        last.then_inc(ab_ps, 1)

                    def rank(g):
                        pe.wait_ge(cnt_ok, g + 1)
                        after(pe, pos_ok, g)
                        o = bank[:, 7, 0:GT * E].rearrange("p (t e) -> p t e", t=GT)
                        pe.matmul(o, tri[:], cnt[g % 2], start=True, stop=False, skip_group_check=True)
                        pe.matmul(o, onesb[:], run[g % 2].unsqueeze(1).to_broadcast([P, GT, E]), start=False, stop=False,
                                  skip_group_check=True)
                        for t in range(GT - 1):
                            m = GT - 1 - t
                            last = pe.matmul(o[:, t + 1:, :], onesb[:], cnt[g % 2][:, t:t + 1, :].to_broadcast([P, m, E]),
                                             start=False, stop=(t == GT - 2), skip_group_check=True)
                        last.then_inc(rank_ps, 1)

                    if r == 0:
                        attend(0)
                        attend(1)
                    for g in range(NG + 2):
                        if g < NG:
                            pe.wait_ge(xh_ok, GT * (g + 1))
                            after(pe, xT_ok, g)
                            for c in range(KC):
                                for t in range(GT):
                                    last = pe.transpose(bank[:, 2 + c, t * P:(t + 1) * P], xh[:, g * GT + t, c * P:(c + 1) * P],
                                                        ident[:])
                            last.then_inc(xT_ps, 1)
                        if 1 <= g <= NG:
                            logits(g - 1)
                        if g >= 2:
                            rank(g - 2)
                        if 1 <= g <= NG:
                            dense(g - 1)
                        if r == 0 and g + 2 < NG:
                            attend(g + 2)
                    pe.wait_ge(run_ok, NG)
                    pe.matmul(bank[:, 6, 0:E], onesb[:], run[NG % 2], start=True, stop=True).then_inc(tot_ps, 1)

                    pe.wait_ge(texp_ok, 1)

                    def expert(j):
                        return pe.value_load(texp[0:1, j:j + 1] if isinstance(j, int) else texp[0:1, bass.ds(j, 1)],
                                             min_val=0, max_val=E - 1)

                    def turn_x(j, k, turn):
                        pe.wait_ge(x_ld[k % RING], turn * 16 + 16)
                        after(pe, xrT_ok, j - 1)
                        for c in range(KC):
                            last = pe.transpose(bank[:, k % 2, c * P:(c + 1) * P], xr[k % RING][:, c * P:(c + 1) * P], ident[:])
                        last.then_inc(xrT_ps, 1)

                    def up(j, k):
                        e = expert(j)
                        pe.wait_ge(xrT_ok, j + 1)
                        after(pe, hid_ok, j - 1)
                        o = bank[:, 2 + k % 2, :]
                        for c in range(KC):
                            pe.matmul(o, xrT[k % 2][:, c, :], ew1[:, c, bass.ds(e, 1), :], start=(c == 0), stop=False)
                        pe.matmul(o, sel[:, bass.ds(e, 1), :], eb1p[:], start=False, stop=True).then_inc(up_ps, 1)

                    def turn_h(j, k):
                        pe.wait_ge(hid_ok, j + 1)
                        after(pe, hidT_ok, j - 1)
                        for c in range(HC):
                            last = pe.transpose(bank[:, 4 + k % 2, c * P:(c + 1) * P], hid[k % 2][:, c * P:(c + 1) * P], ident[:])
                        last.then_inc(hidT_ps, 1)

                    def down(j, k):
                        e = expert(j)
                        pe.wait_ge(hidT_ok, j + 1)
                        after(pe, y_ok, j - 1)
                        o = bank[:, 6 + k % 2, 0:C]
                        for c in range(HC):
                            pe.matmul(o, hidT[k % 2][:, c, :], ew2[:, c, bass.ds(e, 1), :], start=(c == 0), stop=False)
                        pe.matmul(o, sel[:, bass.ds(e, 1), :], eb2p[:], start=False, stop=True).then_inc(dn_ps, 1)

                    def step(j, k, turn):
                        up(j, k)
                        if not is_last(j):
                            turn_x(j + 1, k + 1, turn + (k + 1) // RING)
                        if not isinstance(j, int) or j >= 1:
                            down(j - 1, k - 1)
                        turn_h(j, k)

                    turn_x(0, 0, 0)
                    over_tiles(pe, step)
                    down(SLOTS - 1, SLOTS - 1)

        def attention():
            a = Arena(flat(xh))
            lnT, qpT = a.take(KC, N), a.take(KC, N)
            a2 = Arena(flat(ab))
            val = a2.take(BT, C)
            prob = [a2.take(N) for _ in range(2)]
            w = Arena(work[:])
            ln = [w.take(GT, C) for _ in range(2)]
            pT = [w.take(BANK) for _ in range(2)]
            nb = [w.take(GT) for _ in range(2)]
            nmax, rsum, rinv = w.take(BT), w.take(BT), w.take(BT)
            nrm = Norm("b", w)
            nb_ok, ln_ok, lnT_ps, lnT_ok = sem("b_nb"), sem("b_ln"), sem("b_lnT_ps"), sem("b_lnT")
            qv_ps, q_ok, v_ok = sem("b_qv_ps"), sem("b_q"), sem("b_v")
            sc_ps, max_ok, exp_ok = sem("b_sc_ps"), sem("b_max"), sem("b_exp")
            pT_ps, pT_ok, pv_ok, inv_ok, x3_ok = sem("b_pT_ps"), sem("b_pT"), sem("b_pv"), sem("b_inv"), sem("b_x3")
            GB = NG // B
            chunks = [(b, i, c) for b in range(B) for i in range(BT) for c in range(i // GT + 1)]
            at = {x: n for n, x in enumerate(chunks)}

            def weighed(n):
                return at[(n - 1) // BT, (n - 1) % BT, (n - 1) % BT // GT] + 1 if n >= 1 else 0

            def blocks(i, c):
                return min(GT, i + 1 - c * GT)

            with nc.Block() as block:
                @block.gpsimd
                def _(pool):
                    for g in range(NG):
                        nrm.roots(pool, g)

                @block.vector
                def _(v):
                    for b in range(B):
                        for g in range(b * GB, (b + 1) * GB):
                            u = g % 2
                            nrm.statistics(v, g, xs[:, g * GT:(g + 1) * GT, :])
                            v.wait_ge(nrm.root_ok, g + 1)
                            v.scalar_tensor_tensor(nb[u], nrm.sum[u], -0.5, nrm.root[u][:, 0, :], ALU.mult, ALU.mult).then_inc(nb_ok, 1)
                            v.wait_ge(nb_ok, g + 1)
                            after(v, lnT_ps, g - 1)
                            for t in range(GT):
                                v.tensor_scalar(ln[u][:, t, :], xs[:, g * GT + t, :], nrm.root[u][:, 0, t:t + 1],
                                                nb[u][:, t:t + 1], ALU.mult, ALU.add).then_inc(ln_ok, 1)
                        for i in range(BT + 1):
                            n = b * BT + i
                            if i < BT:
                                v.wait_ge(sc_ps, n + 1)
                                v.tensor_reduce(nmax[:, i:i + 1], psum(0, 4)[:, 0:(i + 1) * P], AX.X, ALU.max, negate=True).then_inc(max_ok, 1)
                            if i >= 1:
                                v.wait_ge(exp_ok, n)
                                v.reciprocal(rinv[:, i - 1:i], rsum[:, i - 1:i]).then_inc(inv_ok, 1)
                                v.wait_ge(inv_ok, n)
                                v.wait_ge(pv_ok, weighed(n))
                                v.scalar_tensor_tensor(xs[:, n - 1, :], bank[:, 6 + (n - 1) % 2, 0:C], rinv[:, i - 1:i], xs[:, n - 1, :],
                                                       ALU.mult, ALU.add).then_inc(x3_ok, 1)

                @block.scalar
                def _(act):
                    for b in range(B):
                        after(act, pv_ok, weighed(b * BT))
                        for g in range(b * GB, (b + 1) * GB + 1):
                            l = g - b * GB
                            if l < GB:
                                act.wait_ge(lnT_ps, g + 1)
                                copy(act, lnT[:, :, l * BANK:(l + 1) * BANK], bank[:, 0:2, :]).then_inc(lnT_ok, 1)
                            if l >= 1:
                                act.wait_ge(qv_ps, g)
                                for c in range(KC):
                                    act.activation(qpT[:, c, (l - 1) * BANK:l * BANK], bank[:, 2 + c, :], ACT.Identity,
                                                   bias=qbias[:, c:c + 1]).then_inc(q_ok, 1)
                                copy(act, val[:, (l - 1) * GT:l * GT, :].rearrange("p t c -> p (t c)"), psum(4, 2)).then_inc(v_ok, 1)
                        for i in range(BT + 1):
                            n = b * BT + i
                            if i >= 1:
                                for c in range((i - 1) // GT + 1):
                                    k = at[b, i - 1, c]
                                    act.wait_ge(pT_ps, k + 1)
                                    after(act, pv_ok, k - 1)
                                    wd = blocks(i - 1, c) * P
                                    copy(act, pT[k % 2][:, 0:wd], bank[:, 4 + k % 2, 0:wd]).then_inc(pT_ok, 1)
                            if i < BT:
                                act.wait_ge(max_ok, n + 1)
                                after(act, pv_ok, weighed(n - 1))
                                act.activation(prob[n % 2][:, 0:(i + 1) * P], psum(0, 4)[:, 0:(i + 1) * P], ACT.Exp,
                                               bias=nmax[:, i:i + 1], accum_out=rsum[:, i:i + 1]).then_inc(exp_ok, 1)

                @block.tensor
                def _(pe):
                    def scores(b, i):
                        n = b * BT + i
                        if i == 0:
                            pe.wait_ge(q_ok, KC * GB * (b + 1))
                            pe.wait_ge(v_ok, GB * (b + 1))
                        else:
                            pe.wait_ge(exp_ok, n)
                        for c in range(i // GT + 1):
                            wd = blocks(i, c) * P
                            for k in range(KC):
                                last = pe.matmul(bank[:, c, 0:wd], qpT[:, k, i * P:(i + 1) * P], lnT[:, k, c * BANK:c * BANK + wd],
                                                 start=(k == 0), stop=(k == KC - 1 and c < i // GT), skip_group_check=True)
                        last = pe.matmul(bank[:, i // GT, (i % GT) * P:(i % GT + 1) * P], identb[:], causal[:],
                                         start=False, stop=True, skip_group_check=True)
                        last.then_inc(sc_ps, 1)

                    def weigh(b, i):
                        n = b * BT + i
                        pe.wait_ge(exp_ok, n + 1)
                        o = bank[:, 6 + n % 2, 0:C]
                        last_c = i // GT
                        for c in range(last_c + 2):
                            if c <= last_c:
                                k = at[b, i, c]
                                after(pe, pT_ok, k - 1)
                                for q in range(blocks(i, c)):
                                    last = pe.transpose(bank[:, 4 + k % 2, q * P:(q + 1) * P],
                                                        prob[n % 2][:, (c * GT + q) * P:(c * GT + q + 1) * P], ident[:])
                                last.then_inc(pT_ps, 1)
                            if c >= 1:
                                k = at[b, i, c - 1]
                                pe.wait_ge(pT_ok, k + 1)
                                if c == 1:
                                    after(pe, x3_ok, n - 1)
                                for q in range(blocks(i, c - 1)):
                                    s = (c - 1) * GT + q
                                    last = pe.matmul(o, pT[k % 2][:, q * P:(q + 1) * P], val[:, s, :], start=(s == 0), stop=(s == i))
                                last.then_inc(pv_ok, 1)

                    for b in range(B):
                        for g in range(b * GB, (b + 1) * GB + 1):
                            l = g - b * GB
                            if l < GB:
                                u = g % 2
                                pe.wait_ge(ln_ok, GT * (g + 1))
                                after(pe, lnT_ok, g)
                                if l == 0:
                                    after(pe, exp_ok, b * BT)
                                for c in range(KC):
                                    for t in range(GT):
                                        last = pe.transpose(bank[:, c, t * P:(t + 1) * P], ln[u][:, t, c * P:(c + 1) * P], ident[:])
                                last.then_inc(lnT_ps, 1)
                            if l >= 1:
                                h, m = g - 1, l - 1
                                pe.wait_ge(lnT_ok, h + 1)
                                after(pe, q_ok, KC * h)
                                after(pe, v_ok, h)
                                for j in range(KC):
                                    for c in range(KC):
                                        pe.matmul(bank[:, 2 + j, :], wa[:, c, j * P:(j + 1) * P], lnT[:, c, m * BANK:(m + 1) * BANK],
                                                  start=(c == 0), stop=(c == KC - 1))
                                for t in range(GT):
                                    o = bank[:, 4 + t // 2, (t % 2) * C:(t % 2 + 1) * C]
                                    for c in range(KC):
                                        pe.matmul(o, lnT[:, c, (m * GT + t) * P:(m * GT + t + 1) * P], wvo[:, c, :],
                                                  start=(c == 0), stop=False)
                                    last = pe.matmul(o, onesb[0:2 * QROW + 1, :], vbp[:], start=False, stop=True)
                                last.then_inc(qv_ps, 1)
                        for i in range(BT + 1):
                            if i < BT:
                                scores(b, i)
                            if i >= 1:
                                weigh(b, i - 1)

        weights()
        context()
        release(1)
        mixture(0)
        attention()
        mixture(1)


_INS = ["L0_attn_a_x", "L0_attn_a_Wqkv", "L0_attn_a_Wout", "L0_attn_a_bout", "L0_attn_b_Wq", "L0_attn_b_bq",
        "L0_attn_b_Wk", "L0_attn_b_bk", "L0_attn_b_Wv", "L0_attn_b_bv", "L0_attn_b_Wo", "L0_attn_b_bo",
        "L0_ffn_ln_gamma", "L0_ffn_ln_beta", "L0_ffn_abel_w", "L0_ffn_abel_b", "L0_ffn_moe_gate_w",
        "L0_ffn_moe_gate_b", "L0_ffn_ew1", "L0_ffn_eb1", "L0_ffn_ew2", "L0_ffn_eb2", "L0_ffn_gens", "L0_ffn_gc_w",
        "L0_ffn_gc_b"]


def kernel(**inputs):
    import numpy as _np
    import concourse.bacc as _bacc
    from concourse import mybir as _mybir
    from concourse.bass_utils import run_bass_kernel_spmd as _run

    nc = _bacc.Bacc("TRN2", target_bir_lowering=False, num_devices=1)
    arrays, aps = {}, {}
    for name in _INS:
        a = _np.ascontiguousarray(inputs[name])
        arrays[f"in_{name}_dram"] = a
        aps[name] = nc.dram_tensor(f"in_{name}_dram", a.shape, _mybir.dt.from_np(a.dtype), kind="ExternalInput").ap()
    shape = arrays["in_L0_attn_a_x_dram"].shape
    out = nc.dram_tensor("out_0_dram", shape, _mybir.dt.float32, kind="ExternalOutput").ap()
    build(nc, aps, out)
    r = _run(nc, [arrays], core_ids=[0])
    return r.results[0]["out_0_dram"]
```

```python
from contextlib import ExitStack

import concourse.bass as bass
from concourse import mybir

F32, F32R, BF16, I32 = mybir.dt.float32, mybir.dt.float32r, mybir.dt.bfloat16, mybir.dt.int32
ACT, ALU, AX = mybir.ActivationFunctionType, mybir.AluOpType, mybir.AxisListType
P = 128
EPS = 1e-5
BANK = 512
LOWEST = -3.0e38


def build(nc, d, out):
    B, N, C = d["L0_attn_a_x"].shape
    HD = d["L0_attn_a_Wout"].shape[0]
    E, _, H = d["L0_ffn_ew1"].shape
    NROT = d["L0_ffn_gens"].shape[0]
    HEADS = 8
    DH = HD // HEADS
    T = B * N
    NT = T // P
    BT = N // P
    KC = C // P
    HC = H // P
    GT = BANK // P
    NG = NT // GT
    SLOTS = 2 * T // P + E - 1
    REGION = T + P
    CW = C + 2
    WORK = 7168
    ROUTE = 669
    QROW = 32

    ctx = ExitStack()
    with ctx:
        def sb(name, shape, dt=F32):
            return ctx.enter_context(nc.sbuf_tensor(name, shape, dt))

        taken = []

        def sem(name):
            taken.append(nc.alloc_semaphore(name))
            return taken[-1]

        def release(first):
            nc.clear_and_free_semaphores(taken[first:])
            del taken[first:]
            nc.all_engine_barrier()

        def under(name, shape, dt):
            with nc.sbuf_tensor(name, shape, dt) as t:
                return t

        low1_in = under("low1_in", [P, E, KC, H], F32)
        xs = sb("xs", [P, NT, C])
        keys = under("keys", [P, 2, KC, N], F32)
        rows = under("rows", [P, 2, 2, (KC + HC) * P], F32)
        xh = sb("xh", [P, NT, CW])
        values = under("values", [P, 2, BT, C], F32)
        low2_in = under("low2_in", [P, E, HC, C], F32)
        ab = sb("ab", [P, NT, C])
        ew1 = sb("ew1", [P, KC, E, H])
        queries = under("queries", [P, 2, KC, N], F32)
        ew2 = sb("ew2", [P, HC, E, C])
        abw = sb("abw", [P, KC, C + E])
        gcw = sb("gcw", [P, 2, C])
        gcb = sb("gcb", [P, 1])
        eb1p = sb("eb1p", [2 * QROW + E, H], BF16)
        eb2p = sb("eb2p", [2 * QROW + E, C], BF16)
        abbp = sb("abbp", [2 * QROW + 1, C + E], BF16)
        vbp = sb("vbp", [2 * QROW + 1, C], BF16)
        sel = sb("sel", [2 * QROW + E, E, P], BF16)
        wa = sb("wa", [P, KC, C])
        wvo = sb("wvo", [P, KC, C])
        qbias = sb("qbias", [P, KC])
        gam = sb("gam", [P, KC])
        ident = sb("ident", [P, P])
        identb = sb("identb", [P, P], BF16)
        causal = sb("causal", [P, P], BF16)
        tri = sb("tri", [P, P], BF16)
        onesb = sb("onesb", [P, P], BF16)
        onesf = sb("onesf", [1, P])
        mhalf = sb("mhalf", [P, 2 * GT])
        eidx = sb("eidx", [P, E])
        ebase = sb("ebase", [P, E])
        steps = sb("steps", [P, NT])
        sidx = sb("sidx", [P, SLOTS])
        zero = sb("zero", [P, CW])
        token = sb("token", [P, NT])
        ctxm = sb("ctxm", [HD + 1, B, C])
        wout = sb("wout", [HD, C])
        hmask = sb("hmask", [HD, HD])
        shares = under("shares", [P, 2, 2, BANK], F32)
        work = sb("work", [P, WORK])
        bank = ctx.enter_context(nc.psum_tensor("bank", [P, 8, BANK], F32))
        xg = nc.dram_tensor("slots_in", (E * REGION + P, CW), F32).ap()
        yg = nc.dram_tensor("results", (2 * T + 2 * P, CW), F32).ap()

        low1 = nc.dram_tensor("low1", (E, P, KC * H), F32).ap()
        low2 = nc.dram_tensor("low2", (E, P, HC * C), F32).ap()
        high2 = nc.dram_tensor("high2", (E, P, HC * C), F32).ap()
        xs_out = nc.dram_tensor("residual", (NG, P, GT * C), F32).ap()
        ab_out = nc.dram_tensor("dense", (NG, P, GT * C), F32).ap()

        x_in = sem("x_in")

        class Arena:
            def __init__(self, flat):
                self.flat, self.at = flat, 0

            def take(self, *shape, dt=F32, rows=P):
                n = 1
                for s in shape:
                    n *= s
                w = n if dt in (F32, I32) else (n + 1) // 2
                v = self.flat[0:rows, self.at:self.at + w]
                self.at += w
                assert self.at <= self.flat.shape[1], self.at
                if dt != F32:
                    v = v.bitcast(dt)
                if len(shape) == 2:
                    v = v.rearrange("p (a b) -> p a b", a=shape[0])
                if len(shape) == 3:
                    v = v.rearrange("p (a b c) -> p a b c", a=shape[0], b=shape[1])
                return v

        def flat(t):
            return t[:].rearrange("p a b -> p (a b)")

        wqkv = flat(ab)[:, NT * C - KC * 3 * HD:].rearrange("p (c n) -> p c n", c=KC)

        R = flat(xh)[:, 0:KC * C].rearrange("p (c j) -> p c j", c=KC)

        def cols(view, bc):
            return view.unsqueeze(len(view.shape)).to_broadcast(list(view.shape) + [bc])

        def f32r(view):
            return view.bitcast(F32R)

        def psum(b, n=1):
            return bank[:, b:b + n, :].rearrange("p a b -> p (a b)")

        def copy(eng, o, i, scale=1.0):
            return eng.activation(o, i, ACT.Copy, scale=scale)

        def weights():
            a = Arena(flat(xh))
            a.take(KC, C)
            gens = a.take(NROT, KC, C)
            A = a.take(NROT, KC, C)
            AT = a.take(NROT, KC, C)
            X = a.take(NROT, KC, C)
            eye = a.take(KC, C)
            w = work[:]
            a2 = Arena(w)
            a3 = Arena(flat(ab)[:, NT * C // 2:])
            w4 = [a3.take(KC, C) for _ in range(4)]
            woT = a2.take(KC, C)
            bsel = a2.take(KC, E * E)
            bet = a2.take(KC)
            bqc, bvc = a2.take(KC), a2.take(KC)
            eb2s = a2.take(C, rows=E)
            eb2T = a2.take(KC, E)
            eb1s = a2.take(H, rows=E)
            row = a2.take(2, C, rows=1)
            frow = a2.take(C + E, rows=1)
            rem = a2.take(H, rows=E)
            rem2 = a2.take(C, rows=E)
            p2 = a2.take(H, rows=E, dt=BF16)
            gsum = a2.take(NROT * KC)
            gmx, gall = a2.take(1), a2.take(1)
            thr = a2.take(24)
            cmp = a2.take(24)
            sf, scf, scale = a2.take(1), a2.take(1), a2.take(1)
            sqi = a2.take(1, dt=I32)
            ki = a2.take(24, dt=I32)
            ei, bi = a2.take(E, dt=I32), a2.take(E, dt=I32)
            ti, ri, zi = a2.take(NT, dt=I32), a2.take(NT, dt=I32), a2.take(1, dt=I32)
            ji = a2.take(SLOTS, dt=I32)

            w_small, w_ew, w_gens, w_proj = sem("w_small"), sem("w_ew"), sem("w_gens"), sem("w_proj")
            zero_ok, zeroed = sem("zero_ok"), sem("blank_tile")
            consts, iotas, order = sem("consts"), sem("iotas"), sem("pool_order")
            bsel_ok, beta_mm, row_ok = sem("bsel_ok"), sem("beta_mm"), sem("row_ok")
            dve = sem("dve_order")
            g_mx, g_all, A_ok, AT_ps, AT_ok = sem("g_mx"), sem("g_all"), sem("A_ok"), sem("AT_ps"), sem("AT_ok")
            horner_ps, X_ok, s_ok = sem("horner_ps"), sem("X_ok"), sem("s_ok")
            A2_ps, A2_ok, A3_ps, A3_ok, A3T_ps, A3T_ok = (sem("A2_ps"), sem("A2_ok"), sem("A3_ps"), sem("A3_ok"),
                                                          sem("A3T_ps"), sem("A3T_ok"))
            poly_ok, b_ok = sem("poly_ok"), sem("b_ok")
            sq_T, ET_ok, sq_Y = sem("sq_T"), sem("ET_ok"), sem("sq_Y")
            rot_T, rot_TS, rot_Y, rot_ok = sem("rot_T"), sem("rot_TS"), sem("rot_Y"), sem("rot_ok")
            eb2_T, eb2_TS, eb2_Y = sem("eb2_T"), sem("eb2_TS"), sem("eb2_Y")
            at_ps, at_ok, vb_ok = sem("at_ps"), sem("at_ok"), sem("vb_ok")
            POLY = 4
            polys = [A, a2.take(NROT, KC, C), a2.take(NROT, KC, C), X]
            A3 = a3.take(NROT, KC, C)
            A2 = gens
            ratio = [1.0 / ((3 * i + 1) * (3 * i + 2) * (3 * i + 3)) for i in range(POLY)]

            with nc.Block() as block:
                @block.sync
                def _(sp):
                    one = lambda k: d[k].rearrange("(o n) -> o n", o=1)
                    colv = lambda k: d[k].rearrange("(c p) -> p c", p=P)
                    chunked = lambda k: d[k].rearrange("(c p) n -> p c n", p=P)
                    small = [
                        (gam[:], colv("L0_ffn_ln_gamma")), (bet, colv("L0_ffn_ln_beta")),
                        (bqc, colv("L0_attn_b_bq")), (bvc, colv("L0_attn_b_bv")),
                        (abw[:, :, 0:C], chunked("L0_ffn_abel_w")), (abw[:, :, C:], chunked("L0_ffn_moe_gate_w")),
                        (eb1s, d["L0_ffn_eb1"]), (eb2s, d["L0_ffn_eb2"]),
                        (frow[:, 0:C], one("L0_ffn_abel_b")), (row[:, 0, :], one("L0_attn_b_bo")),
                        (frow[:, C:], one("L0_ffn_moe_gate_b")),
                    ]
                    assert len(small) == 11
                    for o, i in small:
                        sp.dma_start(o, i, allow_slow_non_contiguous=True).then_inc(w_small, 16)
                    for h in range(2):
                        sp.dma_start(gcw[:, h, :], d["L0_ffn_gc_w"][(1 - h) * C:(2 - h) * C, :].rearrange("n o -> (o n)")
                                     .partition_broadcast(P)).then_inc(w_small, 16)
                    sp.dma_start(gcb[:], d["L0_ffn_gc_b"].partition_broadcast(P)).then_inc(w_small, 16)
                    sp.wait_ge(w_gens, 16)
                    for c in range(KC):
                        sp.dma_start(ew1[:, c, :, :], d["L0_ffn_ew1"][:, c * P:(c + 1) * P, :].rearrange("e p h -> p e h")
                                     ).then_inc(w_ew, 16)
                    for c in range(HC):
                        sp.dma_start(ew2[:, c, :, :], d["L0_ffn_ew2"][:, c * P:(c + 1) * P, :].rearrange("e p h -> p e h")
                                     ).then_inc(w_ew, 16)
                    sp.wait_ge(zero_ok, 2)
                    sp.dma_start(xg[E * REGION:E * REGION + P, :], zero[:]).then_inc(zeroed, 16)
                    sp.wait_ge(zeroed, 16)

                @block.gpsimd
                def _(pool):
                    n = 0

                    def then(ins):
                        nonlocal n
                        n += 1
                        ins.then_inc(order, 1)
                        pool.wait_ge(order, n)

                    def select(t, pattern, base, cm, op, fill):
                        return pool.affine_select(out=t, in_=t, compare_op=op, fill=fill, base=base, pattern=pattern,
                                                  channel_multiplier=cm)

                    pool.iota(ki, pattern=[[1, 24]], base=127, channel_multiplier=0).then_inc(iotas, 1)
                    pool.iota(ei, pattern=[[1, E]], base=-E, channel_multiplier=0).then_inc(iotas, 1)
                    pool.iota(bi, pattern=[[REGION, E]], base=0, channel_multiplier=0).then_inc(iotas, 1)
                    pool.iota(ti, pattern=[[P, NT]], base=0, channel_multiplier=0).then_inc(iotas, 1)
                    pool.iota(ri, pattern=[[2 * P, NT]], base=0, channel_multiplier=2).then_inc(iotas, 1)
                    pool.iota(zi, pattern=[[0, 1]], base=2 * T, channel_multiplier=2).then_inc(iotas, 1)
                    pool.iota(ji, pattern=[[1, SLOTS]], base=0, channel_multiplier=0).then_inc(iotas, 1)
                    then(pool.memset(ident[:], 0.0))
                    select(ident[:], [[-1, P]], 0, 1, ALU.not_equal, 1.0).then_inc(consts, 1)
                    then(pool.memset(eye, 0.0))
                    select(eye, [[P, KC], [-1, C]], 0, 1, ALU.not_equal, 1.0).then_inc(consts, 1)
                    then(pool.memset(identb[:], 0.0))
                    select(identb[:], [[-1, P]], 0, 1, ALU.not_equal, 1.0).then_inc(consts, 1)
                    then(pool.memset(zero[:], 0.0))
                    pool.memset(zero[:, C + 1:], -1.0).then_inc(zero_ok, 1)
                    then(pool.memset(tri[:], 1.0))
                    select(tri[:], [[1, P]], 0, -1, ALU.is_gt, 0.0).then_inc(consts, 1)
                    then(pool.memset(causal[:], 0.0))
                    select(causal[:], [[-1, P]], 0, 1, ALU.is_ge, LOWEST).then_inc(consts, 1)
                    then(pool.memset(sel[:], 0.0))
                    for q in range(3):
                        then(select(sel[:], [[-1, E], [0, P]], -QROW * q, 1, ALU.not_equal, 1.0))
                    hm = hmask[:].rearrange("p (h e) -> p h e", h=HEADS)
                    then(pool.memset(hmask[:], 1.0))
                    then(select(hm, [[-DH, HEADS], [0, DH]], 0, 1, ALU.is_ge, 0.0))
                    then(select(hm, [[DH, HEADS], [0, DH]], DH - 1, -1, ALU.is_ge, 0.0))
                    pool.memset(onesb[:], 1.0).then_inc(consts, 1)
                    pool.memset(onesf[:], 1.0).then_inc(consts, 1)
                    pool.memset(mhalf[:], -0.5).then_inc(consts, 1)
                    for t in (eb1p, eb2p, abbp, vbp):
                        pool.memset(t[:], 0.0).then_inc(consts, 1)
                    pool.wait_ge(g_mx, 1)
                    pool.partition_all_reduce(gall, gmx, P, bass.bass_isa.ReduceOp.max).then_inc(g_all, 1)

                @block.vector
                def _(v):
                    n = 0

                    def then(ins):
                        nonlocal n
                        n += 1
                        ins.then_inc(dve, 1)
                        v.wait_ge(dve, n)

                    def parts(o, src, width, rows):
                        r, q = rem[0:rows, 0:width], p2[0:rows, 0:width]
                        then(v.tensor_copy(o[0:rows, :], src))
                        then(v.tensor_tensor(r, src, o[0:rows, :], ALU.subtract))
                        then(v.tensor_copy(q, r))
                        then(v.tensor_copy(o[QROW:QROW + rows, :], q))
                        then(v.tensor_tensor(r, r, q, ALU.subtract))
                        then(v.tensor_copy(o[2 * QROW:2 * QROW + rows, :], r))

                    v.wait_ge(iotas, 7)
                    then(v.tensor_scalar(thr.bitcast(I32), ki, 23, None, ALU.logical_shift_left))
                    v.tensor_copy(eidx[:], ei)
                    v.tensor_copy(ebase[:], bi)
                    v.tensor_copy(steps[:], ti)
                    v.tensor_copy(token[:], ri)
                    then(v.tensor_copy(sidx[:], ji))
                    v.wait_ge(w_gens, 16)
                    then(v.tensor_reduce(gsum, gens.rearrange("p m c j -> p (m c) j"), AX.X, ALU.add,
                                         apply_absolute_value=True))
                    v.tensor_reduce(gmx, gsum, AX.X, ALU.max).then_inc(g_mx, 1)
                    v.wait_ge(g_all, 1)
                    then(v.tensor_scalar(cmp, thr, gall, None, ALU.is_lt))
                    then(v.tensor_reduce(sf, cmp, AX.X, ALU.add))
                    then(v.tensor_scalar(sf, sf, 1.0, None, ALU.max))
                    v.tensor_copy(sqi, sf).then_inc(s_ok, 1)
                    then(v.tensor_scalar(scf, sf, -1.0, 127.0, ALU.mult, ALU.add))
                    then(v.tensor_copy(scale.bitcast(I32), scf))
                    then(v.tensor_scalar(scale.bitcast(I32), scale.bitcast(I32), 23, None, ALU.logical_shift_left))
                    for m in range(NROT):
                        v.tensor_scalar(A[:, m], gens[:, m], scale, None, ALU.mult).then_inc(A_ok, 1)
                    v.wait_ge(A_ok, NROT)
                    v.wait_ge(consts, 2)
                    for m in range(NROT):
                        v.wait_ge(A2_ps, m + 1)
                        v.tensor_copy(A2[:, m], bank[:, NROT + m, :].rearrange("p (c j) -> p c j", c=KC)).then_inc(A2_ok, 1)
                    v.wait_ge(A2_ok, NROT)
                    for q, i in enumerate((3, 2, 1, 0)):
                        for m in range(NROT):
                            v.scalar_tensor_tensor(polys[i][:, m], A[:, m], 1.0 / (3 * i + 1), eye, ALU.mult, ALU.add).then_inc(poly_ok, 1)
                        for m in range(NROT):
                            v.wait_ge(poly_ok, NROT * q + m + 1)
                            last = v.scalar_tensor_tensor(polys[i][:, m], A2[:, m], 1.0 / ((3 * i + 1) * (3 * i + 2)), polys[i][:, m],
                                                          ALU.mult, ALU.add)
                            last.then_inc(X_ok if i == 3 else b_ok, 1)
                    then(v.memset(bsel, 0.0))
                    v.wait_ge(w_small, 16 * 14)
                    for c in range(KC):
                        last = v.tensor_copy(bsel[:, c, 0:E * E:E + 1], bet[:, c:c + 1].to_broadcast([P, E]))
                    last.then_inc(bsel_ok, 1)
                    v.wait_ge(zero_ok, 1)
                    v.tensor_copy(zero[:, C:C + 1], zi).then_inc(zero_ok, 1)
                    for q, i in enumerate((2, 1, 0)):
                        v.wait_ge(b_ok, NROT * (q + 1))
                        for m in range(NROT):
                            v.wait_ge(horner_ps, NROT * q + m + 1)
                            v.scalar_tensor_tensor(X[:, m], bank[:, m, :].rearrange("p (c j) -> p c j", c=KC), ratio[i],
                                                   polys[i][:, m], ALU.mult, ALU.add).then_inc(X_ok, 1)
                    v.wait_ge(s_ok, 1)
                    s = v.value_load(sqi[0:1, 0:1], min_val=1, max_val=24)
                    with v.Fori(0, s) as i:
                        for m in range(NROT):
                            v.wait_ge(sq_Y, i * NROT + (m + 1))
                            v.tensor_copy(X[:, m], bank[:, NROT + m, :].rearrange("p (c j) -> p c j", c=KC)).then_inc(X_ok, 1)
                    v.wait_ge(rot_Y, 1)
                    v.tensor_copy(X[:, 0], bank[:, 6, :].rearrange("p (c j) -> p c j", c=KC)).then_inc(rot_ok, 1)
                    v.wait_ge(rot_Y, 2)
                    v.tensor_copy(R, bank[:, 7, :].rearrange("p (c j) -> p c j", c=KC)).then_inc(rot_ok, 1)
                    v.wait_ge(consts, 12)
                    v.wait_ge(beta_mm, 1)
                    then(v.tensor_tensor(eb1s, eb1s, bank[0:E, 3, :], ALU.add))
                    then(v.tensor_tensor(frow, frow, bank[0:1, 4, 0:C + E], ALU.add))
                    parts(eb1p, eb1s, H, E)
                    parts(abbp, frow, C + E, 1)
                    for c in range(KC):
                        v.tensor_scalar(abw[:, c], abw[:, c], gam[:, c:c + 1], None, ALU.mult)
                    v.wait_ge(at_ps, 4)
                    then(v.tensor_tensor(row[:, 1, :], row[:, 0, :], bank[0:1, 5, 0:C], ALU.add))
                    parts(vbp, row[:, 1, :], C, 1)
                    v.tensor_scalar(qbias[:], bank[:, 6, 0:KC], C ** -0.5, None, ALU.mult).then_inc(vb_ok, 1)
                    v.wait_ge(eb2_Y, 1)
                    then(v.tensor_copy(rem2[0:E, :], bank[0:E, 2, 0:C]))
                    parts(eb2p, rem2[0:E, :], C, E)

                @block.scalar
                def _(act):
                    act.dma_start(gens, d["L0_ffn_gens"].rearrange("m (c p) j -> p m c j", p=P)).then_inc(w_gens, 16)
                    for o, k in zip(w4, "qkvo"):
                        act.dma_start(o, d[f"L0_attn_b_W{k}"].rearrange("(c p) n -> p c n", p=P)).then_inc(w_proj, 16)
                    for q in range(4):
                        ts = slice(q * NT // 4, (q + 1) * NT // 4)
                        act.dma_start(xs[:, ts, :], d["L0_attn_a_x"].rearrange("b (n p) c -> p (b n) c", p=P)[:, ts, :]
                                      ).then_inc(x_in, 16)
                    act.dma_start(wqkv, d["L0_attn_a_Wqkv"].rearrange("(c p) n -> p c n", p=P)).then_inc(x_in, 16)
                    act.dma_start(wout[:], d["L0_attn_a_Wout"]).then_inc(x_in, 16)
                    for b in range(B):
                        act.dma_start(ctxm[HD:HD + 1, b, :], d["L0_attn_a_bout"].rearrange("(o n) -> o n", o=1)).then_inc(x_in, 16)
                    for m in range(NROT):
                        act.wait_ge(AT_ps, m + 1)
                        copy(act, AT[:, m], bank[:, m, :].rearrange("p (c j) -> p c j", c=KC)).then_inc(AT_ok, 1)
                    for m in range(NROT):
                        act.wait_ge(A3_ps, m + 1)
                        copy(act, A3[:, m], bank[:, m, :].rearrange("p (c j) -> p c j", c=KC)).then_inc(A3_ok, 1)
                    for m in range(NROT):
                        act.wait_ge(A3T_ps, m + 1)
                        copy(act, AT[:, m], bank[:, NROT + m, :].rearrange("p (c j) -> p c j", c=KC)).then_inc(A3T_ok, 1)
                    act.wait_ge(s_ok, 1)
                    s = act.value_load(sqi[0:1, 0:1], min_val=1, max_val=24)
                    with act.Fori(0, s) as i:
                        for m in range(NROT):
                            act.wait_ge(sq_T, i * NROT + (m + 1))
                            copy(act, AT[:, m], bank[:, m, :].rearrange("p (c j) -> p c j", c=KC)).then_inc(ET_ok, 1)
                    for q in range(2):
                        act.wait_ge(rot_T, q + 1)
                        copy(act, AT[:, 0], bank[:, 0, :].rearrange("p (c j) -> p c j", c=KC)).then_inc(rot_TS, 1)
                    act.wait_ge(at_ps, 1)
                    copy(act, wa[:], bank[:, 0, :].rearrange("p (c j) -> p c j", c=KC), C ** -0.5).then_inc(at_ok, 1)
                    act.wait_ge(at_ps, 2)
                    copy(act, woT, bank[:, 1, :].rearrange("p (c j) -> p c j", c=KC)).then_inc(at_ok, 1)
                    act.wait_ge(at_ps, 3)
                    copy(act, wvo[:], bank[:, 2, :].rearrange("p (c j) -> p c j", c=KC)).then_inc(at_ok, 1)
                    act.wait_ge(eb2_T, 1)
                    copy(act, eb2T, bank[:, 0, 0:KC * E].rearrange("p (c e) -> p c e", c=KC)).then_inc(eb2_TS, 1)

                @block.tensor
                def _(pe):
                    def transposed(b, src, m):
                        for kc in range(KC):
                            for ic in range(KC):
                                last = pe.transpose(bank[:, b, kc * C + ic * P:kc * C + (ic + 1) * P],
                                                    src[:, ic, kc * P:(kc + 1) * P], ident[:])
                        return last

                    def product(b, leftT, right):
                        for rc in range(KC):
                            for kc in range(KC):
                                last = pe.matmul(bank[:, b, rc * C:(rc + 1) * C], leftT[:, kc, rc * P:(rc + 1) * P],
                                                 right[:, kc, :], start=(kc == 0), stop=(kc == KC - 1))
                        return last

                    pe.wait_ge(consts, 1)
                    for m in range(NROT):
                        pe.wait_ge(A_ok, m + 1)
                        transposed(m, A[:, m], m).then_inc(AT_ps, 1)
                    for m in range(NROT):
                        pe.wait_ge(AT_ok, m + 1)
                        product(NROT + m, AT[:, m], A[:, m]).then_inc(A2_ps, 1)
                    for m in range(NROT):
                        pe.wait_ge(A2_ok, m + 1)
                        product(m, AT[:, m], A2[:, m]).then_inc(A3_ps, 1)
                    for m in range(NROT):
                        pe.wait_ge(A3_ok, m + 1)
                        transposed(NROT + m, A3[:, m], m).then_inc(A3T_ps, 1)
                    for q in range(POLY - 1):
                        for m in range(NROT):
                            pe.wait_ge(A3T_ok, m + 1)
                            pe.wait_ge(X_ok, NROT * q + m + 1)
                            product(m, AT[:, m], X[:, m]).then_inc(horner_ps, 1)
                    pe.wait_ge(s_ok, 1)
                    done = NROT * (POLY - 1)
                    s = pe.value_load(sqi[0:1, 0:1], min_val=1, max_val=24)
                    with pe.Fori(0, s) as i:
                        for m in range(NROT):
                            pe.wait_ge(X_ok, i * NROT + (done + m + 1))
                            transposed(m, X[:, m], m).then_inc(sq_T, 1)
                        for m in range(NROT):
                            pe.wait_ge(ET_ok, i * NROT + (m + 1))
                            product(NROT + m, AT[:, m], X[:, m]).then_inc(sq_Y, 1)
                    pe.wait_ge(X_ok, s * NROT + (done + NROT))
                    transposed(0, X[:, 0], 0).then_inc(rot_T, 1)
                    pe.wait_ge(rot_TS, 1)
                    product(6, AT[:, 0], X[:, 1]).then_inc(rot_Y, 1)
                    pe.wait_ge(rot_ok, 1)
                    transposed(0, X[:, 0], 0).then_inc(rot_T, 1)
                    pe.wait_ge(rot_TS, 2)
                    product(7, AT[:, 0], X[:, 2]).then_inc(rot_Y, 1)
                    pe.wait_ge(w_small, 16 * 14)
                    pe.wait_ge(w_ew, 16 * (KC + HC))
                    pe.wait_ge(bsel_ok, 1)
                    for e in range(E):
                        for c in range(KC):
                            pe.matmul(bank[0:E, 3, :], bsel[:, c, e * E:(e + 1) * E], ew1[:, c, e, :],
                                      start=(e == 0 and c == 0), stop=(e == E - 1 and c == KC - 1))
                    for c in range(KC):
                        last = pe.matmul(bank[0:1, 4, 0:C + E], bet[:, c:c + 1], abw[:, c, :], start=(c == 0), stop=(c == KC - 1))
                    last.then_inc(beta_mm, 1)
                    pe.wait_ge(w_proj, 16 * 4)
                    wq, wk, wv, wo = w4
                    product(0, wq, wk).then_inc(at_ps, 1)
                    transposed(1, wo, 0).then_inc(at_ps, 1)
                    pe.wait_ge(at_ok, 2)
                    product(2, wv, woT).then_inc(at_ps, 1)
                    for c in range(KC):
                        pe.matmul(bank[0:1, 5, 0:C], bvc[:, c:c + 1], woT[:, c, :], start=(c == 0), stop=(c == KC - 1))
                    for j in range(KC):
                        for c in range(KC):
                            last = pe.matmul(bank[:, 6, j:j + 1], wk[:, c, j * P:(j + 1) * P], bqc[:, c:c + 1],
                                             start=(j == 0 and c == 0), stop=(c == KC - 1), skip_group_check=True)
                    last.then_inc(at_ps, 1)
                    pe.wait_ge(rot_ok, 2)
                    pe.wait_ge(at_ok, 3)
                    for c in range(KC):
                        last = pe.transpose(bank[:, 0, c * E:(c + 1) * E], eb2s[:, c * P:(c + 1) * P], ident[0:E, 0:E])
                    last.then_inc(eb2_T, 1)
                    pe.wait_ge(eb2_TS, 1)
                    for c in range(KC):
                        last = pe.matmul(bank[0:E, 2, 0:C], eb2T[:, c, :], R[:, c, :], start=(c == 0), stop=(c == KC - 1))
                    last.then_inc(eb2_Y, 1)
        def after(eng, semaphore, value):
            if not isinstance(value, int) or value >= 1:
                eng.wait_ge(semaphore, value)

        class Norm:
            def __init__(self, name, arena, ring=2):
                self.ring = ring
                self.st = [arena.take(GT, 6) for _ in range(2)]
                self.sum = [arena.take(GT) for _ in range(ring)]
                self.dif, self.m2, self.var = arena.take(GT), arena.take(GT), arena.take(GT)
                self.args, self.roots_ = arena.take(ring * 2 * GT), arena.take(ring * 2 * GT)
                self.arg, self.root = ([v[:, u * 2 * GT:(u + 1) * 2 * GT].rearrange("p (a t) -> p a t", a=2) for u in range(ring)]
                                       for v in (self.args, self.roots_))
                self.stats_ok, self.sums_ok = sem(name + "_stats"), sem(name + "_sums")
                self.var_ok, self.arg_ok, self.root_ok = sem(name + "_var"), sem(name + "_arg"), sem(name + "_root")

            def statistics(self, v, n, tiles):
                u = n % self.ring
                st, dif, m2, var = self.st[n % 2], self.dif, self.m2, self.var
                for t in range(GT):
                    v.bn_stats(st[:, t, :], tiles[:, t, :]).then_inc(self.stats_ok, 1)
                v.wait_ge(self.stats_ok, GT * (n + 1))
                v.tensor_tensor(self.sum[u], st[:, :, 1], st[:, :, 4], ALU.add).then_inc(self.sums_ok, 1)
                v.tensor_tensor(dif, st[:, :, 1], st[:, :, 4], ALU.subtract).then_inc(self.sums_ok, 1)
                v.tensor_tensor(m2, st[:, :, 2], st[:, :, 5], ALU.add).then_inc(self.sums_ok, 1)
                v.wait_ge(self.sums_ok, 3 * (n + 1))
                v.scalar_tensor_tensor(dif, dif, 0.25, dif, ALU.mult, ALU.mult).then_inc(self.var_ok, 1)
                v.wait_ge(self.var_ok, 2 * n + 1)
                v.scalar_tensor_tensor(var, m2, 1.0 / C, dif, ALU.mult, ALU.add).then_inc(self.var_ok, 1)
                v.wait_ge(self.var_ok, 2 * n + 2)
                v.tensor_scalar(self.arg[u][:, 0, :], var, EPS, None, ALU.add).then_inc(self.arg_ok, 1)
                v.tensor_scalar(self.arg[u][:, 1, :], var, 1.0 + EPS, EPS * EPS, ALU.mult, ALU.add).then_inc(self.arg_ok, 1)

            def roots(self, pool, n, many=1):
                u = n % self.ring
                at = slice(u * 2 * GT, (u + many) * 2 * GT)
                pool.wait_ge(self.arg_ok, 2 * (n + many))
                pool.tensor_tensor(self.roots_[:, at], self.args[:, at], mhalf[:, 0:1].to_broadcast([P, many * 2 * GT]), ALU.pow).then_inc(self.root_ok, 1)

        qT = work[0:HD + 1, 0:T]
        route = Arena(work[:, WORK - ROUTE:WORK])
        zab = route.take(NT)
        oh = route.take(2 * NT, E, dt=BF16).rearrange("p (k t) e -> p k t e", k=2)
        dtop, wts = route.take(NT), route.take(NT, 2)
        slot = route.take(2, NT, dt=I32)
        either = route.take(2 * SLOTS)
        texp, trow = (either[:, q * SLOTS:(q + 1) * SLOTS].bitcast(I32) for q in range(2))
        texpf = route.take(SLOTS)
        tails = route.take(E, dt=I32)

        def context():
            a = Arena(flat(ab))
            ln = [a.take(GT, C) for _ in range(2)]
            lnT = [a.take(KC, BANK) for _ in range(2)]
            vs = [a.take(GT, HD) for _ in range(2)]
            ks = [a.take(GT * HEADS, DH) for _ in range(2)]
            kmax, ksum = a.take(GT * HEADS), a.take(GT * HEADS)
            nb = [a.take(GT) for _ in range(2)]
            cm = [a.take(HD, rows=HD) for _ in range(B)]
            nrm = Norm("a", a)
            nb_ok, ln_ok, lnT_ps, lnT_ok = sem("a_nb"), sem("a_ln"), sem("a_lnT_ps"), sem("a_lnT")
            kvq_ps, vq_ok, kmax_ok, ksh_ok = sem("a_kvq_ps"), sem("a_vq"), sem("a_kmax"), sem("a_kshift")
            kexp_ok, ksum_ok, k_ok, ctx_ps = sem("a_kexp"), sem("a_ksum"), sem("a_k"), sem("a_ctx_ps")
            cm_ok, m_ps, ones_ok, m_ok = sem("a_cm"), sem("a_m_ps"), sem("a_ones"), sem("a_m")
            GB = NG // B
            fa = Arena(flat(xh)[:, KC * C:])
            HH = HC // 2
            ew2T = [fa.take(KC, HH * P) for _ in range(2)]
            fold_T, fold_TS, fold_Y, fold_ok = sem("fold_T"), sem("fold_TS"), sem("fold_Y"), sem("fold_ok")
            high1 = [fa.take(KC, H) for _ in range(2)]
            rest1 = [fa.take(KC, H) for _ in range(2)]
            rest2 = [fa.take(HH, C) for _ in range(4)]
            high1_ok, rest1_ok, ew1_ok, rest2_ok = sem("high1"), sem("rest1"), sem("ew1"), sem("rest2")
            st_high = sem("high2_stored")
            st1 = [sem(f"low1_stored{k}") for k in range(2)]
            st2 = [sem(f"low2_stored{k}") for k in range(4)]
            half = lambda n: (n // 2, slice(n % 2 * HH, (n % 2 + 1) * HH))
            FY = (3, 7)
            assert 2 * E == 2 * NG

            with nc.Block() as block:
                @block.sync
                def _(sp):
                    for n in range(2 * E):
                        if n % 2 == 0:
                            e = n // 2
                            sp.wait_ge(rest1_ok, KC * (e + 1))
                            sp.dma_start(low1[e], rest1[e % 2].rearrange("p c h -> p (c h)")).then_inc(st1[e % 2], 16)
                        sp.wait_ge(rest2_ok, n + 1)
                        sp.dma_start(low2[n // 2][:, n % 2 * HH * C:(n % 2 + 1) * HH * C], rest2[n % 4].rearrange("p h c -> p (h c)")
                                     ).then_inc(st2[n % 4], 16)
                        if n % 2:
                            sp.dma_start(high2[n // 2].rearrange("p (h c) -> p h c", h=HC), ew2[:, :, n // 2, :]).then_inc(st_high, 16)
                    sp.wait_ge(st_high, 16 * E)
                    for k in range(2):
                        sp.wait_ge(st1[k], 16 * E // 2)
                    for k in range(4):
                        sp.wait_ge(st2[k], 16 * 2 * E // 4)

                @block.gpsimd
                def _(pool):
                    pool.memset(work[HD:HD + 1, 0:T], 1.0).then_inc(ones_ok, 1)
                    pool.wait_ge(ones_ok, 1)
                    for g in range(NG):
                        nrm.roots(pool, g)

                @block.vector
                def _(v):
                    def rest_first(e):
                        v.wait_ge(high1_ok, KC * (e + 1))
                        after(v, st1[e % 2], 16 * (e // 2))
                        for c in range(KC):
                            v.scalar_tensor_tensor(rest1[e % 2][:, c], ew1[:, c, e, :], gam[:, c:c + 1], high1[e % 2][:, c],
                                                   ALU.mult, ALU.subtract).then_inc(rest1_ok, 1)

                    def rest_second(n):
                        e, hs = half(n)
                        v.wait_ge(fold_ok, n + 1)
                        after(v, st2[n % 4], 16 * (n // 4))
                        v.tensor_tensor(rest2[n % 4], bank[:, FY[n % 2], :].rearrange("p (h c) -> p h c", h=HH), ew2[:, hs, e, :],
                                        ALU.subtract).then_inc(rest2_ok, 1)

                    def normalise(g):
                        u = g % 2
                        nrm.statistics(v, g, xs[:, g * GT:(g + 1) * GT, :])
                        v.wait_ge(nrm.root_ok, g + 1)
                        v.scalar_tensor_tensor(nb[u], nrm.sum[u], -0.5, nrm.root[u][:, 0, :], ALU.mult, ALU.mult
                                               ).then_inc(nb_ok, 1)
                        v.wait_ge(nb_ok, g + 1)
                        after(v, lnT_ps, g - 1)
                        for t in range(GT):
                            v.tensor_scalar(ln[u][:, t, :], xs[:, g * GT + t, :], nrm.root[u][:, 0, t:t + 1],
                                            nb[u][:, t:t + 1], ALU.mult, ALU.add).then_inc(ln_ok, 1)

                    v.wait_ge(x_in, 16 * 8)
                    normalise(0)
                    for g in range(NG + 1):
                        if g >= 1:
                            rest_second(2 * g - 2)
                        if g + 1 < NG:
                            normalise(g + 1)
                        if g >= 1:
                            h, u = g - 1, (g - 1) % 2
                            kps = bank[:, 4, :].rearrange("p (t x) -> p t x", t=GT)[:, :, 0:HD].rearrange(
                                "p t (h e) -> p t h e", h=HEADS)
                            k4 = ks[u].rearrange("p (t h) e -> p t h e", t=GT)
                            v.wait_ge(kvq_ps, h + 1)
                            v.tensor_reduce(kmax.rearrange("p (t h) -> p t h", t=GT), kps, AX.X, ALU.max).then_inc(kmax_ok, 1)
                            v.wait_ge(kmax_ok, h + 1)
                            after(v, ctx_ps, h - 1)
                            v.tensor_tensor(k4, kps, cols(kmax.rearrange("p (t h) -> p t h", t=GT), DH), ALU.subtract
                                            ).then_inc(ksh_ok, 1)
                            v.wait_ge(kexp_ok, h + 1)
                            v.tensor_reduce(ksum, ks[u], AX.X, ALU.add).then_inc(ksum_ok, 1)
                            v.wait_ge(ksum_ok, 2 * h + 1)
                            v.reciprocal(ksum, ksum).then_inc(ksum_ok, 1)
                            v.wait_ge(ksum_ok, 2 * h + 2)
                            v.tensor_tensor(ks[u], ks[u], cols(ksum, DH), ALU.mult).then_inc(k_ok, 1)
                            rest_second(2 * g - 1)
                            rest_first(g - 1)
                    v.wait_ge(ctx_ps, NG)
                    for b in range(B):
                        v.tensor_tensor(cm[b], bank[0:HD, 6, b * HD:(b + 1) * HD], hmask[:], ALU.mult).then_inc(cm_ok, 1)

                @block.scalar
                def _(act):
                    def turn(n):
                        act.wait_ge(fold_T, n + 1)
                        after(act, fold_Y, n - 1)
                        copy(act, ew2T[n % 2].rearrange("p c h -> p (c h)"), bank[:, 2, :]).then_inc(fold_TS, 1)

                    def high_first(e, o, signal):
                        for c in range(KC):
                            act.activation(f32r(o[:, c]), ew1[:, c, e, :], ACT.Copy, scale=gam[:, c:c + 1]).then_inc(signal, 1)

                    def folded(n):
                        e, hs = half(n)
                        act.wait_ge(fold_Y, n + 1)
                        copy(act, f32r(ew2[:, hs, e, :]), bank[:, FY[n % 2], :].rearrange("p (h c) -> p h c", h=HH)).then_inc(fold_ok, 1)

                    for g in range(NG + 1):
                        if g < NG:
                            u = g % 2
                            act.wait_ge(lnT_ps, g + 1)
                            after(act, kvq_ps, g - 1)
                            copy(act, lnT[u].rearrange("p c n -> p (c n)"), psum(0, 2)).then_inc(lnT_ok, 1)
                            turn(2 * g)
                            after(act, rest1_ok, KC * (g - 1))
                            high_first(g, high1[g % 2], high1_ok)
                        if g >= 1:
                            folded(2 * g - 1)

                        if g >= 1:
                            h, u = g - 1, (g - 1) % 2
                            act.wait_ge(kvq_ps, h + 1)
                            after(act, ctx_ps, h - 1)
                            copy(act, qT[0:HD, h * BANK:(h + 1) * BANK], bank[0:HD, 5, :]).then_inc(vq_ok, 1)
                            act.wait_ge(ksh_ok, h + 1)
                            copy(act, vs[u], bank[:, 4, :].rearrange("p (t x) -> p t x", t=GT)[:, :, HD:2 * HD]).then_inc(vq_ok, 1)
                            act.activation(ks[u], ks[u], ACT.Exp).then_inc(kexp_ok, 1)
                        if g < NG:
                            folded(2 * g)
                            turn(2 * g + 1)
                        if g >= 1:
                            act.wait_ge(rest1_ok, KC * g)
                            high_first(g - 1, ew1[:, :, g - 1, :], ew1_ok)
                    for b in range(B):
                        act.wait_ge(m_ps, b + 1)
                        copy(act, ctxm[0:HD, b, :], bank[0:HD, b, 0:C], HD ** -0.5).then_inc(m_ok, 1)

                @block.tensor
                def _(pe):
                    def turn(n):
                        e, hs = half(n)
                        after(pe, fold_TS, n)
                        for c in range(KC):
                            for h in range(HH):
                                last = pe.transpose(bank[:, 2, (c * HH + h) * P:(c * HH + h + 1) * P],
                                                    ew2[:, hs.start + h, e, c * P:(c + 1) * P], ident[:])
                        last.then_inc(fold_T, 1)

                    def fold(n):
                        pe.wait_ge(fold_TS, n + 1)
                        after(pe, rest2_ok, n - 1)
                        for h in range(HH):
                            for c in range(KC):
                                last = pe.matmul(bank[:, FY[n % 2], h * C:(h + 1) * C], ew2T[n % 2][:, c, h * P:(h + 1) * P],
                                                 R[:, c, :], start=(c == 0), stop=(c == KC - 1))
                        last.then_inc(fold_Y, 1)

                    for g in range(NG + 2):
                        if g < NG:
                            u = g % 2
                            pe.wait_ge(ln_ok, GT * (g + 1))
                            after(pe, lnT_ok, g)
                            for c in range(KC):
                                for t in range(GT):
                                    last = pe.transpose(bank[:, c, t * P:(t + 1) * P], ln[u][:, t, c * P:(c + 1) * P],
                                                        ident[:])
                            last.then_inc(lnT_ps, 1)
                            turn(2 * g)
                        if 1 <= g <= NG:
                            h, u = g - 1, (g - 1) % 2
                            pe.wait_ge(lnT_ok, h + 1)
                            after(pe, ksh_ok, h)
                            after(pe, vq_ok, 2 * h)
                            for t in range(GT):
                                for c in range(KC):
                                    pe.matmul(bank[:, 4, t * 2 * HD:(t + 1) * 2 * HD], lnT[u][:, c, t * P:(t + 1) * P],
                                              wqkv[:, c, HD:3 * HD], start=(c == 0), stop=(c == KC - 1))
                            for c in range(KC):
                                last = pe.matmul(bank[0:HD, 5, :], wqkv[:, c, 0:HD], lnT[u][:, c, :],
                                                 start=(c == 0), stop=(c == KC - 1))
                            last.then_inc(kvq_ps, 1)
                        if g < NG:
                            fold(2 * g)
                            turn(2 * g + 1)
                        if g >= 2:
                            h, u = g - 2, (g - 2) % 2
                            b = h // GB
                            pe.wait_ge(k_ok, h + 1)
                            pe.wait_ge(vq_ok, 2 * (h + 1))
                            for t in range(GT):
                                last = pe.matmul(bank[0:HD, 6, b * HD:(b + 1) * HD], vs[u][:, t, :],
                                                 ks[u].rearrange("p (t h) e -> p t (h e)", t=GT)[:, t, :],
                                                 start=(h % GB == 0 and t == 0), stop=(h % GB == GB - 1 and t == GT - 1), skip_group_check=True)
                            last.then_inc(ctx_ps, 1)
                        if g < NG:
                            fold(2 * g + 1)
                    for b in range(B):
                        pe.wait_ge(cm_ok, b + 1)
                        pe.matmul(bank[0:HD, b, 0:C], cm[b], wout[:], start=True, stop=True).then_inc(m_ps, 1)

        def mixture(r):
            a = Arena(work[:, T:WORK - ROUTE])
            xT = [a.take(KC, BANK) for _ in range(2)]
            nrm = Norm(f"f{r}", a, 4)
            nb = [a.take(2, GT) for _ in range(2)]
            c1 = [a.take(GT) for _ in range(2)]
            m1, m2, i1 = (a.take(GT) for _ in range(3))
            posf = a.take(2, GT)
            i2 = posf[:, 0]
            mine = a.take(2, GT, E)
            eq, cand = mine[:, 0], mine[:, 1]
            cnt = [a.take(GT, E, dt=BF16) for _ in range(2)]
            run = [a.take(E, dt=BF16) for _ in range(2)]
            lg = [a.take(GT, E) for _ in range(2)]
            rt = Arena(work[:, 0:T])
            prod = rt.take(C, dt=BF16)
            ones, total = rt.take(NT), rt.take(E)
            done = rt.take(E, dt=I32)
            ntile, tincl, ends = rt.take(E), rt.take(E), rt.take(E)
            cmpn, cmpt, weight = rt.take(E, NT), rt.take(SLOTS, E - 1), rt.take(SLOTS, E - 1)
            tf, row, used = rt.take(SLOTS), rt.take(SLOTS), rt.take(SLOTS)
            z, gate, shut = ([rt.take(GT) for _ in range(2)] for _ in range(3))
            zz, gw2 = ([rt.take(GT, 2) for _ in range(2)] for _ in range(2))
            RING = 4
            x = Arena(flat(xh))
            x.take(2 * 2 * (KC + HC) * P)
            xr = [x.take(CW) for _ in range(RING)]
            xrT = [rows[:, u, :, 0:KC * P] for u in range(2)]
            hid = [x.take(H) for _ in range(2)]
            hidT = [rows[:, u, :, KC * P:] for u in range(2)]
            yr = [x.take(CW) for _ in range(RING)]
            junk = x.take(C)
            back = [x.take(1, dt=I32) for _ in range(RING)]
            cb = Arena(flat(xh))
            res = [cb.take(GT, 2 * CW).rearrange("p t (k c) -> p t k c", k=2) for _ in range(RING)]
            s = lambda name: sem(f"m{r}_" + name)
            if r == 0:
                att_ps, x1_ok = s("att_ps"), s("x1")
            nb_ok, xh_ok, res_ok = s("nb"), s("xh"), s("res")
            xT_ps, xT_ok, ab_ps, gelu_ok, lg_ok = s("xT_ps"), s("xT"), s("dense_ps"), s("gelu"), s("logits")
            dve, cnt_ok, rank_ps, pos_ok, slot_ok, rows_ok = (s("order"), s("cnt"), s("rank_ps"), s("pos"), s("slot"), s("rows"))
            run_ok, d_ok, ed_ok, tot_ps = s("run"), s("d"), s("ed"), s("tot_ps")
            zab_ok = s("zab")
            lg_ps = s("logits_ps")
            tails_ok, padded, texp_ok, scat = s("tails"), s("padded"), s("texp"), s("scattered")
            x_ld = [s(f"x_loaded{k}") for k in range(RING)]
            y_st, back_ok, zy_ok = s("y_scattered"), s("back"), s("zy")
            xrT_ps, xhigh_ok, xrT_ok, up_ps, hid_ok = s("xrT_ps"), s("xhigh"), s("xrT"), s("up_ps"), s("hid")
            low_ld = s("weights_loaded")
            WEIGHTS = 48 if r == 1 else 32
            spilled = [s(f"spilled{k}") for k in range(4)]
            BACK = 32 * NG // 4
            hidT_ps, hhigh_ok, hidT_ok, dn_ps, y_ok = s("hidT_ps"), s("hhigh"), s("hidT"), s("down_ps"), s("y")
            y_ld = [s(f"results_loaded{k}") for k in range(RING)]
            z_ok, ez_ok, gate_ok, y2_ok, xab_ok, y1_ok, x2_ok, o_st = (
                s("z"), s("ez"), s("gate"), s("y2"), s("xab"), s("y1"), s("x2"), s("stored"))
            sab_ok = s("shut_dense")
            FIRST = 2 * RING - 1
            TURNS = (SLOTS - 1 - FIRST) // RING
            HALF = GT // 2
            assert GT == 4
            TAIL = FIRST + TURNS * RING
            ranks = bank[:, 7, 0:GT * E].rearrange("p (t e) -> p t e", t=GT)
            logits = bank[:, 6, 0:GT * E].rearrange("p (t e) -> p t e", t=GT)
            tiles = lambda g: slice(g * GT, (g + 1) * GT)

            def over_tiles(eng, step=None, run=None):
                run = run or (lambda tiles: [step(*t) for t in tiles])
                run([(j, j % RING, j // RING) for j in range(FIRST)])
                with eng.Fori(0, TURNS) as i:
                    run([(i * RING + k, k % RING, i + k // RING) for k in range(FIRST, FIRST + RING)])
                run([(j, j % RING, j // RING) for j in range(TAIL, SLOTS)])

            def is_last(j):
                return isinstance(j, int) and j == SLOTS - 1

            with nc.Block() as block:
                @block.vector
                def _(v):
                    n = 0

                    def then(ins):
                        nonlocal n
                        n += 1
                        ins.then_inc(dve, 1)
                        v.wait_ge(dve, n)

                    def statistics(g):
                        if r == 0:
                            v.wait_ge(att_ps, g + 1)
                            for h in range(2):
                                x2 = xs[:, g * GT + 2 * h:g * GT + 2 * h + 2, :].rearrange("p t c -> p (t c)")
                                v.tensor_tensor(x2, x2, bank[:, h, :], ALU.add).then_inc(x1_ok, 1)
                            v.wait_ge(x1_ok, 2 * (g + 1))
                        nrm.statistics(v, g, xs[:, tiles(g), :])

                    def normalise(g):
                        u, q = g % 2, g % nrm.ring
                        v.wait_ge(nrm.root_ok, g + 1 if g < 4 else 3 + g // 2)
                        after(v, res_ok, GT * (g - 1))
                        for k in range(2):
                            v.scalar_tensor_tensor(nb[u][:, k, :], nrm.sum[q], -0.5, nrm.root[q][:, k, :], ALU.mult, ALU.mult
                                                   ).then_inc(nb_ok, 1)
                        v.tensor_scalar(c1[u], nrm.root[q][:, 0, :], 1.0, None, ALU.add).then_inc(nb_ok, 1)
                        v.wait_ge(nb_ok, 3 * (g + 1))
                        for t in range(GT):
                            v.tensor_scalar(xh[:, g * GT + t, 0:C], xs[:, g * GT + t, :], nrm.root[q][:, 1, t:t + 1],
                                            nb[u][:, 1, t:t + 1], ALU.mult, ALU.add).then_inc(xh_ok, 1)

                    eb = eidx[:].unsqueeze(1).to_broadcast([P, GT, E])

                    def best(src, m, i, onehot):
                        then(v.tensor_reduce(m, src, AX.X, ALU.max))
                        then(v.tensor_tensor(eq, src, cols(m, E), ALU.is_ge))
                        then(v.tensor_tensor(cand, eq, eb, ALU.mult))
                        then(v.tensor_reduce(i, cand, AX.X, ALU.min))
                        then(v.tensor_tensor(onehot, eb, cols(i, E), ALU.is_equal))

                    def choose(g):
                        found = lg[g % 2]
                        oh1, oh2 = oh[:, 0, tiles(g), :], oh[:, 1, tiles(g), :]
                        v.wait_ge(lg_ok, g + 1)
                        best(found, m1, i1, oh1)
                        v.tensor_copy(xh[:, tiles(g), C], token[:, tiles(g)]).then_inc(rows_ok, 1)
                        v.tensor_scalar(xh[:, tiles(g), C + 1], i1, float(E), None, ALU.add).then_inc(rows_ok, 1)
                        then(v.scalar_tensor_tensor(found, oh1, LOWEST, found, ALU.mult, ALU.add))
                        best(found, m2, i2, oh2)
                        v.tensor_tensor(cnt[g % 2], oh1, oh2, ALU.add).then_inc(cnt_ok, 1)
                        v.tensor_tensor(dtop[:, tiles(g)], m2, m1, ALU.subtract).then_inc(d_ok, 1)
                        v.wait_ge(cnt_ok, g + 1)
                        csum = found[:, 0]
                        then(v.tensor_reduce(csum, cnt[g % 2].rearrange("p t e -> p e t"), AX.X, ALU.add))
                        v.tensor_tensor(run[(g + 1) % 2], run[g % 2], csum, ALU.add).then_inc(run_ok, 1)
                        v.wait_ge(run_ok, g + 1)

                    def locate(g):
                        v.wait_ge(rank_ps, g + 1)
                        pos = lg[g % 2]
                        v.tensor_tensor(pos, ranks,
                                        ebase[:].unsqueeze(1).to_broadcast([P, GT, E]), ALU.add).then_inc(pos_ok, 1)
                        v.wait_ge(pos_ok, g + 1)
                        then(v.tensor_tensor(mine, oh[:, :, tiles(g), :], pos.unsqueeze(1).to_broadcast([P, 2, GT, E]), ALU.mult))
                        then(v.tensor_reduce(posf, mine, AX.X, ALU.add))
                        v.tensor_copy(slot[:, :, tiles(g)], posf).then_inc(slot_ok, 1)

                    def dense_gate(g):
                        v.wait_ge(gelu_ok, g + 1)
                        for t in range(g * GT, (g + 1) * GT):
                            after(v, zab_ok, t)
                            v.scalar_tensor_tensor(prod, ab[:, t, :], 1.0, gcw[:, 1, :], ALU.mult, ALU.mult,
                                                   accum_out=zab[:, t:t + 1]).then_inc(zab_ok, 1)

                    LATE = {NG // 2: (0,), NG // 2 + 1: (1,), NG // 2 + 2: (2, 3)}
                    assert NG == 8
                    then(v.memset(run[0], 0.0))
                    statistics(0)
                    statistics(1)
                    normalise(0)
                    statistics(2)
                    normalise(1)
                    statistics(3)
                    for g in range(NG):
                        choose(g)
                        if g == 0:
                            locate(g)
                        if g + 2 < NG:
                            normalise(g + 2)
                        if g + 4 < NG:
                            statistics(g + 4)
                        if g >= 1:
                            locate(g)
                        for h in LATE.get(g, ()):
                            dense_gate(h)

                    v.wait_ge(tot_ps, 1)
                    then(v.tensor_copy(total, bank[:, 6, 0:E]))
                    then(v.tensor_tensor(ends, total, ebase[:], ALU.add))
                    v.tensor_copy(tails, ends).then_inc(tails_ok, 1)
                    then(v.memset(ones, 1.0))
                    then(v.tensor_tensor(cmpn, cols(total, NT), steps[:].unsqueeze(1).to_broadcast([P, E, NT]), ALU.is_gt))
                    then(v.tensor_reduce(ntile, cmpn, AX.X, ALU.add))
                    then(v.tensor_tensor_scan(tincl, ones[:, 0:E], ntile, 0.0, ALU.mult, ALU.add))
                    sx = cols(sidx[:], E - 1)
                    then(v.tensor_tensor(cmpt, sx, tincl[:, 0:E - 1].unsqueeze(1).to_broadcast([P, SLOTS, E - 1]), ALU.is_ge))
                    then(v.tensor_reduce(texpf, cmpt, AX.X, ALU.add))
                    v.tensor_copy(texp, texpf).then_inc(texp_ok, 1)
                    then(v.tensor_tensor(weight, cmpt, ntile[:, 0:E - 1].unsqueeze(1).to_broadcast([P, SLOTS, E - 1]), ALU.mult))
                    then(v.tensor_reduce(row, weight, AX.X, ALU.add))
                    then(v.tensor_tensor(row, sidx[:], row, ALU.subtract))
                    then(v.tensor_scalar(tf, texpf, float(REGION), float(-E * REGION), ALU.mult, ALU.add))
                    then(v.scalar_tensor_tensor(row, row, float(P), tf, ALU.mult, ALU.add))
                    then(v.tensor_scalar(used, sidx[:], tincl[:, E - 1:E], None, ALU.is_lt))
                    then(v.tensor_tensor(row, row, used, ALU.mult))
                    then(v.tensor_scalar(row, row, float(E * REGION), None, ALU.add))
                    v.tensor_copy(trow, row).then_inc(texp_ok, 1)
                    v.tensor_scalar(done, tincl, 1.0, None, ALU.max).then_inc(texp_ok, 1)
                    v.wait_ge(ed_ok, 1)
                    then(v.tensor_scalar(wts[:, :, 0], dtop, 1.0, None, ALU.add))
                    then(v.reciprocal(wts[:, :, 0], wts[:, :, 0]))
                    then(v.tensor_tensor(wts[:, :, 1], dtop, wts[:, :, 0], ALU.mult))
                    for g in range(NG // 2, NG):
                        dense_gate(g)
                    v.wait_ge(zab_ok, NT)

                    def copy_x(j, k, turn):
                        v.wait_ge(xhigh_ok, j + 1)
                        after(v, up_ps, j - 1)
                        q = xrT[k % 2]
                        v.tensor_tensor(f32r(q[:, 1]), bank[:, k % 2, 0:C], q[:, 0], ALU.subtract).then_inc(xrT_ok, 1)

                    def route_back(j, k):
                        b = k % RING
                        after(v, y_st, 16 * (j - RING + 1))
                        e = texpf[:, j:j + 1] if isinstance(j, int) else texpf[:, bass.ds(j, 1)]
                        v.scalar_tensor_tensor(back[b], xr[b][:, C + 1:], e, xr[b][:, C:C + 1], ALU.not_equal, ALU.add
                                               ).then_inc(back_ok, 1)

                    def gate_part(j, k):
                        v.wait_ge(y_ok, j + 1)
                        after(v, zy_ok, j)
                        y = yr[k % RING]
                        v.scalar_tensor_tensor(junk, y[:, 0:C], 1.0, gcw[:, 0, :], ALU.mult, ALU.mult,
                                               accum_out=y[:, C:C + 1]).then_inc(zy_ok, 1)

                    def step(j, k, turn):
                        if not is_last(j):
                            copy_x(j + 1, k + 1, turn)
                        v.wait_ge(hhigh_ok, j + 1)
                        after(v, dn_ps, j - 1)
                        q = hidT[k % 2]
                        v.tensor_tensor(f32r(q[:, 1]), bank[:, 4 + k % 2, :], q[:, 0], ALU.subtract).then_inc(hidT_ok, 1)
                        if not isinstance(j, int) or j >= 1:
                            gate_part(j - 1, k - 1)
                        if not is_last(j):
                            route_back(j + 1, k + 1)

                    copy_x(0, 0, 0)
                    route_back(0, 0)
                    over_tiles(v, step)
                    gate_part(SLOTS - 1, SLOTS - 1)


                    def small(ins):
                        nonlocal n
                        n += 1
                        ins.then_inc(dve, 1)

                    def results(g, t):
                        if 0 <= g < NG:
                            q, i = res[g % RING], g * GT + t
                            v.wait_ge(y2_ok, i + 1)
                            v.scalar_tensor_tensor(q[:, t, 0, 0:C], q[:, t, 0, 0:C], gw2[g % 2][:, t, 0:1], q[:, t, 1, 0:C],
                                                   ALU.mult, ALU.add).then_inc(y1_ok, 1)

                    def whole(g, h):
                        if g >= 0:
                            v.wait_ge(xab_ok, 2 * g + h + 1)
                            v.wait_ge(y1_ok, GT * g + HALF * (h + 1))
                            o = xs[:, g * GT + h * HALF:g * GT + (h + 1) * HALF, :]
                            v.tensor_tensor(o, o, res[g % RING][:, h * HALF:(h + 1) * HALF, 0, 0:C], ALU.add).then_inc(x2_ok, 1)

                    for g in range(NG + 2):
                        u = g % 2
                        if g < NG:
                            v.wait_ge(y_ld[g % RING], 16 * (g // RING + 1))
                            v.wait_ge(spilled[g % 4], BACK + 32 * (g // 4 + 1))
                            then(v.tensor_tensor(zz[u], res[g % RING][:, :, :, C], wts[:, tiles(g), :], ALU.mult))
                            small(v.tensor_reduce(z[u], zz[u], AX.X, ALU.add))
                            results(g - 1, 0)
                            v.wait_ge(dve, n)
                            small(v.scalar_tensor_tensor(z[u], z[u], gcb[:], zab[:, tiles(g)], ALU.add, ALU.add))
                            results(g - 1, 1)
                            v.wait_ge(dve, n)
                            v.tensor_scalar(z[u], z[u], -87.0, None, ALU.max).then_inc(z_ok, 1)
                            results(g - 1, 2)
                            results(g - 1, 3)
                            v.wait_ge(ez_ok, g + 1)
                            small(v.tensor_scalar(gate[u], z[u], 1.0, None, ALU.add))
                            whole(g - 2, 0)
                            v.wait_ge(dve, n)
                            small(v.reciprocal(gate[u], gate[u]))
                            whole(g - 2, 1)
                            v.wait_ge(dve, n)
                            after(v, sab_ok, GT * (g - 1))
                            v.tensor_tensor(gw2[u], wts[:, tiles(g), :], cols(gate[u], 2), ALU.mult).then_inc(gate_ok, 1)
                            v.tensor_tensor(shut[u], z[u], gate[u], ALU.mult).then_inc(gate_ok, 1)
                            v.wait_ge(gate_ok, 2 * (g + 1))
                        else:
                            for t in range(GT):
                                results(g - 1, t)
                            for h in range(2):
                                whole(g - 2, h)

                @block.gpsimd
                def _(pool):
                    for g in range(4):
                        nrm.roots(pool, g)
                    for h in range(NG):
                        if h % 2 == 1 and h + 3 < NG:
                            nrm.roots(pool, h + 3, 2)
                        pool.wait_ge(rows_ok, 2 * (h + 1))
                        pool.wait_ge(slot_ok, h + 1)
                        for t in range(h * GT, (h + 1) * GT):
                            for k in range(2):
                                pool.indirect_dma_start(out=xg, out_offset=bass.IndirectOffsetOnAxis(ap=slot[:, k, t:t + 1], axis=0),
                                                        in_=xh[:, t, :], in_offset=None).then_inc(scat, 16)
                    pool.wait_ge(texp_ok, 2)
                    pool.wait_ge(padded, 16 * E)
                    pool.wait_ge(scat, 16 * 2 * NT)

                    def fetch(j):
                        at = pool.value_load(trow[0:1, j:j + 1], min_val=0, max_val=E * REGION)
                        pool.dma_start(xr[j % RING], xg[bass.ds(at, P), :]).then_inc(x_ld[j % RING], 16)

                    for j in range(RING):
                        fetch(j)
                    for j in range(SLOTS):
                        if j + RING < SLOTS:
                            pool.wait_ge(back_ok, j + 1)
                            fetch(j + RING)
                        pool.wait_ge(zy_ok, j + 1)
                        pool.wait_ge(back_ok, j + 1)
                        after(pool, y_st, 16 * j)
                        pool.indirect_dma_start(out=yg, out_offset=bass.IndirectOffsetOnAxis(ap=back[j % RING], axis=0),
                                                in_=yr[j % RING], in_offset=None).then_inc(y_st, 16)
                    for g in range(NG):
                        for h in range(2):
                            pool.wait_ge(sab_ok, GT * g + HALF * (h + 1))
                            i = slice(g * GT + h * HALF, g * GT + (h + 1) * HALF)
                            pool.tensor_tensor(xs[:, i, :], xs[:, i, :], ab[:, i, :], ALU.add).then_inc(xab_ok, 1)

                @block.sync
                def _(sp):
                    def spill(g):
                        sp.wait_ge(res_ok, GT * (g + 1))
                        sp.dma_start(xs_out[g], xs[:, tiles(g), :].rearrange("p t c -> p (t c)")).then_inc(spilled[g % 4], 16)
                        sp.wait_ge(gelu_ok, g + 1)
                        sp.dma_start(ab_out[g], ab[:, tiles(g), :].rearrange("p t c -> p (t c)")).then_inc(spilled[g % 4], 16)

                    def fetch_weights(e):
                        after(sp, low_ld, WEIGHTS * e)
                        sp.wait_ge(spilled[e % 4], 32 * (e // 4 + 1))
                        sp.wait_ge(zab_ok, GT * (e + 1))
                        sp.dma_start(low1_in[:, e].rearrange("p c h -> p (c h)"), low1[e]).then_inc(low_ld, 16)
                        sp.dma_start(low2_in[:, e].rearrange("p h c -> p (h c)"), low2[e]).then_inc(low_ld, 16)
                        if r == 1:
                            sp.dma_start(ew2[:, :, e, :], high2[e].rearrange("p (h c) -> p h c", h=HC)).then_inc(low_ld, 16)

                    assert E == NG
                    EARLY = 2
                    for g in range(NG):
                        spill(g)
                        if 0 <= g - 3 < EARLY:
                            fetch_weights(g - 3)
                    sp.wait_ge(tails_ok, 1)
                    for e in range(E):
                        at = sp.value_load(tails[0:1, e:e + 1], min_val=e * REGION, max_val=e * REGION + T)
                        sp.dma_start(xg[bass.ds(at, P), :], zero[:]).then_inc(padded, 16)
                    sp.wait_ge(x_ld[RING - 1], 16)
                    for e in range(EARLY, E):
                        fetch_weights(e)
                    sp.wait_ge(texp_ok, 3)
                    for g in range(NG):
                        if g < E - 1:
                            sp.wait_ge(dn_ps, sp.value_load(done[0:1, g:g + 1], min_val=1, max_val=SLOTS))
                        else:
                            sp.wait_ge(dn_ps, SLOTS)
                        sp.wait_ge(spilled[g % 4], BACK + 32 * (g // 4))
                        for o, i in ((xs, xs_out), (ab, ab_out)):
                            sp.dma_start(o[:, tiles(g), :].rearrange("p t c -> p (t c)"), i[g]).then_inc(spilled[g % 4], 16)
                    sp.wait_ge(y_st, 16 * SLOTS)
                    y = yg[0:2 * T, :].rearrange("(t p k) c -> p t (k c)", p=P, k=2)
                    for g in range(NG):
                        after(sp, x2_ok, 2 * (g - RING + 1))
                        sp.dma_start(res[g % RING].rearrange("p t k c -> p t (k c)"), y[:, tiles(g), :]).then_inc(y_ld[g % RING], 16)
                    if r == 1:
                        o = out.rearrange("b (n p) c -> p (b n) c", p=P)
                        for g in range(NG):
                            sp.wait_ge(x2_ok, 2 * (g + 1))
                            sp.dma_start(o[:, tiles(g), :], xs[:, tiles(g), :]).then_inc(o_st, 16)
                        sp.wait_ge(o_st, 16 * NG)

                @block.scalar
                def _(act):
                    for g in range(NG + 1):
                        if g < NG:
                            act.wait_ge(xT_ps, g + 1)
                            after(act, ab_ps, g - 1)
                            copy(act, xT[g % 2].rearrange("p c n -> p (c n)"), psum(2, 2)).then_inc(xT_ok, 1)
                            act.wait_ge(xh_ok, GT * (g + 1))
                            for t in range(GT):
                                act.activation(xs[:, g * GT + t, :], xs[:, g * GT + t, :], ACT.Identity, scale=c1[g % 2][:, t:t + 1],
                                               bias=nb[g % 2][:, 0, t:t + 1]).then_inc(res_ok, 1)
                            act.wait_ge(lg_ps, g + 1)
                            after(act, slot_ok, g - 1)
                            copy(act, lg[g % 2], logits).then_inc(lg_ok, 1)
                        if g >= 1:
                            act.wait_ge(ab_ps, g)
                            act.activation(ab[:, tiles(g - 1), :].rearrange("p t c -> p (t c)"), psum(4, 2), ACT.Gelu
                                           ).then_inc(gelu_ok, 1)
                    act.wait_ge(d_ok, NG)
                    act.activation(dtop, dtop, ACT.Exp).then_inc(ed_ok, 1)

                    def copy_y(j, k, turn):
                        act.wait_ge(dn_ps, j + 1)
                        after(act, y_st, 16 * (j - RING + 1))
                        copy(act, yr[k % RING][:, 0:C], bank[:, 6 + k % 2, 0:C]).then_inc(y_ok, 1)

                    def high_x(j, k):
                        act.wait_ge(xrT_ps, j + 1)
                        after(act, up_ps, j - 1)
                        copy(act, f32r(xrT[k % 2][:, 0]), bank[:, k % 2, 0:C]).then_inc(xhigh_ok, 1)

                    def step(j, k, turn):
                        act.wait_ge(up_ps, j + 1)
                        after(act, hidT_ps, j - 1)
                        act.activation(hid[k % 2], bank[:, 2 + k % 2, :], ACT.Gelu).then_inc(hid_ok, 1)
                        if not is_last(j):
                            high_x(j + 1, k + 1)
                        if not isinstance(j, int) or j >= 1:
                            copy_y(j - 1, (k - 1) % RING, turn if k >= 1 else turn - 1)
                        act.wait_ge(hidT_ps, j + 1)
                        after(act, dn_ps, j - 1)
                        copy(act, f32r(hidT[k % 2][:, 0]), bank[:, 4 + k % 2, :]).then_inc(hhigh_ok, 1)

                    high_x(0, 0)
                    over_tiles(act, step)
                    copy_y(SLOTS - 1, (SLOTS - 1) % RING, (SLOTS - 1) // RING)
                    for g in range(NG + 1):
                        h = g - 1
                        if g >= 1:
                            act.wait_ge(gate_ok, 2 * (h + 1))
                            for t in range(GT):
                                copy(act, res[h % RING][:, t, 1, 0:C], res[h % RING][:, t, 1, 0:C], gw2[h % 2][:, t, 1:2]).then_inc(y2_ok, 1)
                        if g < NG:
                            act.wait_ge(z_ok, g + 1)
                            act.activation(z[g % 2], z[g % 2], ACT.Exp, scale=-1.0).then_inc(ez_ok, 1)
                        if g >= 1:
                            for t in range(GT):
                                i = h * GT + t
                                copy(act, ab[:, i, :], ab[:, i, :], shut[h % 2][:, t:t + 1]).then_inc(sab_ok, 1)

                @block.tensor
                def _(pe):
                    def attend(g):
                        after(pe, x1_ok, 2 * g)
                        for t in range(GT):
                            last = pe.matmul(bank[:, t // 2, (t % 2) * C:(t % 2 + 1) * C],
                                             qT[:, (g * GT + t) * P:(g * GT + t + 1) * P], ctxm[:, g * B // NG, :],
                                             start=True, stop=True)
                        last.then_inc(att_ps, 1)

                    def turn(g):
                        pe.wait_ge(xh_ok, GT * (g + 1))
                        after(pe, xT_ok, g)
                        for c in range(KC):
                            for t in range(GT):
                                last = pe.transpose(bank[:, 2 + c, t * P:(t + 1) * P], xh[:, g * GT + t, c * P:(c + 1) * P], ident[:])
                        last.then_inc(xT_ps, 1)

                    def times(o, g, t, some):
                        for c in range(KC):
                            pe.matmul(o, xT[g % 2][:, c, t * P:(t + 1) * P], abw[:, c, some], start=(c == 0), stop=False)
                        return pe.matmul(o, onesb[0:2 * QROW + 1, :], abbp[:, some], start=False, stop=True)

                    def route(g):
                        pe.wait_ge(xT_ok, g + 1)
                        after(pe, lg_ok, g)
                        for t in range(GT):
                            last = times(logits[:, t, :], g, t, slice(C, C + E))
                        last.then_inc(lg_ps, 1)

                    def dense(g):
                        after(pe, gelu_ok, g)
                        for t in range(GT):
                            last = times(bank[:, 4 + t // 2, t % 2 * C:(t % 2 + 1) * C], g, t, slice(0, C))
                        last.then_inc(ab_ps, 1)

                    def rank(g):
                        pe.wait_ge(cnt_ok, g + 1)
                        after(pe, run_ok, g)
                        after(pe, pos_ok, g)
                        o = ranks
                        pe.matmul(o, tri[:], cnt[g % 2], start=True, stop=False, skip_group_check=True)
                        pe.matmul(o, onesb[:], run[g % 2].unsqueeze(1).to_broadcast([P, GT, E]), start=False, stop=False,
                                  skip_group_check=True)
                        for t in range(GT - 1):
                            m = GT - 1 - t
                            last = pe.matmul(o[:, t + 1:, :], onesb[:], cnt[g % 2][:, t:t + 1, :].to_broadcast([P, m, E]),
                                             start=False, stop=(t == GT - 2), skip_group_check=True)
                        last.then_inc(rank_ps, 1)

                    if r == 0:
                        attend(0)
                        attend(1)
                        attend(2)
                    for g in range(NG + 1):
                        if g < NG:
                            turn(g)
                        if r == 0 and g + 3 < NG:
                            attend(g + 3)
                        if g >= 2:
                            dense(g - 1)
                        if g == 1:
                            rank(0)
                        if g < NG:
                            route(g)
                        if g >= 2:
                            rank(g - 1)
                        if g == 1:
                            dense(0)
                    pe.wait_ge(run_ok, NG)
                    pe.wait_ge(lg_ok, NG)
                    pe.matmul(bank[:, 6, 0:E], onesb[:], run[NG % 2], start=True, stop=True).then_inc(tot_ps, 1)

                    pe.wait_ge(texp_ok, 1)

                    def expert(j):
                        return pe.value_load(texp[0:1, j:j + 1] if isinstance(j, int) else texp[0:1, bass.ds(j, 1)],
                                             min_val=0, max_val=E - 1)

                    def split(o, rows, chunks, high, low):
                        for c in range(chunks):
                            hi, lo = (f32r(rows[:, q, c * P:(c + 1) * P]) for q in range(2))
                            pe.matmul(o, hi, f32r(high(c)), start=(c == 0), stop=False)
                            pe.matmul(o, hi, f32r(low(c)), start=False, stop=False)
                            pe.matmul(o, lo, f32r(high(c)), start=False, stop=False)

                    def turn_x(j, k, turn):
                        pe.wait_ge(x_ld[k % RING], turn * 16 + 16)
                        after(pe, xrT_ok, j - 1)
                        for c in range(KC):
                            last = pe.transpose(bank[:, k % 2, c * P:(c + 1) * P], xr[k % RING][:, c * P:(c + 1) * P], ident[:])
                        last.then_inc(xrT_ps, 1)

                    def up(j, k, e, load):
                        pe.wait_ge(low_ld, e * WEIGHTS + WEIGHTS)
                        pe.wait_ge(xrT_ok, j + 1)
                        after(pe, hid_ok, j - 1)
                        o = bank[:, 2 + k % 2, :]
                        split(o, xrT[k % 2], KC, lambda c: ew1[:, c, bass.ds(e, 1), :], lambda c: low1_in[:, bass.ds(e, 1), c, :])
                        loaded = [expert(t) for t in load]
                        pe.matmul(o, sel[:, bass.ds(e, 1), :], eb1p[:], start=False, stop=True).then_inc(up_ps, 1)
                        return loaded

                    def turn_h(j, k):
                        pe.wait_ge(hid_ok, j + 1)
                        after(pe, hidT_ok, j - 1)
                        for c in range(HC):
                            last = pe.transpose(bank[:, 4 + k % 2, c * P:(c + 1) * P], hid[k % 2][:, c * P:(c + 1) * P], ident[:])
                        last.then_inc(hidT_ps, 1)

                    def down(j, k, e):
                        pe.wait_ge(hidT_ok, j + 1)
                        after(pe, y_ok, j - 1)
                        o = bank[:, 6 + k % 2, 0:C]
                        split(o, hidT[k % 2], HC, lambda c: ew2[:, c, bass.ds(e, 1), :], lambda c: low2_in[:, bass.ds(e, 1), c, :])
                        pe.matmul(o, sel[:, bass.ds(e, 1), :], eb2p[:], start=False, stop=True).then_inc(dn_ps, 1)

                    kept = [pe.alloc_register(f"m{r}_expert{q}") for q in range(2)]

                    def run_tiles(run):
                        if isinstance(run[0][0], int) and run[0][0] == 0:
                            e, before = expert(0), None
                        else:
                            e, before = (pe.snap(q, min_val=0, max_val=E - 1) for q in kept)
                        for j, k, turn in run:
                            behind = before is not None
                            ahead = up(j, k, e, [] if is_last(j) else [j + 1])
                            if not is_last(j):
                                turn_x(j + 1, k + 1, turn + (k + 1) // RING)
                            if behind:
                                down(j - 1, k - 1, before)
                            turn_h(j, k)
                            before, e = e, ahead[0] if ahead else None
                        if e is not None:
                            pe.reg_mov(kept[0], e)
                            pe.reg_mov(kept[1], before)

                    turn_x(0, 0, 0)
                    over_tiles(pe, run=run_tiles)
                    down(SLOTS - 1, SLOTS - 1, expert(SLOTS - 1))

        def attention():
            w = Arena(work[:])
            w.take(2 * 2 * BANK)
            prob = [w.take(N) for _ in range(2)]
            pw = Arena(work[:, 2 * 2 * BANK:])
            ln = [pw.take(GT, C) for _ in range(2)]
            assert pw.at <= 2 * N
            nb = [w.take(GT) for _ in range(2)]
            nmax, rsum, rinv = w.take(BT), w.take(BT), w.take(BT)
            nrm = Norm("b", w)
            nb_ok, ln_ok, lnT_ps = sem("b_nb"), sem("b_ln"), sem("b_lnT_ps")
            whigh_ok, wlow_ok = sem("b_whigh"), sem("b_wlow")
            khigh_ok, klow_ok, qhigh_ok, vhigh_ok, phigh_ok = (sem("b_khigh"), sem("b_klow"), sem("b_qhigh"), sem("b_vhigh"),
                                                               sem("b_phigh"))
            q_ps, v_ps, q_ok, v_ok = sem("b_q_ps"), sem("b_v_ps"), sem("b_q"), sem("b_v")
            sc_ps, max_ok, exp_ok = sem("b_sc_ps"), sem("b_max"), sem("b_exp")
            pT_ps, pT_ok, pv_ok, inv_ok, x3_ok = sem("b_pT_ps"), sem("b_pT"), sem("b_pv"), sem("b_inv"), sem("b_x3")
            GB = NG // B
            chunks = [(b, i, c) for b in range(B) for i in range(BT) for c in range(i // GT + 1)]
            at = {x: n for n, x in enumerate(chunks)}

            assert KC * C == BANK
            weights_in = (wa, wvo)
            WA, WVO = range(2)

            def weight(which, part, c, some):
                return shares[:, which, part, c * C + some.start:c * C + some.stop]

            def weighed(n):
                return at[(n - 1) // BT, (n - 1) % BT, (n - 1) % BT // GT] + 1 if n >= 1 else 0

            def blocks(i, c):
                return min(GT, i + 1 - c * GT)

            with nc.Block() as block:
                @block.gpsimd
                def _(pool):
                    for g in range(NG):
                        nrm.roots(pool, g)

                @block.vector
                def _(v):
                    def normalise(g):
                        u = g % 2
                        nrm.statistics(v, g, xs[:, g * GT:(g + 1) * GT, :])
                        v.wait_ge(nrm.root_ok, g + 1)
                        v.scalar_tensor_tensor(nb[u], nrm.sum[u], -0.5, nrm.root[u][:, 0, :], ALU.mult, ALU.mult).then_inc(nb_ok, 1)
                        v.wait_ge(nb_ok, g + 1)
                        after(v, lnT_ps, g - 1)
                        for t in range(GT):
                            v.tensor_scalar(ln[u][:, t, :], xs[:, g * GT + t, :], nrm.root[u][:, 0, t:t + 1],
                                            nb[u][:, t:t + 1], ALU.mult, ALU.add).then_inc(ln_ok, 1)

                    def low_keys(g):
                        m = slice(g % GB * BANK, (g % GB + 1) * BANK)
                        v.wait_ge(khigh_ok, g + 1)
                        v.tensor_tensor(f32r(keys[:, 1, :, m]), bank[:, 0:2, :], keys[:, 0, :, m], ALU.subtract).then_inc(klow_ok, 1)

                    def low_queries_values(g):
                        l = g % GB
                        m = slice(l * BANK, (l + 1) * BANK)
                        v.wait_ge(qhigh_ok, KC * (g + 1))
                        for c in range(KC):
                            v.scalar_tensor_tensor(f32r(queries[:, 1, c, m]), bank[:, 2 + c, :], qbias[:, c:c + 1], queries[:, 0, c, m],
                                                   ALU.add, ALU.subtract).then_inc(q_ok, 1)
                        v.wait_ge(vhigh_ok, g + 1)
                        ts = slice(l * GT, (l + 1) * GT)
                        v.tensor_tensor(f32r(values[:, 1, ts, :].rearrange("p t c -> p (t c)")), psum(4, 2),
                                        values[:, 0, ts, :].rearrange("p t c -> p (t c)"), ALU.subtract).then_inc(v_ok, 1)

                    def low_shares(n, some):
                        b, i = n // BT, n % BT
                        for c in range(i // GT + 1)[some]:
                            k, wd = at[b, i, c], blocks(i, c) * P
                            v.wait_ge(phigh_ok, k + 1)
                            after(v, pv_ok, k - 1)
                            v.tensor_tensor(f32r(shares[:, k % 2, 1, 0:wd]), bank[:, 4 + k % 2, 0:wd], shares[:, k % 2, 0, 0:wd],
                                            ALU.subtract).then_inc(pT_ok, 1)

                    for b in range(B):
                        after(v, exp_ok, b * BT)
                        after(v, pv_ok, weighed(b * BT))
                        normalise(b * GB)
                        for q in (WA, WVO):
                            v.wait_ge(whigh_ok, 2 * b + q + 1)
                            v.tensor_tensor(f32r(shares[:, q, 1, :]), flat(weights_in[q]), shares[:, q, 0, :], ALU.subtract).then_inc(wlow_ok, 1)
                        for g in range(b * GB, (b + 1) * GB):
                            if g + 1 < (b + 1) * GB:
                                normalise(g + 1)
                            low_keys(g)
                            if g > b * GB:
                                low_queries_values(g - 1)
                        low_queries_values((b + 1) * GB - 1)
                        for i in range(BT + 1):
                            n = b * BT + i
                            if i >= 1:
                                low_shares(n - 1, slice(0, 2))
                            if i < BT:
                                v.wait_ge(sc_ps, n + 1)
                                v.tensor_reduce(nmax[:, i:i + 1], psum(0, 4)[:, 0:(i + 1) * P], AX.X, ALU.max, negate=True).then_inc(max_ok, 1)
                            if i >= 1:
                                low_shares(n - 1, slice(2, None))
                                v.wait_ge(exp_ok, n)
                                v.reciprocal(rinv[:, i - 1:i], rsum[:, i - 1:i]).then_inc(inv_ok, 1)
                                v.wait_ge(inv_ok, n)
                                v.wait_ge(pv_ok, weighed(n))
                                v.scalar_tensor_tensor(xs[:, n - 1, :], bank[:, 6 + (n - 1) % 2, 0:C], rinv[:, i - 1:i], xs[:, n - 1, :],
                                                       ALU.mult, ALU.add).then_inc(x3_ok, 1)

                @block.scalar
                def _(act):
                    for b in range(B):
                        after(act, pv_ok, weighed(b * BT))
                        for q in (WA, WVO):
                            copy(act, f32r(shares[:, q, 0, :]), flat(weights_in[q])).then_inc(whigh_ok, 1)
                        for g in range(b * GB, (b + 1) * GB + 1):
                            l = g - b * GB
                            if l < GB:
                                act.wait_ge(lnT_ps, g + 1)
                                copy(act, f32r(keys[:, 0, :, l * BANK:(l + 1) * BANK]), bank[:, 0:2, :]).then_inc(khigh_ok, 1)
                            if l >= 1:
                                act.wait_ge(q_ps, g)
                                for c in range(KC):
                                    act.activation(f32r(queries[:, 0, c, (l - 1) * BANK:l * BANK]), bank[:, 2 + c, :], ACT.Identity,
                                                   bias=qbias[:, c:c + 1]).then_inc(qhigh_ok, 1)
                                act.wait_ge(v_ps, g)
                                copy(act, f32r(values[:, 0, (l - 1) * GT:l * GT, :].rearrange("p t c -> p (t c)")), psum(4, 2)
                                     ).then_inc(vhigh_ok, 1)
                        for i in range(BT + 1):
                            n = b * BT + i
                            if i >= 1:
                                for c in range((i - 1) // GT + 1):
                                    k = at[b, i - 1, c]
                                    act.wait_ge(pT_ps, k + 1)
                                    after(act, pv_ok, k - 1)
                                    wd = blocks(i - 1, c) * P
                                    copy(act, f32r(shares[:, k % 2, 0, 0:wd]), bank[:, 4 + k % 2, 0:wd]).then_inc(phigh_ok, 1)
                            if i < BT:
                                act.wait_ge(max_ok, n + 1)
                                after(act, pv_ok, weighed(n - 1))
                                act.activation(prob[n % 2][:, 0:(i + 1) * P], psum(0, 4)[:, 0:(i + 1) * P], ACT.Exp,
                                               bias=nmax[:, i:i + 1], accum_out=rsum[:, i:i + 1]).then_inc(exp_ok, 1)

                @block.tensor
                def _(pe):
                    def split(o, left, right, start, stop):
                        for q, (x, y) in enumerate(((0, 0), (0, 1), (1, 0))):
                            last = pe.matmul(o, f32r(left(x)), f32r(right(y)), start=(start and q == 0), stop=(stop and q == 2),
                                             skip_group_check=True)
                        return last

                    def scores(b, i):
                        n = b * BT + i
                        if i == 0:
                            pe.wait_ge(q_ok, KC * GB * (b + 1))
                            pe.wait_ge(v_ok, GB * (b + 1))
                            pe.wait_ge(klow_ok, GB * (b + 1))
                        else:
                            pe.wait_ge(exp_ok, n)
                        for c in range(i // GT + 1):
                            wd = max(blocks(i, c), 2) * P
                            for k in range(KC):
                                split(bank[:, c, 0:wd], lambda x: queries[:, x, k, i * P:(i + 1) * P],
                                      lambda y: keys[:, y, k, c * BANK:c * BANK + wd], k == 0, k == KC - 1 and c < i // GT)
                        last = pe.matmul(bank[:, i // GT, (i % GT) * P:(i % GT + 1) * P], identb[:], causal[:],
                                         start=False, stop=True, skip_group_check=True)
                        last.then_inc(sc_ps, 1)

                    def turn(b, i, c):
                        n, k = b * BT + i, at[b, i, c]
                        after(pe, pT_ok, k - 1)
                        for q in range(blocks(i, c)):
                            last = pe.transpose(bank[:, 4 + k % 2, q * P:(q + 1) * P],
                                                prob[n % 2][:, (c * GT + q) * P:(c * GT + q + 1) * P], ident[:])
                        last.then_inc(pT_ps, 1)

                    def weigh(b, i, c):
                        n, k = b * BT + i, at[b, i, c]
                        o = bank[:, 6 + n % 2, 0:C]
                        pe.wait_ge(pT_ok, k + 1)
                        if c == 0:
                            after(pe, x3_ok, n - 1)
                        for q in range(blocks(i, c)):
                            s = c * GT + q
                            last = split(o, lambda x: shares[:, k % 2, x, q * P:(q + 1) * P], lambda y: values[:, y, s, :], s == 0, s == i)
                        last.then_inc(pv_ok, 1)

                    for b in range(B):
                        for g in range(b * GB, (b + 1) * GB + 1):
                            l = g - b * GB
                            if l < GB:
                                u = g % 2
                                pe.wait_ge(ln_ok, GT * (g + 1))
                                after(pe, klow_ok, g)
                                if l == 0:
                                    after(pe, exp_ok, b * BT)
                                for c in range(KC):
                                    for t in range(GT):
                                        last = pe.transpose(bank[:, c, t * P:(t + 1) * P], ln[u][:, t, c * P:(c + 1) * P], ident[:])
                                last.then_inc(lnT_ps, 1)
                            if l >= 1:
                                h = g - 1
                                m = (h - b * GB) * BANK
                                pe.wait_ge(klow_ok, h + 1)
                                pe.wait_ge(wlow_ok, 2 * (b + 1))
                                after(pe, q_ok, KC * h)
                                for j in range(KC):
                                    for c in range(KC):
                                        last = split(bank[:, 2 + j, :], lambda x: weight(WA, x, c, slice(j * P, (j + 1) * P)),
                                                     lambda y: keys[:, y, c, m:m + BANK], c == 0, c == KC - 1)
                                last.then_inc(q_ps, 1)
                                after(pe, v_ok, h)
                                for t in range(GT):
                                    o = bank[:, 4 + t // 2, (t % 2) * C:(t % 2 + 1) * C]
                                    for c in range(KC):
                                        split(o, lambda x: keys[:, x, c, m + t * P:m + (t + 1) * P],
                                              lambda y: weight(WVO, y, c, slice(0, C)), c == 0, False)
                                    last = pe.matmul(o, onesb[0:2 * QROW + 1, :], vbp[:], start=False, stop=True, skip_group_check=True)
                                last.then_inc(v_ps, 1)
                        for i in range(BT + 1):
                            turned = (i - 1) // GT + 1
                            if i >= 1:
                                pe.wait_ge(exp_ok, b * BT + i)
                                for c in range(min(2, turned)):
                                    turn(b, i - 1, c)
                            if i < BT:
                                scores(b, i)
                            if i >= 1:
                                for c in range(turned):
                                    weigh(b, i - 1, c)
                                    if c + 2 < turned:
                                        turn(b, i - 1, c + 2)

        weights()
        context()
        release(1)
        mixture(0)
        release(1)
        attention()
        mixture(1)


_INS = ["L0_attn_a_x", "L0_attn_a_Wqkv", "L0_attn_a_Wout", "L0_attn_a_bout", "L0_attn_b_Wq", "L0_attn_b_bq",
        "L0_attn_b_Wk", "L0_attn_b_bk", "L0_attn_b_Wv", "L0_attn_b_bv", "L0_attn_b_Wo", "L0_attn_b_bo",
        "L0_ffn_ln_gamma", "L0_ffn_ln_beta", "L0_ffn_abel_w", "L0_ffn_abel_b", "L0_ffn_moe_gate_w",
        "L0_ffn_moe_gate_b", "L0_ffn_ew1", "L0_ffn_eb1", "L0_ffn_ew2", "L0_ffn_eb2", "L0_ffn_gens", "L0_ffn_gc_w",
        "L0_ffn_gc_b"]


def kernel(**inputs):
    import numpy as _np
    import concourse.bacc as _bacc
    from concourse import mybir as _mybir
    from concourse.bass_utils import run_bass_kernel_spmd as _run

    nc = _bacc.Bacc("TRN2", target_bir_lowering=False, num_devices=1)
    arrays, aps = {}, {}
    for name in _INS:
        a = _np.ascontiguousarray(inputs[name])
        arrays[f"in_{name}_dram"] = a
        aps[name] = nc.dram_tensor(f"in_{name}_dram", a.shape, _mybir.dt.from_np(a.dtype), kind="ExternalInput").ap()
    shape = arrays["in_L0_attn_a_x_dram"].shape
    out = nc.dram_tensor("out_0_dram", shape, _mybir.dt.float32, kind="ExternalOutput").ap()
    build(nc, aps, out)
    r = _run(nc, [arrays], core_ids=[0])
    return r.results[0]["out_0_dram"]
```
